# Optimizing a Trainium2 kernel written in Bass

```python
import numpy as np
import jax
import jax.numpy as jnp

def _softmax(x, axis=-1):
    return jax.nn.softmax(x, axis=axis)

def _gelu(x):
    return jax.nn.gelu(x, approximate=True)

def _silu(x):
    return jax.nn.silu(x)

def _sigmoid(x):
    return jax.nn.sigmoid(x)

def _layernorm(x, axis=-1, eps=1e-05):
    m = jnp.mean(x, axis=axis, keepdims=True)
    v = jnp.var(x, axis=axis, keepdims=True)
    return (x - m) / jnp.sqrt(v + eps)

def _scatter_add(tgt, idx, src, axis=0):
    return tgt.at[idx].add(src)

def _segment_sum(src, seg, n):
    return jax.ops.segment_sum(src, seg, n)
kernel_name = 'mk_adaln_d1_jaxref_r8_f18e88'

def setup_inputs(seed: int=0):
    np.random.seed(seed)
    _w = jnp.asarray

    def _L0_attn_setup():
        import jax, jax.numpy as jnp
        import numpy as np
        CHUNK = 32

        def _l2norm(x):
            return x * jax.lax.rsqrt(jnp.sum(x * x, -1, keepdims=True) + 1e-06)

        def _short_conv(x, w):
            K = w.shape[-1]
            L = x.shape[1]
            xp = jnp.pad(x, ((0, 0), (K - 1, 0), (0, 0)))
            y = sum((xp[:, t:t + L, :] * w[:, t] for t in range(K)))
            return jax.nn.silu(y)

        def _fir_conv(x, w):
            B, L, H, D = x.shape
            K = w.shape[-1]
            xf = x.reshape(B, L, H * D).transpose(0, 2, 1)
            wf = w.reshape(H * D, 1, K)
            y = jax.lax.conv_general_dilated(xf, wf, (1,), [(K - 1, 0)], feature_group_count=H * D, dimension_numbers=('NCH', 'OIH', 'NCH'))
            return y.transpose(0, 2, 1).reshape(B, L, H, D)

        def _delta_rule(q, k, v, beta, chunk=CHUNK):
            B, H, L, Dk = q.shape
            Dv = v.shape[-1]
            pad = -L % chunk
            if pad:
                q, k, v = (jnp.pad(t, ((0, 0), (0, 0), (0, pad), (0, 0))) for t in (q, k, v))
                beta = jnp.pad(beta, ((0, 0), (0, 0), (0, pad)))
            Lp = L + pad
            n = Lp // chunk
            q = _l2norm(q)
            k = _l2norm(k)
            v = v * beta[..., None]
            kb = k * beta[..., None]
            resh = lambda t: t.reshape(B, H, n, chunk, -1)
            q, k, v, kb = map(resh, (q, k, v, kb))
            tri = jnp.triu(jnp.ones((chunk, chunk), bool))
            tri_s = jnp.triu(tri, 1)
            A = jnp.where(tri, 0.0, -jnp.einsum('bhncd,bhnmd->bhncm', kb, k))
            for i in range(1, chunk):
                A = A.at[..., i, :i].add(jnp.einsum('...j,...jk->...k', A[..., i, :], A[..., :, :i]))
            T = A + jnp.eye(chunk, dtype=A.dtype)
            u = T @ v
            w = T @ kb

            def step(S, inp):
                qi, ki, ui, wi = inp
                attn = jnp.where(tri_s, 0.0, qi @ jnp.swapaxes(ki, -1, -2))
                u_i = ui - wi @ S
                o = qi @ S + attn @ u_i
                S = S + jnp.swapaxes(ki, -1, -2) @ u_i
                return (S, o)
            S0 = jnp.zeros((B, H, Dk, Dv), q.dtype)
            blocks = lambda t: jnp.moveaxis(t, 2, 0)
            S, out = jax.lax.scan(step, S0, (blocks(q), blocks(k), blocks(u), blocks(w)))
            out = jnp.moveaxis(out, 0, 2).reshape(B, H, Lp, Dv)[:, :, :L]
            return (out, S)
        key = jax.random.key(seed)
        B, L, D, H = (2, 256, 128, 4)
        Dv = D // H
        ks = jax.random.split(key, 16)
        nrm = lambda k, s, sc: jax.random.normal(k, s, jnp.float32) * sc
        gate_in_dim = D + 2 * H * 4
        hid = 2 * D
        return {'hidden_states': nrm(ks[0], (B, L, D), 1.0), 'Wq': nrm(ks[1], (D, D), D ** (-0.5)), 'Wk': nrm(ks[2], (D, D), D ** (-0.5)), 'Wv': nrm(ks[3], (D, D), D ** (-0.5)), 'Wb': nrm(ks[4], (H, D), D ** (-0.5)), 'qconv_w': nrm(ks[5], (D, 4), 0.5), 'kconv_w': nrm(ks[6], (D, 4), 0.5), 'vconv_w': nrm(ks[7], (D, 4), 0.5), 'fir_short_w': jnp.zeros((H, Dv, 3)).at[..., -1].set(1.0) + nrm(ks[8], (H, Dv, 3), 0.02), 'fir_long_w': jnp.zeros((H, Dv, 63)).at[..., -1].set(1.0) + nrm(ks[9], (H, Dv, 63), 0.02), 'gate_w1': nrm(ks[10], (hid, gate_in_dim), gate_in_dim ** (-0.5)), 'gate_b1': jnp.zeros((hid,), jnp.float32), 'gate_w2': nrm(ks[11], (H * 4, hid), hid ** (-0.5)), 'log_temp': jnp.zeros((H,), jnp.float32), 'base_bias': jnp.zeros((H, 4)).at[:, 3].set(2.0), 'floor_raw': jnp.full((H, 4), float(np.log(0.5)), jnp.float32), 'onorm_w': jnp.ones((Dv,), jnp.float32), 'Wo': nrm(ks[12], (D, D), D ** (-0.5))}
    _L0_attn_in = _L0_attn_setup()

    def _L0_ffn_setup():
        import jax, jax.numpy as jnp
        import numpy as np
        B, T, D, E, H = (4, 256, 128, 4, 8)
        EPS = 1e-05

        def _uniform(k, shape, bound):
            return jax.random.uniform(k, shape, jnp.float32, -bound, bound)

        def _layernorm(x, w, b):
            mu = jnp.mean(x, axis=-1, keepdims=True)
            var = jnp.mean(jnp.square(x - mu), axis=-1, keepdims=True)
            return (x - mu) * jax.lax.rsqrt(var + EPS) * w + b
        key = jax.random.key(seed)
        ks = jax.random.split(key, 12)
        wb = np.sqrt(6.0 / D) / np.sqrt(6.0)
        wb = 1.0 / np.sqrt(D)
        return {'x': jax.random.normal(ks[0], (B, T, D), jnp.float32), 'router_prob': jax.random.uniform(ks[1], (B, T, E), jnp.float32), 'norm_w': jnp.ones((D,), jnp.float32), 'norm_b': jnp.zeros((D,), jnp.float32), 'q_w': _uniform(ks[2], (D, D), wb), 'q_b': _uniform(ks[3], (D,), wb), 'k_w': _uniform(ks[4], (D, D), wb), 'k_b': _uniform(ks[5], (D,), wb), 'v_w': _uniform(ks[6], (D, D), wb), 'v_b': _uniform(ks[7], (D,), wb), 'o_w': _uniform(ks[8], (D, D), wb), 'o_b': _uniform(ks[9], (D,), wb)}
    _L0_ffn_in = _L0_ffn_setup()
    _L0_c = _w((lambda *s: np.random.randn(*s).astype(np.float32) * 0.05)(8, 128))
    _L0_wmod = _w((lambda *s: np.random.randn(*s).astype(np.float32) * 0.05)(128, 6 * 128) * 128 ** (-0.5))
    _d = {'L0_attn_hidden_states': _L0_attn_in['hidden_states'], 'L0_attn_Wq': _L0_attn_in['Wq'], 'L0_attn_Wk': _L0_attn_in['Wk'], 'L0_attn_Wv': _L0_attn_in['Wv'], 'L0_attn_Wb': _L0_attn_in['Wb'], 'L0_attn_qconv_w': _L0_attn_in['qconv_w'], 'L0_attn_kconv_w': _L0_attn_in['kconv_w'], 'L0_attn_vconv_w': _L0_attn_in['vconv_w'], 'L0_attn_fir_short_w': _L0_attn_in['fir_short_w'], 'L0_attn_fir_long_w': _L0_attn_in['fir_long_w'], 'L0_attn_gate_w1': _L0_attn_in['gate_w1'], 'L0_attn_gate_b1': _L0_attn_in['gate_b1'], 'L0_attn_gate_w2': _L0_attn_in['gate_w2'], 'L0_attn_log_temp': _L0_attn_in['log_temp'], 'L0_attn_base_bias': _L0_attn_in['base_bias'], 'L0_attn_floor_raw': _L0_attn_in['floor_raw'], 'L0_attn_onorm_w': _L0_attn_in['onorm_w'], 'L0_attn_Wo': _L0_attn_in['Wo'], 'L0_ffn_router_prob': _L0_ffn_in['router_prob'], 'L0_ffn_norm_w': _L0_ffn_in['norm_w'], 'L0_ffn_norm_b': _L0_ffn_in['norm_b'], 'L0_ffn_q_w': _L0_ffn_in['q_w'], 'L0_ffn_q_b': _L0_ffn_in['q_b'], 'L0_ffn_k_w': _L0_ffn_in['k_w'], 'L0_ffn_k_b': _L0_ffn_in['k_b'], 'L0_ffn_v_w': _L0_ffn_in['v_w'], 'L0_ffn_v_b': _L0_ffn_in['v_b'], 'L0_ffn_o_w': _L0_ffn_in['o_w'], 'L0_ffn_o_b': _L0_ffn_in['o_b'], 'L0_c': _L0_c, 'L0_wmod': _L0_wmod}
    _x0 = _d['L0_attn_hidden_states']
    _d['L0_attn_hidden_states'] = jax.random.normal(jax.random.fold_in(jax.random.key(seed), 1), (8, 512, 128), dtype=_x0.dtype)
    del _x0
    return _d

def reference(L0_attn_hidden_states, L0_attn_Wq, L0_attn_Wk, L0_attn_Wv, L0_attn_Wb, L0_attn_qconv_w, L0_attn_kconv_w, L0_attn_vconv_w, L0_attn_fir_short_w, L0_attn_fir_long_w, L0_attn_gate_w1, L0_attn_gate_b1, L0_attn_gate_w2, L0_attn_log_temp, L0_attn_base_bias, L0_attn_floor_raw, L0_attn_onorm_w, L0_attn_Wo, L0_ffn_router_prob, L0_ffn_norm_w, L0_ffn_norm_b, L0_ffn_q_w, L0_ffn_q_b, L0_ffn_k_w, L0_ffn_k_b, L0_ffn_v_w, L0_ffn_v_b, L0_ffn_o_w, L0_ffn_o_b, L0_c, L0_wmod):

    def _L0_attn_ref(hidden_states, Wq, Wk, Wv, Wb, qconv_w, kconv_w, vconv_w, fir_short_w, fir_long_w, gate_w1, gate_b1, gate_w2, log_temp, base_bias, floor_raw, onorm_w, Wo):
        import jax, jax.numpy as jnp
        import numpy as np
        CHUNK = 32

        def _l2norm(x):
            return x * jax.lax.rsqrt(jnp.sum(x * x, -1, keepdims=True) + 1e-06)

        def _short_conv(x, w):
            K = w.shape[-1]
            L = x.shape[1]
            xp = jnp.pad(x, ((0, 0), (K - 1, 0), (0, 0)))
            y = sum((xp[:, t:t + L, :] * w[:, t] for t in range(K)))
            return jax.nn.silu(y)

        def _fir_conv(x, w):
            B, L, H, D = x.shape
            K = w.shape[-1]
            xf = x.reshape(B, L, H * D).transpose(0, 2, 1)
            wf = w.reshape(H * D, 1, K)
            y = jax.lax.conv_general_dilated(xf, wf, (1,), [(K - 1, 0)], feature_group_count=H * D, dimension_numbers=('NCH', 'OIH', 'NCH'))
            return y.transpose(0, 2, 1).reshape(B, L, H, D)

        def _delta_rule(q, k, v, beta, chunk=CHUNK):
            B, H, L, Dk = q.shape
            Dv = v.shape[-1]
            pad = -L % chunk
            if pad:
                q, k, v = (jnp.pad(t, ((0, 0), (0, 0), (0, pad), (0, 0))) for t in (q, k, v))
                beta = jnp.pad(beta, ((0, 0), (0, 0), (0, pad)))
            Lp = L + pad
            n = Lp // chunk
            q = _l2norm(q)
            k = _l2norm(k)
            v = v * beta[..., None]
            kb = k * beta[..., None]
            resh = lambda t: t.reshape(B, H, n, chunk, -1)
            q, k, v, kb = map(resh, (q, k, v, kb))
            tri = jnp.triu(jnp.ones((chunk, chunk), bool))
            tri_s = jnp.triu(tri, 1)
            A = jnp.where(tri, 0.0, -jnp.einsum('bhncd,bhnmd->bhncm', kb, k))
            for i in range(1, chunk):
                A = A.at[..., i, :i].add(jnp.einsum('...j,...jk->...k', A[..., i, :], A[..., :, :i]))
            T = A + jnp.eye(chunk, dtype=A.dtype)
            u = T @ v
            w = T @ kb

            def step(S, inp):
                qi, ki, ui, wi = inp
                attn = jnp.where(tri_s, 0.0, qi @ jnp.swapaxes(ki, -1, -2))
                u_i = ui - wi @ S
                o = qi @ S + attn @ u_i
                S = S + jnp.swapaxes(ki, -1, -2) @ u_i
                return (S, o)
            S0 = jnp.zeros((B, H, Dk, Dv), q.dtype)
            blocks = lambda t: jnp.moveaxis(t, 2, 0)
            S, out = jax.lax.scan(step, S0, (blocks(q), blocks(k), blocks(u), blocks(w)))
            out = jnp.moveaxis(out, 0, 2).reshape(B, H, Lp, Dv)[:, :, :L]
            return (out, S)
        B, L, D = hidden_states.shape
        H = log_temp.shape[0]
        P = 4
        q = _short_conv(hidden_states @ Wq.T, qconv_w).reshape(B, L, H, -1)
        k = _short_conv(hidden_states @ Wk.T, kconv_w).reshape(B, L, H, -1)
        v = _short_conv(hidden_states @ Wv.T, vconv_w).reshape(B, L, H, -1)
        beta = jax.nn.sigmoid(hidden_states @ Wb.T)
        tr = lambda t: jnp.swapaxes(t, 1, 2)
        delta, _S = _delta_rule(tr(q), tr(k), tr(v), jnp.swapaxes(beta, 1, 2))
        delta = jnp.swapaxes(delta, 1, 2)
        short = _fir_conv(v, fir_short_w)
        longp = _fir_conv(v, fir_long_w)
        paths = (short, longp, delta, v)

        def stats(p):
            m = p.mean(-1)
            va = p.var(-1)
            return jnp.stack([m, va], -1).reshape(B, L, H * 2)
        gate_in = jnp.concatenate([hidden_states] + [stats(p) for p in paths], -1)
        hmid = jax.nn.gelu(gate_in @ gate_w1.T + gate_b1, approximate=False)
        logits = hmid @ gate_w2.T + base_bias.reshape(-1)
        temp = jax.nn.softplus(log_temp) + 0.0001
        logits = logits.reshape(B, L, H, P) / temp[None, None, :, None]
        probs = jax.nn.softmax(logits, -1)
        floor_val = 0.05 * jax.nn.sigmoid(floor_raw)
        probs = jnp.maximum(probs, floor_val)
        probs = probs / probs.sum(-1, keepdims=True)
        out = sum((probs[..., i, None] * p for i, p in enumerate(paths)))
        out = out * jax.lax.rsqrt(jnp.mean(out * out, -1, keepdims=True) + 1e-05) * onorm_w
        return out.reshape(B, L, -1) @ Wo.T

    def _L0_ffn_ref(x, router_prob, norm_w, norm_b, q_w, q_b, k_w, k_b, v_w, v_b, o_w, o_b):
        import jax, jax.numpy as jnp
        import numpy as np
        B, T, D, E, H = (4, 256, 128, 4, 8)
        EPS = 1e-05

        def _uniform(k, shape, bound):
            return jax.random.uniform(k, shape, jnp.float32, -bound, bound)

        def _layernorm(x, w, b):
            mu = jnp.mean(x, axis=-1, keepdims=True)
            var = jnp.mean(jnp.square(x - mu), axis=-1, keepdims=True)
            return (x - mu) * jax.lax.rsqrt(var + EPS) * w + b
        e_cnt = router_prob.shape[2]
        b, t, d = x.shape
        n = t // e_cnt
        h = H
        scale = d ** (-0.5)
        qs, ks_, vs = ([], [], [])
        for e in range(e_cnt):
            xe = x[:, e * n:(e + 1) * n, :]
            xn = _layernorm(xe, norm_w, norm_b)
            m = d // 2 ** e
            xm = xn[..., :m]
            qs.append(jnp.einsum('bnm,dm->bnd', xm, q_w[:, :m]) + q_b)
            ks_.append(jnp.einsum('bnm,dm->bnd', xm, k_w[:, :m]) + k_b)
            vs.append(jnp.einsum('bnm,dm->bnd', xm, v_w[:, :m]) + v_b)
        q = jnp.concatenate(qs, axis=1)
        k = jnp.concatenate(ks_, axis=1)
        v = jnp.concatenate(vs, axis=1)
        dh = d // h
        q = q.reshape(b, t, h, dh).transpose(0, 2, 1, 3)
        k = k.reshape(b, t, h, dh).transpose(0, 2, 1, 3)
        v = v.reshape(b, t, h, dh).transpose(0, 2, 1, 3)
        attn = jnp.einsum('bhqd,bhkd->bhqk', q, k) * scale
        attn = jax.nn.softmax(attn, axis=-1)
        attn_out = jnp.einsum('bhqk,bhkd->bhqd', attn, v)
        attn_out = attn_out.transpose(0, 2, 1, 3).reshape(b, t, d)
        outs = []
        for e in range(e_cnt):
            sl = slice(e * n, (e + 1) * n)
            m = d // 2 ** e
            xm = attn_out[:, sl, :m]
            out = jnp.einsum('bnm,om->bno', xm, o_w[:m, :m]) + o_b[:m]
            pad = d - m
            if pad:
                out = jnp.pad(out, ((0, 0), (0, 0), (0, pad)))
            outs.append(out + x[:, sl, :])
        return jnp.concatenate(outs, axis=1)
    x = L0_attn_hidden_states
    mod = (_silu(L0_c) @ L0_wmod).reshape(L0_c.shape[0], 6, 1, -1)
    sa, ca, ga, sb, cb, gb = (mod[:, 0], mod[:, 1], mod[:, 2], mod[:, 3], mod[:, 4], mod[:, 5])
    ga = (2 * (ga >= 0) - 1) * jnp.maximum(jnp.abs(ga), 0.25)
    gb = (2 * (gb >= 0) - 1) * jnp.maximum(jnp.abs(gb), 0.25)
    h = _layernorm(x, axis=-1) * (1 + ca) + sa
    x = x + ga * _L0_attn_ref(h, L0_attn_Wq, L0_attn_Wk, L0_attn_Wv, L0_attn_Wb, L0_attn_qconv_w, L0_attn_kconv_w, L0_attn_vconv_w, L0_attn_fir_short_w, L0_attn_fir_long_w, L0_attn_gate_w1, L0_attn_gate_b1, L0_attn_gate_w2, L0_attn_log_temp, L0_attn_base_bias, L0_attn_floor_raw, L0_attn_onorm_w, L0_attn_Wo)
    h = _layernorm(x, axis=-1) * (1 + cb) + sb
    x = x + gb * _L0_ffn_ref(h, L0_ffn_router_prob, L0_ffn_norm_w, L0_ffn_norm_b, L0_ffn_q_w, L0_ffn_q_b, L0_ffn_k_w, L0_ffn_k_b, L0_ffn_v_w, L0_ffn_v_b, L0_ffn_o_w, L0_ffn_o_b)
    return x

_drawn_inputs = setup_inputs


def setup_inputs(seed=0):
    import zlib

    import numpy as np

    out = dict(_drawn_inputs(seed))
    spreads = {'L0_attn_gate_b1': (0.0, 0.8),
     'L0_attn_log_temp': (0.0, 2.0),
     'L0_attn_floor_raw': (-0.6931471824645996, 0.6),
     'L0_attn_onorm_w': (1.0, 0.2),
     'L0_ffn_norm_w': (1.0, 0.6),
     'L0_ffn_norm_b': (0.0, 0.8)}
    factors = {'L0_attn_Wq': 2.966,
     'L0_attn_Wk': 2.946,
     'L0_attn_Wb': 6.785,
     'L0_attn_qconv_w': 2.996,
     'L0_attn_kconv_w': 2.952,
     'L0_attn_fir_short_w': 8.0,
     'L0_attn_gate_w1': 3.231,
     'L0_attn_gate_w2': 3.509,
     'L0_ffn_q_w': 8.0,
     'L0_ffn_q_b': 8.0,
     'L0_ffn_k_w': 8.0,
     'L0_ffn_k_b': 64.0,
     'L0_ffn_v_w': 8.0,
     'L0_ffn_v_b': 8.0,
     'L0_ffn_o_w': 8.0,
     'L0_ffn_o_b': 31.155}
    for name, (base, spread) in spreads.items():
        noise = np.random.default_rng([zlib.crc32(name.encode()), seed]).standard_normal(out[name].shape)
        drawn = base * np.exp(spread * noise) if base else spread * noise
        out[name] = jnp.asarray(drawn.astype(out[name].dtype))
    for name, factor in factors.items():
        out[name] = (out[name] * factor).astype(out[name].dtype)
    return out
```

```python
from contextlib import ExitStack

import numpy as np
import concourse.bass as bass
from concourse import mybir

F32 = mybir.dt.float32
BF16 = mybir.dt.bfloat16
ALU = mybir.AluOpType
ACT = mybir.ActivationFunctionType
AX = mybir.AxisListType.X

P = 128
B, T, D = 8, 512, 128
NT = B * T // P
TPB = T // P
H, DH = 4, 32
C = 32
NCH = B * T // C
CPB = T // C
TAPS = 4
SHORT, LONG = 3, 63
WIN = C + LONG - 1
FH, FD = 8, 16
HPAD = T + TAPS - 1
LN_EPS = 1e-5
HID = 256
ROW = 4096

C_IDENT, C_BONES, C_NEGA, C_CAUSAL, C_EYE, C_END = 0, 128, 256, 288, 320, 352


class Chain:

    def __init__(self, engine, sem):
        self.engine, self.sem, self.n = engine, sem, 0

    def link(self, ins):
        self.n += 1
        ins.then_inc(self.sem, 1)
        self.engine.wait_ge(self.sem, self.n)


def bc(ap, axis, n):
    ap = ap.unsqueeze(axis)
    shape = list(ap.shape)
    shape[axis] = n
    return ap.broadcast_to(shape)


def build(nc, a, out, stop=99):
    with ExitStack() as ctx:
        def sb(name, shape, dt=F32):
            return ctx.enter_context(nc.sbuf_tensor(name, shape, dt))

        def sem(name):
            return ctx.enter_context(nc.semaphore(name))

        psum = ctx.enter_context(nc.psum_tensor("psum", [P, 8, 512], F32))
        bank = [psum[:, i, :] for i in range(8)]
        wide = [psum[:, 2:4, :], psum[:, 4:6, :]]
        slab = sb("slab", [P, 11, ROW])
        hT = sb("hT", [P, B, HPAD])
        cst = sb("cst", [P, C_END])
        ident = cst[:, C_IDENT:C_IDENT + P]
        bones = cst[:, C_BONES:C_BONES + P]
        neg_strict = cst[:, C_NEGA:C_NEGA + C]
        causal = cst[:, C_CAUSAL:C_CAUSAL + C]
        eye32 = cst[:, C_EYE:C_EYE + C]
        cT = sb("cT", [P, B])
        modF = sb("modF", [P, 2, B])
        eps = sb("eps", [P, 3])
        eps_ln, eps_l2, one1 = eps[:, 0:1], eps[:, 1:2], eps[:, 2:3]
        chain_act, chain_dve, chain_pool = sem("chain_act"), sem("chain_dve"), sem("chain_pool")
        order = {}

        def chain(engine, s):
            if s not in order:
                order[s] = [0]
            count = order[s]

            def link(ins):
                count[0] += 1
                ins.then_inc(s, 1)
                engine.wait_ge(s, count[0])
            return link

        v_dram = nc.dram_tensor("v_padded", (B, LONG - 1 + T, D), F32, kind="Internal")
        a_dram = nc.dram_tensor("a_scratch", (NT, P, P), F32, kind="Internal").ap()
        t_dram = nc.dram_tensor("t_scratch", (NT, P, P), F32, kind="Internal").ap()

        xN = slab[:, 0, :].rearrange("p (t d) -> p t d", d=D)
        wmodF = slab[:, 1, 0:2 * D].rearrange("p (k d) -> p k d", k=2)
        wT = slab[:, 9, 0:3 * D].rearrange("p (k d) -> p k d", k=3)
        conv_row = slab[:, 9, 512:512 + 12 * D].rearrange("p (k d) -> p k d", k=12)
        wconv = slab[:, 9, 2048:2048 + 12 * D].rearrange("p (k d) -> p k d", k=12)
        wbrep = slab[:, 9, 3584:3584 + D]
        stats = slab[:, 10, 0:6 * NT].rearrange("p (t s) -> p t s", s=6)
        meanvar = slab[:, 10, 256:256 + 2 * NT].rearrange("p (t s) -> p t s", s=2)
        rstd = slab[:, 10, 384:384 + NT]
        lnv = slab[:, 10, 448:448 + NT]
        xh = xN
        s_x = [sem(f"s_x{g}") for g in range(4)]
        s_w, s_c, s_eps = sem("s_w"), sem("s_c"), sem("s_eps")
        s_silu, s_mod, s_modc, s_stats, s_rstd, s_xh, s_wc = (
            sem(x) for x in ("s_silu", "s_mod", "s_modc", "s_stats", "s_rstd", "s_xh", "s_wc"))
        with nc.Block() as block:
            @block.sync
            def _(sp):
                for g in range(4):
                    sp.dma_start(xN[:, 8 * g:8 * g + 8, :],
                                 a["x"][8 * g:8 * g + 8].rearrange("t p d -> p t d")).then_inc(s_x[g], 16)

            @block.gpsimd
            def _(pool):
                pool.memset(eps[:, 0:1], LN_EPS).then_inc(s_eps, 1)
                pool.memset(eps[:, 1:2], 1e-6).then_inc(s_eps, 1)
                pool.memset(eps[:, 2:3], 1.0).then_inc(s_eps, 1)
                pool.memset(hT[:, :, 0:TAPS - 1], 0.0).then_inc(s_eps, 1)

            @block.scalar
            def _(act):
                act.dma_start(cT[:], a["cT"]).then_inc(s_c, 16)
                act.dma_start(wmodF, a["wmod1"]).then_inc(s_c, 16)
                act.dma_start(cst[:], a["consts"]).then_inc(s_w, 16)
                act.dma_start(wT, a["wqkvT"]).then_inc(s_w, 16)
                act.dma_start(conv_row, a["convw"].partition_broadcast(P)).then_inc(s_w, 16)
                act.dma_start(wbrep, a["wbrep"]).then_inc(s_w, 16)
                act.wait_ge(s_c, 32)
                act.activation(cT[:], cT[:], ACT.Silu).then_inc(s_silu, 1)
                act.wait_ge(s_eps, 4)
                act.preload_act_table_set("natural_log_exp_and_others")
                for g in range(4):
                    act.wait_ge(s_stats, g + 1)
                    link = chain(act, chain_act)
                    link(act.activation(lnv[:, 8 * g:8 * g + 8], meanvar[:, 8 * g:8 * g + 8, 1], ACT.Ln, bias=eps_ln))
                    act.activation(rstd[:, 8 * g:8 * g + 8], lnv[:, 8 * g:8 * g + 8], ACT.Exp, scale=-0.5).then_inc(s_rstd, 1)

            @block.tensor
            def _(pe):
                pe.wait_ge(s_silu, 1)
                for k in range(2):
                    m = pe.matmul(bank[0][:, k * B:(k + 1) * B], wmodF[:, k, :], cT[:], start=True, stop=True)
                m.then_inc(s_mod, 1)

            @block.vector
            def _(dve):
                link = chain(dve, chain_dve)
                for g in range(4):
                    dve.wait_ge(s_x[g], 16)
                    for t in range(8 * g, 8 * g + 8):
                        i = dve.bn_stats(stats[:, t, :], xN[:, t, :])
                    link(i)
                    for t in range(8 * g, 8 * g + 8):
                        i = dve.bn_aggr(meanvar[:, t, :], stats[:, t, :])
                    i.then_inc(s_stats, 1)
                dve.wait_ge(s_mod, 1)
                dve.tensor_copy(modF[:, 0, :], bank[0][:, 0:B]).then_inc(s_modc, 1)
                dve.tensor_scalar(modF[:, 1, :], bank[0][:, B:2 * B], 1.0, None, ALU.add).then_inc(s_modc, 1)
                dve.wait_ge(s_w, 64)
                for k in range(3):
                    for j in range(TAPS):
                        i = dve.tensor_tensor(wconv[:, TAPS * k + j, :], wT[:, k, :], conv_row[:, TAPS * k + j, :], ALU.mult)
                i.then_inc(s_wc, 1)
                for g in range(4):
                    dve.wait_ge(s_rstd, g + 1)
                    for t in range(8 * g, 8 * g + 8):
                        i = dve.tensor_scalar(xh[:, t, :], xN[:, t, :], meanvar[:, t, 0:1], rstd[:, t:t + 1],
                                              ALU.subtract, ALU.mult)
                    i.then_inc(s_xh, 1)

        qs, ks, vT, bt = (slab[:, s, :] for s in (1, 2, 3, 4))
        s_pe, s_evac = sem("s_pe"), sem("s_evac")
        with nc.Block() as block:
            outputs = [("t", 0)]
            for b in range(B):
                if b + 1 < B:
                    outputs.append(("t", b + 1))
                outputs += [("q", b), ("k", b), ("v", b), ("beta", b)]

            @block.tensor
            def _(pe):
                for n, (kind, b) in enumerate(outputs):
                    if n >= 8:
                        pe.wait_ge(s_evac, n - 7)
                    o = bank[n % 8]
                    if kind == "t":
                        for t in range(TPB):
                            m = pe.transpose(o[:, P * t:P * t + P], xh[:, TPB * b + t, :], ident)
                    elif kind == "beta":
                        m = pe.matmul(o[:], wbrep, hT[:, b, TAPS - 1:HPAD], start=True, stop=True)
                    else:
                        if kind == "q":
                            pe.wait_ge(s_evac, outputs.index(("t", b)) + 1)
                        k = "qkv".index(kind)
                        for j in range(TAPS):
                            m = pe.matmul(o[:], wconv[:, TAPS * k + j, :], hT[:, b, j:j + T],
                                          start=j == 0, stop=j == TAPS - 1)
                    m.then_inc(s_pe, 1)

            @block.scalar
            def _(act):
                for n, (kind, b) in enumerate(outputs):
                    act.wait_ge(s_pe, n + 1)
                    o, cols = bank[n % 8][:], slice(T * b, T * b + T)
                    if kind == "t":
                        i = act.activation(hT[:, b, TAPS - 1:HPAD], o, ACT.Identity,
                                           bias=modF[:, 0, b:b + 1], scale=modF[:, 1, b:b + 1])
                    elif kind == "beta":
                        i = act.activation(bt[:, cols], o, ACT.Tanh, scale=0.5)
                    else:
                        i = act.activation({"q": qs, "k": ks, "v": vT}[kind][:, cols], o, ACT.Silu)
                    i.then_inc(s_evac, 1)
        if stop == 2:
            return dump(nc, sem, out, slab, [1, 2, 3, 4])

        kbq = slab[:, 5:7, :].rearrange("p k (c i) -> p k c i", i=C)
        vk = slab[:, 0:2, :].rearrange("p s (t h k d) -> p (s t) h k d", h=H, k=2, d=DH)
        ak = slab[:, 7:9, :].rearrange("p s (t h k d) -> p (s t) h k d", h=H, k=2, d=DH)
        kn, vb = ks, bt
        sq = slab[:, 10, :].rearrange("p (n t) -> p n t", t=T)
        vnat = slab[:, 9, :].rearrange("p (n t d) -> p n t d", n=B, t=TPB)
        s_bt, s_sq, s_ss, s_rs, s_qn, s_kn, s_vb, s_norm = (
            sem(x) for x in ("s_bt", "s_sq", "s_ss", "s_rs", "s_qn", "s_kn", "s_vb", "s_norm"))
        s_zero, s_vout, s_nat, s_nact, s_ndve, s_lnb = (sem(x) for x in ("s_zero", "s_vout", "s_nat", "s_nact", "s_ndve", "s_lnb"))
        zeros = cst[0:LONG - 1, C_BONES:C_BONES + P]
        with nc.Block() as block:
            @block.gpsimd
            def _(pool):
                for b in range(B):
                    cols = slice(T * b, T * b + T)
                    pool.tensor_scalar(bt[:, cols], bt[:, cols], 0.5, 0.5, ALU.mult, ALU.add).then_inc(s_bt, 1)
                for b in range(B):
                    cols = slice(T * b, T * b + T)
                    pool.wait_ge(s_kn, b + 1)
                    pool.tensor_tensor(vb[:, cols], vT[:, cols], bt[:, cols], ALU.mult).then_inc(s_vb, 1)

            @block.scalar
            def _(act):
                act.preload_act_table_set("natural_log_exp_and_others")
                for b in range(B):
                    cols = slice(T * b, T * b + T)
                    for k, src in enumerate((qs, ks)):
                        n = 2 * b + k
                        if n >= 4:
                            act.wait_ge(s_norm, n - 3)
                        act.activation(sq[:, n % 4, :], src[:, cols], ACT.Square).then_inc(s_sq, 1)
                    for k in range(2):
                        n = 2 * b + k
                        act.wait_ge(s_ss, n + 1)
                        act.activation(sq[:, 4 + n % 4, :], bank[n % 2][:], ACT.Ln, bias=eps_l2).then_inc(s_lnb, 1)
                        act.wait_ge(s_lnb, n + 1)
                        act.activation(sq[:, n % 4, :], sq[:, 4 + n % 4, :], ACT.Exp, scale=-0.5).then_inc(s_rs, 1)

                for b in range(B):
                    tiles = slice(TPB * b, TPB * b + TPB)
                    act.wait_ge(s_nat, 4 * b + 1)
                    act.activation(vnat[:, b, :, :], bank[2][:].rearrange("p (t d) -> p t d", d=D), ACT.Copy).then_inc(s_nact, 1)
                    act.wait_ge(s_nat, 4 * b + 2)
                    act.activation(ak[:, tiles, :, 1, :], bank[3][:].rearrange("p (t h d) -> p t h d", h=H, d=DH),
                                   ACT.Copy).then_inc(s_nact, 1)

            @block.tensor
            def _(pe):
                for n in range(2 * B):
                    pe.wait_ge(s_sq, n + 1)
                    if n >= 2:
                        pe.wait_ge(s_lnb, n - 1)
                    pe.matmul(bank[n % 2][:], bones, sq[:, n % 4, :], start=True, stop=True).then_inc(s_ss, 1)
                pe.wait_ge(s_kn, B)
                for b in range(B):
                    if b:
                        pe.wait_ge(s_nact, 2 * b - 1)
                    for t in range(TPB):
                        m = pe.transpose(bank[2][:, P * t:P * t + P], vT[:, T * b + P * t:T * b + P * t + P], ident)
                    m.then_inc(s_nat, 1)
                    if b:
                        pe.wait_ge(s_nact, 2 * b)
                    for t in range(TPB):
                        m = pe.transpose(bank[3][:, P * t:P * t + P], kn[:, T * b + P * t:T * b + P * t + P], ident)
                    m.then_inc(s_nat, 1)
                    if b:
                        pe.wait_ge(s_ndve, 2 * b - 1)
                    pe.wait_ge(s_vb, b + 1)
                    for t in range(TPB):
                        m = pe.transpose(bank[4][:, P * t:P * t + P], vb[:, T * b + P * t:T * b + P * t + P], ident)
                    m.then_inc(s_nat, 1)
                    if b:
                        pe.wait_ge(s_ndve, 2 * b)
                    for t in range(TPB):
                        c0 = CPB * b + 4 * t
                        m = pe.transpose(bank[5][:, P * t:P * t + P], slab[:, 5, C * c0:C * c0 + P], ident)
                    m.then_inc(s_nat, 1)

            @block.vector
            def _(dve):
                dve.wait_ge(s_bt, B)
                for b in range(B):
                    cols, chunks = slice(T * b, T * b + T), slice(CPB * b, CPB * b + CPB)
                    by_chunk = lambda t: t.rearrange("p (c i) -> p c i", i=C)
                    dve.wait_ge(s_rs, 2 * b + 1)
                    dve.tensor_tensor(kbq[:, 1, chunks, :], by_chunk(qs[:, cols]), by_chunk(sq[:, (2 * b) % 4, :]),
                                      ALU.mult).then_inc(s_norm, 1)
                    dve.wait_ge(s_rs, 2 * b + 2)
                    dve.tensor_tensor(kn[:, cols], ks[:, cols], sq[:, (2 * b + 1) % 4, :], ALU.mult).then_inc(s_norm, 1)
                    dve.wait_ge(s_norm, 2 * b + 2)
                    dve.tensor_tensor(kbq[:, 0, chunks, :], by_chunk(kn[:, cols]), by_chunk(bt[:, cols]),
                                      ALU.mult).then_inc(s_kn, 1)
                for b in range(B):
                    tiles = slice(TPB * b, TPB * b + TPB)
                    for k in range(2):
                        dve.wait_ge(s_nat, 4 * b + 3 + k)
                        dve.tensor_copy(vk[:, tiles, :, k, :], bank[4 + k][:].rearrange("p (t h d) -> p t h d", h=H, d=DH)
                                        ).then_inc(s_ndve, 1)

            @block.sync
            def _(sp):
                for b in range(B):
                    sp.dma_start(v_dram.ap()[b, 0:LONG - 1, :], a["zeros"]).then_inc(s_vout, 16)
                for b in range(B):
                    sp.wait_ge(s_nact, 2 * b + 1)
                    sp.dma_start(v_dram.ap()[b, LONG - 1:, :].rearrange("(t p) d -> p t d", p=P), vnat[:, b, :, :]).then_inc(s_vout, 16)
                sp.wait_ge(s_vout, 32 * B)
        if stop == 3:
            return dump(nc, sem, out, slab, [0, 1, 5, 6])

        a_nat = slab[:, 9, :].rearrange("p (t h i) -> p t h i", h=H, i=C)
        X = slab[:, 10, :]
        s_g, s_ga, s_adma, s_xdma = sem("s_g"), sem("s_ga"), sem("s_adma"), sem("s_xdma")
        TG = 8
        with nc.Block() as block:
            @block.tensor
            def _(pe):
                for g in range(NT // TG):
                    for h in range(H):
                        if g >= 2:
                            pe.wait_ge(s_ga, H * (g - 2) + h + 1)
                        o = bank[h + 4 * (g % 2)][:].rearrange("p (t k i) -> p t k i", k=2, i=C)
                        for t in range(TG):
                            for c in range(4):
                                chunk = 4 * (TG * g + t) + c
                                m = pe.matmul(o[C * c:C * c + C, t, :, :],
                                              kn[DH * h:DH * h + DH, C * chunk:C * chunk + C],
                                              kbq[DH * h:DH * h + DH, :, chunk, :], start=True, stop=True)
                        m.then_inc(s_g, 1)

            @block.vector
            def _(dve):
                for g in range(NT // TG):
                    tiles = slice(TG * g, TG * g + TG)
                    for h in range(H):
                        dve.wait_ge(s_g, H * g + h + 1)
                        o = bank[h + 4 * (g % 2)][:].rearrange("p (t k i) -> p t k i", k=2, i=C)
                        dve.tensor_tensor(a_nat[:, tiles, h, :], o[:, :, 0, :], bc(neg_strict, 1, TG), ALU.mult)
                        dve.tensor_tensor(ak[:, tiles, h, 0, :], o[:, :, 1, :], bc(causal, 1, TG), ALU.mult).then_inc(s_ga, 1)

            @block.sync
            def _(sp):
                for g in range(NT // TG):
                    sp.wait_ge(s_ga, H * (g + 1))
                    sp.dma_start(a_dram[TG * g:TG * g + TG].rearrange("t p x -> p t x"),
                                 slab[:, 9, TG * P * g:TG * P * g + TG * P].rearrange("p (t x) -> p t x", x=P)).then_inc(s_adma, 16)
                    sp.wait_ge(s_adma, 16 * (g + 1))
                    sp.dma_start(X[4 * TG * g:4 * TG * (g + 1), :],
                                 a_dram[TG * g:TG * g + TG].rearrange("t (c j) x -> (t c) (j x)", c=4)).then_inc(s_xdma, 16)
                sp.wait_ge(s_xdma, 16 * (NT // TG))

        X4 = X.rearrange("p (j h i) -> p j h i", h=H, i=C)
        s_xd, s_xp, s_tdma, s_ttdma = sem("s_xd"), sem("s_xp"), sem("s_tdma"), sem("s_ttdma")
        HD = 3

        def invert(engine, s, h0, h1, tmp):
            link = chain(engine, s)
            nh = h1 - h0
            for m in range(1, C - 1):
                w = C - 1 - m
                prod = tmp[:, 0:m * nh * w].rearrange("p (k h i) -> p k h i", h=nh, i=w)
                link(engine.tensor_tensor(prod, bc(X4[:, m, h0:h1, m + 1:], 1, m),
                                          X4[:, 0:m, h0:h1, m:m + 1].broadcast_to([P, m, nh, w]), ALU.mult))
                link(engine.tensor_tensor(X4[:, 0:m, h0:h1, m + 1:], X4[:, 0:m, h0:h1, m + 1:], prod, ALU.add))
            for h in range(h0, h1):
                i = engine.memset(X[:, C * h:C * h + (P + 1) * (C - 1) + 1:P + 1], 1.0)
            return i

        with nc.Block() as block:
            @block.vector
            def _(dve):
                invert(dve, chain_dve, 0, HD, slab[:, 2, 0:3072]).then_inc(s_xd, 1)

            @block.gpsimd
            def _(pool):
                invert(pool, chain_pool, HD, H, slab[:, 2, 3072:4096]).then_inc(s_xp, 1)

            @block.sync
            def _(sp):
                sp.wait_ge(s_xd, 1)
                sp.wait_ge(s_xp, 1)
                sp.dma_start(t_dram.rearrange("t (c j) x -> (t c) (j x)", c=4), X).then_inc(s_tdma, 16)
                sp.wait_ge(s_tdma, 16)
                sp.dma_start(slab[:, 9, :].rearrange("p (t x) -> p t x", x=P), t_dram.rearrange("t p x -> p t x")).then_inc(s_ttdma, 16)
                sp.wait_ge(s_ttdma, 16)
        if stop == 5:
            return dump(nc, sem, out, slab, [7, 8, 9, 10])

        tt = a_nat
        uw = vk
        au = slab[:, 4, :].rearrange("p (c i) -> p c i", i=C)
        N = slab[:, 2, :].rearrange("p (c d) -> p c d", d=DH)
        s_u, s_ua, s_ud, s_pa, s_pb, s_ea, s_eb = (sem(x) for x in ("s_u", "s_ua", "s_ud", "s_pa", "s_pb", "s_ea", "s_eb"))
        with nc.Block() as block:
            @block.tensor
            def _(pe):
                for g in range(NT // 2):
                    if g >= 8:
                        pe.wait_ge(s_ua if g % 2 == 0 else s_ud, (g - 8) // 2 + 1)
                    for t in range(2 * g, 2 * g + 2):
                        for h in range(H):
                            for c in range(4):
                                q = slice(C * c, C * c + C)
                                col = 2 * DH * (H * (t % 2) + h)
                                m = pe.matmul(bank[g % 8][q, col:col + 2 * DH], tt[q, t, h, :], vk[q, t, h, :, :],
                                              start=True, stop=True)
                    m.then_inc(s_u, 1)
                pe.wait_ge(s_ua, NT // 4)
                pe.wait_ge(s_ud, NT // 4)
                for g in range(NT // TG):
                    if g:
                        pe.wait_ge(s_ea, 4 * g)
                    for t in range(TG):
                        tile = TG * g + t
                        for c in range(4):
                            q = slice(C * c, C * c + C)
                            for h in range(H):
                                m = pe.matmul(bank[c][DH * h:DH * h + DH, 2 * C * t:2 * C * t + 2 * C],
                                              uw[q, tile, h, 1, :], ak[q, tile, h, :, :], start=True, stop=True)
                    m.then_inc(s_pa, 1)
                    if g:
                        pe.wait_ge(s_eb, 4 * g)
                    for t in range(TG):
                        tile = TG * g + t
                        for c in range(4):
                            q = slice(C * c, C * c + C)
                            for h in range(H):
                                o = bank[4 + c][DH * h:DH * h + DH, 2 * C * t:2 * C * t + 2 * C]
                                pe.matmul(o[:, 0:C], uw[q, tile, h, 0, :], ak[q, tile, h, 0, :], start=True, stop=True)
                                m = pe.matmul(o[:, C:], ak[q, tile, h, 1, :], uw[q, tile, h, 0, :], start=True, stop=True)
                    m.then_inc(s_pb, 1)

            @block.scalar
            def _(act):
                for g in range(0, NT // 2, 2):
                    act.wait_ge(s_u, g + 1)
                    act.activation(uw[:, 2 * g:2 * g + 2].rearrange("p t h k d -> p (t h k d)"), bank[g % 8][:], ACT.Copy).then_inc(s_ua, 1)
                for g in range(NT // TG):
                    act.wait_ge(s_pb, g + 1)
                    for c in range(4):
                        o = bank[4 + c][:].rearrange("p (t k i) -> p t k i", k=2, i=C)
                        chunks = slice(4 * TG * g + c, 4 * TG * (g + 1), 4)
                        act.activation(au[:, chunks, :], o[:, :, 0, :], ACT.Copy)
                        act.activation(N[:, chunks, :], o[:, :, 1, :], ACT.Copy).then_inc(s_eb, 1)

            @block.vector
            def _(dve):
                for g in range(1, NT // 2, 2):
                    dve.wait_ge(s_u, g + 1)
                    dve.tensor_copy(uw[:, 2 * g:2 * g + 2].rearrange("p t h k d -> p (t h k d)"), bank[g % 8][:]).then_inc(s_ud, 1)
                for g in range(NT // TG):
                    dve.wait_ge(s_pa, g + 1)
                    for c in range(4):
                        o = bank[c][:].rearrange("p (t k i) -> p t k i", k=2, i=C)
                        chunks = slice(4 * TG * g + c, 4 * TG * (g + 1), 4)
                        dve.tensor_tensor(kbq[:, 1, chunks, :], kbq[:, 1, chunks, :], o[:, :, 0, :], ALU.subtract)
                        dve.tensor_tensor(kbq[:, 0, chunks, :], bc(eye32, 1, TG), o[:, :, 1, :], ALU.subtract).then_inc(s_ea, 1)

        Nb = N.rearrange("p (b c) d -> p b c d", c=CPB)
        s_r, s_s, s_o, s_oe = sem("s_r"), sem("s_s"), sem("s_o"), sem("s_oe")
        with nc.Block() as block:
            @block.tensor
            def _(pe):
                for c in range(1, CPB - 1):
                    for half in range(2):
                        if c > 1:
                            pe.wait_ge(s_s, 2 * (c - 2) + half + 1)
                        for b in range(4 * half, 4 * half + 4):
                            for h in range(H):
                                q = slice(DH * h, DH * h + DH)
                                m = pe.matmul(bank[half][q, DH * (b % 4):DH * (b % 4) + DH], kbq[q, 0, CPB * b + c, :],
                                              Nb[q, b, c - 1, :], start=True, stop=True)
                        m.then_inc(s_r, 1)
                pe.wait_ge(s_s, 2 * (CPB - 2))
                for b in range(B):
                    if b >= 4:
                        pe.wait_ge(s_oe, b - 3)
                    for c in range(1, CPB):
                        for h in range(H):
                            q = slice(DH * h, DH * h + DH)
                            m = pe.matmul(bank[2 + b % 4][q, C * c:C * c + C], Nb[q, b, c - 1, :], kbq[q, 1, CPB * b + c, :],
                                          start=True, stop=True)
                    m.then_inc(s_o, 1)

            @block.vector
            def _(dve):
                for c in range(1, CPB - 1):
                    for half in range(2):
                        dve.wait_ge(s_r, 2 * (c - 1) + half + 1)
                        bs = slice(4 * half, 4 * half + 4)
                        dve.tensor_tensor(Nb[:, bs, c, :], Nb[:, bs, c, :],
                                          bank[half][:, 0:4 * DH].rearrange("p (b d) -> p b d", d=DH), ALU.add).then_inc(s_s, 1)
                for b in range(B):
                    dve.wait_ge(s_o, b + 1)
                    cols = slice(T * b + C, T * b + T)
                    dve.tensor_tensor(slab[:, 4, cols], slab[:, 4, cols], bank[2 + b % 4][:, C:], ALU.add).then_inc(s_oe, 1)
        if stop == 7:
            return dump(nc, sem, out, slab, [4, 2, 5, 6])

        win = slab[0:WIN, 5:9, :].rearrange("p s (c d) -> p (s c) d", d=D)
        toep = slab[0:WIN, 0, :].rearrange("p (d i) -> p d i", i=C)
        fo = slab[:, 1, :].rearrange("p (g c) -> p g c", c=NCH)
        fsw = sb("fsw", [P, SHORT])
        short_f, short_c, long_c, delta_c, v_c = (slab[:, s, :] for s in (10, 3, 2, 9, 4))
        s_win = [sem(f"s_win{i}") for i in range(2)]
        s_fw, s_sf, s_cp, s_ca, s_cd, s_vc = (sem(x) for x in ("s_fw", "s_sf", "s_cp", "s_ca", "s_cd", "s_vc"))
        with nc.Block() as block:
            jobs = [(k, g) for k in ("delta", "fir", "short", "long") for g in range(8)]

            def evacuated(engine, n):
                engine.wait_ge(s_ca if n % 2 == 0 else s_cd, n // 2 + 1)

            @block.sync
            def _(sp):
                sp.dma_start(toep, a["toep"]).then_inc(s_win[0], 16)
                for b in range(B):
                    src = bass.AP(v_dram, b * (LONG - 1 + T) * D, [[D, WIN], [C * D, CPB], [1, D]])
                    sp.dma_start(win[:, CPB * b:CPB * b + CPB, :], src).then_inc(s_win[0], 16)
                for n in (6, 7):
                    evacuated(sp, n)
                for b in range(B):
                    sp.dma_start(v_c[CPB * b:CPB * b + CPB, :],
                                 v_dram.ap()[b, LONG - 1:, :].rearrange("(c j) d -> c (j d)", j=C)).then_inc(s_vc, 16)
                sp.wait_ge(s_vc, 16 * B)

            @block.gpsimd
            def _(pool):
                pool.dma_start(fsw[:], a["fsw"]).then_inc(s_fw, 16)

            @block.tensor
            def _(pe):
                for n, (kind, g) in enumerate(jobs):
                    o = bank[n % 8]
                    if n >= 8:
                        evacuated(pe, n - 8)
                    if kind == "fir" and g == 0:
                        pe.wait_ge(s_win[0], 16 * (B + 1))
                    if kind == "short" and g == 0:
                        pe.wait_ge(s_sf, 1)
                    if kind == "long":
                        evacuated(pe, jobs.index(("fir", g)))
                    for i in range(4):
                        j = 4 * g + i
                        cols = slice(P * i, P * i + P)
                        if kind == "fir":
                            for h in range(H):
                                m = pe.matmul(o[DH * h:DH * h + DH, cols], toep[:, DH * h + j, :], win[:, :, DH * h + j],
                                              start=True, stop=True)
                        elif kind == "long":
                            m = pe.transpose(o[:, cols], fo[:, j, :], ident)
                        else:
                            src = slab[:, 4, :] if kind == "delta" else short_f
                            m = pe.transpose(o[:, cols], src[:, j:C * (NCH - 1) + j + 1:C], ident)
                    m.then_inc(s_cp, 1)

            def evacuate(engine, copy, parity, s, jobs_of_call):
                for n, (kind, g) in enumerate(jobs):
                    if n % 2 != parity or n not in jobs_of_call:
                        continue
                    engine.wait_ge(s_cp, n + 1)
                    o = bank[n % 8][:]
                    if kind == "long":
                        dst = long_c.rearrange("p (i h d) -> p h i d", h=H, d=DH)[:, :, :, 4 * g:4 * g + 4]
                        for h in range(H):
                            i = copy(dst[:, h, :, :], o.rearrange("p (d h i) -> p h i d", h=H, i=C)[:, h, :, :])
                        i.then_inc(s, 1)
                    else:
                        dst = {"delta": delta_c, "fir": slab[:, 1, :], "short": short_c}[kind][:, 512 * g:512 * g + 512]
                        copy(dst, o).then_inc(s, 1)

            @block.scalar
            def _(act):
                evacuate(act, lambda d, s: act.activation(d, s, ACT.Copy), 0, s_ca, range(len(jobs)))

            @block.vector
            def _(dve):
                evacuate(dve, dve.tensor_copy, 1, s_cd, range(0, 8))
                link = chain(dve, chain_dve)
                r, v = (x.rearrange("p (b t) -> p b t", t=T) for x in (short_f, vT))
                dve.wait_ge(s_fw, 16)
                link(dve.tensor_scalar(r, v, fsw[:, 2:3], None, ALU.mult))
                link(dve.scalar_tensor_tensor(r[:, :, 1:], v[:, :, :T - 1], fsw[:, 1:2], r[:, :, 1:], ALU.mult, ALU.add))
                dve.scalar_tensor_tensor(r[:, :, 2:], v[:, :, :T - 2], fsw[:, 0:1], r[:, :, 2:], ALU.mult, ALU.add).then_inc(s_sf, 1)
                evacuate(dve, dve.tensor_copy, 1, s_cd, range(8, len(jobs)))
        if stop == 8:
            return dump(nc, sem, out, slab, [3, 2, 9, 4])

        paths = [short_c, long_c, delta_c, v_c]
        NP_ = len(paths)
        K16 = H * NP_
        st = slab[:, 10, 0:1024].rearrange("p (j w h k) -> p j w h k", w=NP_, h=H, k=2)
        sums = slab[:, 10, 1024:1536].rearrange("p (w n) -> p w n", w=NP_)
        sqs = slab[:, 10, 1536:2048].rearrange("p (w n) -> p w n", w=NP_)
        m2 = slab[:, 10, 2048:2560].rearrange("p (w n) -> p w n", w=NP_)
        stT = slab[0:C, 1, :]
        small = slab[:, 10, 2560:4096]
        w1T, w2T = small[:, 0:HID], small[:, 256:288].rearrange("p (m k) -> p m k", m=2)
        b1 = small[:, 288:290]
        w1sT = small[0:C, 290:290 + HID]
        tmp16 = small[0:K16, 546:554]
        fl = small[:, 554:570]
        flt = small[:, 570:586]
        s_sqr, s_red, s_gw, s_st, s_stp, s_sta, s_std, s_tmp, s_tv = (
            sem(x) for x in ("s_sqr", "s_red", "s_gw", "s_st", "s_stp", "s_sta", "s_std", "s_tmp", "s_tv"))
        with nc.Block() as block:
            @block.sync
            def _(sp):
                for dst, name in ((w1T, "w1T"), (w2T, "w2T"), (b1, "b1"), (w1sT, "w1sT"), (tmp16[:, 0:2], "temp_bias")):
                    sp.dma_start(dst, a[name]).then_inc(s_gw, 16)
                sp.dma_start(fl, a["floor"].partition_broadcast(P)).then_inc(s_gw, 16)
                sp.wait_ge(s_gw, 96)

            @block.scalar
            def _(act):
                act.preload_act_table_set("natural_log_exp_and_others")
                link = chain(act, chain_act)
                for w in range(NP_):
                    act.activation(slab[:, 5 + w, :], paths[w], ACT.Square).then_inc(s_sqr, 1)
                act.wait_ge(s_gw, 96)
                link(act.activation(tmp16[:, 2:3], tmp16[:, 0:1], ACT.Abs))
                link(act.activation(tmp16[:, 3:4], tmp16[:, 2:3], ACT.Exp, scale=-1.0))
                act.activation(tmp16[:, 4:5], tmp16[:, 3:4], ACT.Ln, bias=one1[0:K16]).then_inc(s_tmp, 1)
                act.activation(flt, fl, ACT.Exp, scale=-1.0).then_inc(s_tmp, 1)
                for g in range(0, 8, 2):
                    act.wait_ge(s_stp, g + 1)
                    for i in range(4):
                        k = act.activation(stT[:, 4 * g + i:C * (NCH - 1) + 4 * g + i + 1:C],
                                           bank[g][C * i:C * i + C, 0:P], ACT.Copy)
                    k.then_inc(s_sta, 1)

            @block.vector
            def _(dve):
                link = chain(dve, chain_dve)
                for w in range(NP_):
                    dve.tensor_reduce(sums[:, w, :], paths[w].rearrange("p (n d) -> p n d", d=DH), AX, ALU.add).then_inc(s_red, 1)
                    dve.wait_ge(s_sqr, w + 1)
                    dve.tensor_reduce(sqs[:, w, :], slab[:, 5 + w, :].rearrange("p (n d) -> p n d", d=DH), AX, ALU.add).then_inc(s_red, 1)
                dve.wait_ge(s_red, 2 * NP_)
                for w in range(NP_):
                    i = dve.tensor_scalar(st[:, :, w, :, 0], sums[:, w, :].rearrange("p (j h) -> p j h", h=H), 1.0 / DH, None, ALU.mult)
                link(i)
                for w in range(NP_):
                    i = dve.tensor_tensor(m2[:, w, :].rearrange("p (j h) -> p j h", h=H), st[:, :, w, :, 0], st[:, :, w, :, 0], ALU.mult)
                link(i)
                for w in range(NP_):
                    i = dve.scalar_tensor_tensor(st[:, :, w, :, 1], sqs[:, w, :].rearrange("p (j h) -> p j h", h=H), 1.0 / DH,
                                                 m2[:, w, :].rearrange("p (j h) -> p j h", h=H), ALU.mult, ALU.subtract)
                i.then_inc(s_st, 1)
                dve.wait_ge(s_tmp, 2)
                link(dve.tensor_scalar(tmp16[:, 5:6], tmp16[:, 0:1], 0.0, 1e-4, ALU.max, ALU.add))
                link(dve.tensor_tensor(tmp16[:, 6:7], tmp16[:, 5:6], tmp16[:, 4:5], ALU.add))
                link(dve.reciprocal(tmp16[:, 7:8], tmp16[:, 6:7]))
                link(dve.tensor_scalar(flt, flt, 1.0, None, ALU.add))
                link(dve.reciprocal(fl, flt))
                link(dve.tensor_scalar(fl, fl, 0.05, None, ALU.mult))
                for g in range(1, 8, 2):
                    dve.wait_ge(s_stp, g + 1)
                    for i in range(4):
                        k = dve.tensor_copy(stT[:, 4 * g + i:C * (NCH - 1) + 4 * g + i + 1:C], bank[g][C * i:C * i + C, 0:P])
                    k.then_inc(s_std, 1)

            @block.tensor
            def _(pe):
                pe.wait_ge(s_st, 1)
                for g in range(8):
                    pe.transpose(bank[g][:, 0:P], slab[:, 10, P * g:P * g + P], ident).then_inc(s_stp, 1)

        hm = slab[:, 6:8, 0:2048].rearrange("p n (m t) -> p n m t", m=4)
        lT = slab[0:K16, 8, :]
        probs = slab[:, 7, 2048:2560].rearrange("p (n w) -> p n w", w=NP_)
        s_hm, s_gel, s_lg, s_lt, s_ltt = (sem(x) for x in ("s_hm", "s_gel", "s_lg", "s_lt", "s_ltt"))
        with nc.Block() as block:
            @block.tensor
            def _(pe):
                def logits(b):
                    pe.wait_ge(s_gel, 2 * b + 2)
                    if b >= 2:
                        pe.wait_ge(s_lt, b - 1)
                    for k in range(2):
                        m = pe.matmul(bank[4 + b % 2][0:K16, :], w2T[:, k, :], hm[:, b % 2, k, :], start=k == 0, stop=k == 1)
                    m.then_inc(s_lg, 1)

                for b in range(B):
                    for k in range(2):
                        n = 2 * b + k
                        if n >= 4:
                            pe.wait_ge(s_gel, n - 3)
                        o = bank[n % 4]
                        pe.matmul(o[:], w1T[:, P * k:P * k + P], hT[:, b, TAPS - 1:HPAD], start=True, stop=False)
                        pe.matmul(o[:], w1sT[:, P * k:P * k + P], stT[:, T * b:T * b + T], start=False, stop=True).then_inc(s_hm, 1)
                    if b:
                        logits(b - 1)
                logits(B - 1)
                pe.wait_ge(s_lt, B)
                for j in range(C):
                    m = pe.transpose(bank[6][:, K16 * j:K16 * j + K16], lT[:, j:C * (NCH - 1) + j + 1:C], ident[0:K16, 0:K16])
                m.then_inc(s_ltt, 1)

            @block.scalar
            def _(act):
                for b in range(B):
                    for k in range(2):
                        n = 2 * b + k
                        act.wait_ge(s_hm, n + 1)
                        if b >= 2:
                            act.wait_ge(s_lg, b - 1)
                        act.activation(hm[:, b % 2, k, :], bank[n % 4][:], ACT.Gelu, bias=b1[:, k:k + 1]).then_inc(s_gel, 1)

            @block.vector
            def _(dve):
                for b in range(B):
                    dve.wait_ge(s_lg, b + 1)
                    dve.tensor_scalar(lT[:, T * b:T * b + T], bank[4 + b % 2][0:K16, :], tmp16[:, 1:2], tmp16[:, 7:8],
                                      ALU.add, ALU.mult).then_inc(s_lt, 1)

        mixT = slab[:, 1, :]
        x1 = slab[:, 0, :].rearrange("p (t d) -> p t d", d=D)
        gt = slab[:, 10, 0:1024].rearrange("p (s n) -> p s n", n=P)
        e = slab[:, 7, 2560:3072].rearrange("p (n w) -> p n w", w=NP_)
        woT = slab[:, 7, 3072:3072 + D]
        onorm = slab[:, 7, 3200:3201]
        wga = slab[:, 7, 3328:3328 + D]
        crep = slab[:, 10, 1024:2048].rearrange("p (b n) -> p b n", b=B)
        gaR = slab[:, 10, 2048:3072].rearrange("p (b n) -> p b n", b=B)
        gab = slab[:, 10, 3072:4096].rearrange("p (b n) -> p b n", b=B)
        stx = slab[:, 10, 3200:3200 + 6 * NT].rearrange("p (t s) -> p t s", s=6)
        s_vp = sem("s_vp")
        s_xagain, s_wo, s_mx, s_ex, s_pr, s_crep, s_ga2, s_wog, s_m1, s_mix, s_ms, s_rr, s_mixn, s_mt, s_mte, s_wp, s_x1 = (
            sem(x) for x in ("s_xagain", "s_wo", "s_mx", "s_ex", "s_pr", "s_crep", "s_ga2", "s_wog", "s_m1", "s_mix", "s_ms", "s_rr",
                             "s_mixn", "s_mt", "s_mte", "s_wp", "s_x1done"))
        JQ = 4
        with nc.Block() as block:
            @block.sync
            def _(sp):
                sp.dma_start(woT, a["woT"]).then_inc(s_wo, 16)
                sp.dma_start(onorm, a["onorm"]).then_inc(s_wo, 16)
                sp.dma_start(wga, a["wga"]).then_inc(s_wo, 16)
                sp.dma_start(x1, a["x"].rearrange("t p d -> p t d")).then_inc(s_xagain, 16)

            @block.tensor
            def _(pe):
                pe.wait_ge(s_crep, 1)
                pe.wait_ge(s_wo, 48)
                for b in range(B):
                    m = pe.matmul(bank[4 + b // 4][:, P * (b % 4):P * (b % 4) + P], crep[:, b, :], wga, start=True, stop=True)
                m.then_inc(s_ga2, 1)
                for q in range(JQ):
                    pe.wait_ge(s_mixn, q + 1)
                    for g in range(2):
                        n = 2 * q + g
                        if n >= 4:
                            pe.wait_ge(s_mte, n - 3)
                        for i in range(4):
                            j = 4 * n + i
                            m = pe.transpose(bank[n % 4][:, P * i:P * i + P], slab[:, 5, P * j:P * j + P], ident)
                        m.then_inc(s_mt, 1)
                pe.wait_ge(s_mte, 8)
                pe.wait_ge(s_wog, B)
                for b in range(B):
                    if b >= 4:
                        pe.wait_ge(s_x1, b - 3)
                    for t in range(TPB):
                        m = pe.matmul(bank[b % 4][:, P * t:P * t + P], mixT[:, T * b + P * t:T * b + P * t + P], gaR[:, b, :],
                                      start=True, stop=True)
                    m.then_inc(s_wp, 1)

            @block.scalar
            def _(act):
                act.preload_act_table_set("natural_log_exp_and_others")
                act.wait_ge(s_mx, 1)
                act.activation(e, e, ACT.Exp).then_inc(s_ex, 1)
                link = chain(act, chain_act)
                for q in range(JQ):
                    part = slice(1024 * q, 1024 * q + 1024)
                    act.wait_ge(s_mix, q + 1)
                    act.activation(slab[:, 6, part], slab[:, 5, part], ACT.Square).then_inc(s_m1, 1)
                    act.wait_ge(s_ms, q + 1)
                    n = slice(32 * q, 32 * q + 32)
                    link(act.activation(gt[:, 5, n], gt[:, 4, n], ACT.Ln, bias=eps_ln, scale=1.0 / DH))
                    act.activation(gt[:, 6, n], gt[:, 5, n], ACT.Exp, scale=-0.5).then_inc(s_rr, 1)
                for n in range(8):
                    act.wait_ge(s_mt, n + 1)
                    dst = mixT.rearrange("p (c j) -> p c j", j=C)[:, :, 4 * n:4 * n + 4]
                    act.activation(dst, bank[n % 4][:].rearrange("p (j c) -> p c j", j=4), ACT.Copy).then_inc(s_mte, 1)

            @block.gpsimd
            def _(pool):
                pool.tensor_copy(crep, bc(cT[:], 2, P)).then_inc(s_crep, 1)
                pool.wait_ge(s_pr, 1)
                for q in range(JQ):
                    link = chain(pool, chain_pool)
                    part, n = slice(1024 * q, 1024 * q + 1024), slice(32 * q, 32 * q + 32)
                    v3 = lambda t: t[:, part].rearrange("p (n d) -> p n d", d=DH)
                    pool.tensor_tensor(v3(v_c), v3(v_c), bc(probs[:, n, 3], 2, DH), ALU.mult).then_inc(s_vp, 1)

            @block.vector
            def _(dve):
                link = chain(dve, chain_dve)
                logit = bank[6][:].rearrange("p (n w) -> p n w", w=NP_)
                link(dve.tensor_reduce(gt[:, 0, :], logit, AX, ALU.max))
                dve.tensor_tensor(e, logit, bc(gt[:, 0, :], 2, NP_), ALU.subtract).then_inc(s_mx, 1)
                dve.wait_ge(s_ex, 1)
                link(dve.tensor_reduce(gt[:, 1, :], e, AX, ALU.add))
                link(dve.reciprocal(gt[:, 2, :], gt[:, 1, :]))
                link(dve.tensor_tensor(e, e, bc(gt[:, 2, :], 2, NP_), ALU.mult))
                link(dve.tensor_tensor(e.rearrange("p (j h) w -> p j (h w)", h=H), e.rearrange("p (j h) w -> p j (h w)", h=H),
                                       bc(fl, 1, C), ALU.max))
                link(dve.tensor_reduce(gt[:, 1, :], e, AX, ALU.add))
                link(dve.reciprocal(gt[:, 2, :], gt[:, 1, :]))
                dve.tensor_tensor(probs, e, bc(gt[:, 2, :], 2, NP_), ALU.mult).then_inc(s_pr, 1)
                dve.wait_ge(s_pr, 1)
                for q in range(JQ):
                    part, n = slice(1024 * q, 1024 * q + 1024), slice(32 * q, 32 * q + 32)
                    v3 = lambda t: t[:, part].rearrange("p (n d) -> p n d", d=DH)
                    mixed = slab[:, 5, :]
                    dve.tensor_tensor(v3(mixed), v3(short_c), bc(probs[:, n, 0], 2, DH), ALU.mult)
                    dve.tensor_tensor(v3(long_c), v3(long_c), bc(probs[:, n, 1], 2, DH), ALU.mult)
                    link(dve.tensor_tensor(v3(delta_c), v3(delta_c), bc(probs[:, n, 2], 2, DH), ALU.mult))
                    link(dve.tensor_tensor(mixed[:, part], mixed[:, part], long_c[:, part], ALU.add))
                    link(dve.tensor_tensor(mixed[:, part], mixed[:, part], delta_c[:, part], ALU.add))
                    dve.wait_ge(s_vp, q + 1)
                    dve.tensor_tensor(mixed[:, part], mixed[:, part], v_c[:, part], ALU.add).then_inc(s_mix, 1)
                    dve.wait_ge(s_m1, q + 1)
                    dve.tensor_reduce(gt[:, 4, n], slab[:, 6, part].rearrange("p (n d) -> p n d", d=DH), AX, ALU.add).then_inc(s_ms, 1)
                    dve.wait_ge(s_rr, q + 1)
                    dve.tensor_tensor(v3(mixed), v3(mixed), bc(gt[:, 6, n], 2, DH), ALU.mult).then_inc(s_mixn, 1)
                dve.wait_ge(s_ga2, 1)
                for k in range(2):
                    half = slice(4 * k, 4 * k + 4)
                    o = bank[4 + k][:].rearrange("p (b n) -> p b n", b=4)
                    i = dve.tensor_copy(gab[:, half, :], o)
                link(i)
                gate_sign(dve, link, gaR, gab, gab)
                link(dve.tensor_scalar(woT, woT, onorm, None, ALU.mult))
                for b in range(B):
                    dve.tensor_tensor(gaR[:, b, :], gaR[:, b, :], woT, ALU.mult).then_inc(s_wog, 1)
                dve.wait_ge(s_xagain, 16)
                for b in range(B):
                    dve.wait_ge(s_wp, b + 1)
                    tiles = slice(TPB * b, TPB * b + TPB)
                    link(dve.tensor_tensor(x1[:, tiles, :], x1[:, tiles, :], bank[b % 4][:].rearrange("p (t d) -> p t d", d=D),
                                           ALU.add))
                    for t in range(TPB * b, TPB * b + TPB):
                        i = dve.bn_stats(stx[:, t, :], x1[:, t, :])
                    i.then_inc(s_x1, 1)
        if stop == 11:
            return dump(nc, sem, out, slab, [0, 5, 1, 7])

        w2 = slab[:, 1, 0:4 * D].rearrange("p (k d) -> p k d", k=4)
        wmod2 = slab[:, 1, 512:896]
        cols = slab[:, 1, 896:902]
        vbR = slab[:, 1, 1024:1024 + D]
        obR = slab[:, 1, 1152:1152 + T].rearrange("p (t d) -> p t d", d=D)
        modR = slab[:, 2, 0:3 * B * D].rearrange("p (b k d) -> p b k d", b=B, k=3)
        gtmp = slab[:, 2, 3 * B * D:].rearrange("p (b d) -> p b d", b=B)
        gtmp2 = slab[:, 3, 0:B * D].rearrange("p (b d) -> p b d", b=B)
        identb = sb("identb", [P, P], BF16)
        nb = slab[:, 3, :].rearrange("p (n t) -> p n t", t=T)
        h2buf = [nb[:, k, :] for k in range(3)]
        xh2, xn2 = nb[:, 3, :], nb[:, 4, :]
        outbuf = [nb[:, 5 + k, :] for k in range(2)]
        fb = slab[:, 4, :].rearrange("p (n t) -> p n t", t=T)
        xnT = [fb[:, k, :] for k in range(2)]
        qf, kf, att, attT = fb[:, 2, :], fb[:, 3, :], fb[:, 4, :], fb[:, 5, :]
        t1 = fb[:, 6, :]
        half = lambda k, n: slab[:, k, :].bitcast(BF16)[:, n * 4096:n * 4096 + 4096].rearrange("p (h t) -> p h t", h=FH)
        qstack = [half(5 + k, 0) for k in range(3)]
        kstack = [half(5 + k, 1) for k in range(3)]
        vaug = [slab[:, 8, 1024 * k:1024 * k + 1024].rearrange("p (t h d) -> p t h d", t=TPB, h=FH) for k in range(3)]
        oc = [slab[:, 8, 3072 + T * k:3072 + T * k + T] for k in range(2)]
        pT = slab[:, 9, :].rearrange("p (n t) -> p n t", t=T)
        sp10 = slab[:, 10, :]
        qparts = sp10[:, 0:768].bitcast(BF16).rearrange("p (n t) -> p n t", n=3)
        kparts = sp10[:, 768:1536].bitcast(BF16).rearrange("p (n t) -> p n t", n=3)
        res = sp10[:, 1536:2048]
        mx = sp10[:, 2048:2080]
        mm = sp10[:, 2080:2112].bitcast(BF16)
        mT = sp10[0:2 * 32, 2112:2176].bitcast(BF16)
        st3 = sp10[:, 2208:2232].rearrange("p (t s) -> p t s", s=6)
        mv3 = sp10[:, 2232:2240].rearrange("p (t s) -> p t s", s=2)
        rr = sp10[:, 2240:2256].rearrange("p (n t) -> p n t", t=TPB)
        rc = sp10[:, 2256:2288].rearrange("p (g t h) -> p g t h", g=2, t=TPB)
        mvx = slab[:, 10, 3072:3072 + 2 * NT].rearrange("p (t s) -> p t s", s=2)
        lnx = slab[:, 10, 3136:3136 + NT]
        rx = slab[:, 10, 3168:3168 + NT]
        s_mvx, s_lnx, s_rx = sem("s_mvx"), sem("s_lnx"), sem("s_rx")
        crep8 = slab[:, 10, 0:1024].rearrange("p (b n) -> p b n", b=B)
        scale = float(D) ** -0.5
        s_w2, s_cr, s_mr2, s_ms2, s_me2 = (sem(x) for x in ("s_w2", "s_cr", "s_mr2", "s_ms2", "s_me2"))
        with nc.Block() as block:
            @block.sync
            def _(sp):
                sp.dma_start(w2, a["w2"]).then_inc(s_w2, 16)
                sp.dma_start(wmod2, a["wmod2"]).then_inc(s_w2, 16)
                sp.dma_start(cols[:, 0:4], a["cols"]).then_inc(s_w2, 16)
                sp.dma_start(vbR, a["v_b"].partition_broadcast(P)).then_inc(s_w2, 16)
                sp.dma_start(slab[:, 1, 1152:1152 + T], a["obR"].partition_broadcast(P)).then_inc(s_w2, 16)

            @block.gpsimd
            def _(pool):
                link = chain(pool, chain_pool)
                link(pool.tensor_copy(identb[:], ident))
                link(pool.memset(xnT[0], 0.0))
                for k in range(3):
                    link(pool.memset(kstack[k][96:98, :, :], 1.0))
                    link(pool.memset(vaug[k][:, :, :, FD:FD + 1], 1.0))
                    link(pool.memset(vaug[k][:, :, :, FD + 1:], 0.0))

            @block.tensor
            def _(pe):
                pe.wait_ge(s_w2, 80)
                for b in range(B):
                    pe.wait_ge(s_cr, b + 1)
                    pe.matmul(bank[b][:, 0:3 * D], crep8[:, b, :], wmod2, start=True, stop=True).then_inc(s_mr2, 1)

            @block.scalar
            def _(act):
                act.preload_act_table_set("natural_log_exp_and_others")
                act.wait_ge(s_mvx, 1)
                act.activation(lnx, mvx[:, :, 1], ACT.Ln, bias=eps_ln).then_inc(s_lnx, 1)
                act.wait_ge(s_lnx, 1)
                act.activation(rx, lnx, ACT.Exp, scale=-0.5).then_inc(s_rx, 1)
                act.wait_ge(s_rx, 1)

            @block.vector
            def _(dve):
                link = chain(dve, chain_dve)
                for t in range(NT):
                    i = dve.bn_aggr(mvx[:, t, :], stx[:, t, :])
                i.then_inc(s_mvx, 1)
                for b in range(B):
                    dve.tensor_copy(crep8[:, b, :], cT[:, b:b + 1].broadcast_to([P, P])).then_inc(s_cr, 1)
                dve.wait_ge(s_w2, 80)
                link(dve.tensor_scalar(cols[:, 4:5], cols[:, 2:3], scale, None, ALU.mult))
                for b in range(B):
                    dve.wait_ge(s_mr2, b + 1)
                    o = bank[b][:, 0:3 * D].rearrange("p (k d) -> p k d", k=3)
                    dve.tensor_copy(modR[:, b, 0, :], o[:, 0, :])
                    dve.tensor_scalar(modR[:, b, 1, :], o[:, 1, :], 1.0, None, ALU.add)
                    i = dve.tensor_copy(gtmp[:, b, :], o[:, 2, :])
                link(i)
                gate_sign(dve, link, modR[:, :, 2, :], gtmp, gtmp2)

        QP = (0, 0, 1, 1, 0, 2)
        KP = (0, 1, 0, 1, 2, 0)
        part_dram = nc.dram_tensor("qk_parts", (2, FH, FD, 3, T), BF16, kind="Internal").ap()
        m_dram = nc.dram_tensor("neg_max", (64, P), BF16, kind="Internal").ap()
        names = ("f_v1 f_r1 f_xh f_h2 f_v2 f_r2 f_xn f_tT f_xnT f_q f_qf f_k f_kf f_v f_V f_split f_spq f_spk f_stack "
                 "f_s1 f_max f_mm f_mT f_mr f_mw f_mq f_sT f_exp f_pv f_oc f_oT f_rc f_at f_aT f_attT f_op f_t1 f_y "
                 "f_out f_store f_ln f_ob f_st2 f_st3 f_rcy f_mh").split()
        s = {n: sem(n) for n in names}

        def attention(engine, stage):
            for k in (-2, -1):
                stage(k, k % 3, k + 2 < B, k + 1 >= 0, k >= 0)
            with engine.Fori(0, 2) as trip:
                for r in range(3):
                    stage(trip * 3 + r, r, True, True, True)
            for k in (6, 7):
                stage(k, k % 3, False, k + 1 < B, True)

        with nc.Block() as block:
            @block.sync
            def _(sp):
                def stage(k, r, do_a, do_m, do_b):
                    if do_a:
                        b, rb = k + 2, (r + 2) % 3
                        for n, (parts, stack, which, written) in enumerate(((qparts, qstack[rb], QP, "f_spq"),
                                                                            (kparts, kstack[rb], KP, "f_spk"))):
                            sp.wait_ge(s["f_split"], 2 * b + n + 1)
                            sp.dma_start(part_dram[n].rearrange("h d n t -> (h d) n t"), parts).then_inc(s[written], 16)
                            sp.wait_ge(s[written], 16 * b + 16)
                            for g in range(6):
                                sp.dma_start(stack[FD * g:FD * g + FD, :, :],
                                             part_dram[n, :, :, which[g], :].rearrange("h d t -> d h t")).then_inc(s["f_stack"], 16)
                    if do_m:
                        b, rb = k + 1, (r + 1) % 3
                        sp.wait_ge(s["f_mr"], b + 1)
                        sp.dma_start(m_dram, mT).then_inc(s["f_mw"], 16)
                        sp.wait_ge(s["f_mw"], 16 * b + 16)
                        sp.dma_start(qstack[rb][96:98, :, :], m_dram.rearrange("(n h t) q -> n h (t q)", n=2, h=FH)).then_inc(s["f_mq"], 16)
                    if do_b:
                        b = k
                        sp.wait_ge(s["f_out"], b + 1)
                        if isinstance(b, int):
                            dst, src = out[TPB * b:TPB * b + TPB], x1[:, TPB * b:TPB * b + TPB, :]
                        else:
                            dst, src = out[bass.ds(b * TPB, TPB)], x1[:, bass.ds(b * TPB, TPB), :]
                        sp.dma_start(dst.rearrange("t p d -> p t d"), src).then_inc(s["f_store"], 16)
                attention(sp, stage)
                sp.wait_ge(s["f_store"], 16 * B)

            @block.tensor
            def _(pe):
                misc, obank = bank[7], bank[6]

                def share(i):
                    return (28 * i) // 16, (28 * (i + 1)) // 16

                def stage(k, r, do_a, do_m, do_b):
                    a_, m_, b_ = k + 2, k + 1, k
                    ra, rm, rb = (r + 2) % 3, (r + 1) % 3, r
                    pa = {}

                    def pass1(n0, n1):
                        for n in range(n0, n1):
                            h, t = n // TPB, n % TPB
                            if n == 0:
                                pe.wait_ge(s["f_stack"], 192 * m_ + 192)
                            if not (n < 2 and isinstance(k, int) and k == -1):
                                pe.wait_ge(s["f_max"], 32 * m_ + n - 1)
                            pe.matmul(bank[n % 2][:], qstack[rm][0:96, h, P * t:P * t + P], kstack[rm][0:96, h, :],
                                      start=True, stop=True).then_inc(s["f_s1"], 1)

                    def scoresT(u, pr):
                        g, kt = u // 4, u % 4
                        n = 2 * u + pr
                        if n == 0:
                            pe.wait_ge(s["f_mq"], 16 * b_ + 16)
                        if n >= 2:
                            pe.wait_ge(s["f_exp"], 16 * b_ + n - 1)
                        for i in range(2):
                            h = 4 * g + 2 * pr + i
                            m = pe.matmul(bank[2 + 2 * pr + i][:], kstack[rb][0:98, h, P * kt:P * kt + P],
                                          qstack[rb][0:98, h, :], start=True, stop=True)
                        m.then_inc(s["f_sT"], 1)

                    def pv(u):
                        g, kt = u // 4, u % 4
                        if u == 0:
                            pe.wait_ge(s["f_V"], b_ + 1)
                        if kt == 0 and g == 1:
                            pe.wait_ge(s["f_oc"], 2 * b_ + 1)
                        pe.wait_ge(s["f_exp"], 16 * b_ + 2 * u + 2)
                        for i in range(4):
                            m = pe.matmul(obank[32 * i:32 * i + 32, :], vaug[rb][:, kt, 4 * g + i, :], pT[:, 4 * (u % 2) + i, :],
                                          start=kt == 0, stop=kt == 3)
                        m.then_inc(s["f_pv"], 1)

                    def otrans(g):
                        pe.wait_ge(s["f_oc"], 2 * b_ + g + 1)
                        for t in range(TPB):
                            m = pe.transpose(misc[:, P * t:P * t + P], oc[g][:, P * t:P * t + P], ident)
                        m.then_inc(s["f_oT"], 1)

                    def xtrans():
                        pe.wait_ge(s["f_xn"], a_ + 1)
                        for t in range(TPB):
                            m = pe.transpose(misc[:, P * t:P * t + P], xn2[:, P * t:P * t + P], ident)
                        m.then_inc(s["f_tT"], 1)

                    def proj(kind):
                        if kind == 0:
                            pe.wait_ge(s["f_xnT"], a_ + 1)
                            pe.matmul(misc[:], w2[:, 0, :], xnT[0], start=True, stop=True).then_inc(s["f_q"], 1)
                        elif kind == 1:
                            pe.wait_ge(s["f_qf"], a_ + 1)
                            pe.matmul(misc[:], w2[:, 1, :], xnT[0], start=True, stop=True).then_inc(s["f_k"], 1)
                        else:
                            pe.wait_ge(s["f_kf"], a_ + 1)
                            for t in range(TPB):
                                m = pe.matmul(misc[:, P * t:P * t + P], xnT[0][:, P * t:P * t + P], w2[:, 2, :], start=True, stop=True)
                            m.then_inc(s["f_v"], 1)

                    def atrans():
                        pe.wait_ge(s["f_at"], 2 * b_ + 2)
                        for t in range(TPB):
                            m = pe.transpose(misc[:, P * t:P * t + P], att[:, P * t:P * t + P], ident)
                        m.then_inc(s["f_aT"], 1)

                    def oproj():
                        pe.wait_ge(s["f_attT"], b_ + 1)
                        for t in range(TPB):
                            w = D >> t
                            m = pe.matmul(misc[:, P * t:P * t + w], attT[0:w, P * t:P * t + P], w2[0:w, 3, 0:w], start=True, stop=True)
                        m.then_inc(s["f_op"], 1)

                    for u in range(8):
                        for pr in range(2):
                            if do_b:
                                scoresT(u, pr)
                            if do_m:
                                pass1(*share(2 * u + pr))
                        if do_b and u:
                            pv(u - 1)
                        if do_a and u == 1:
                            xtrans()
                        if do_a and u in (2, 3, 4):
                            proj(u - 2)
                        if do_b and u == 6:
                            if do_a:
                                pe.wait_ge(s["f_V"], a_ + 1)
                            otrans(0)
                    if do_b:
                        pv(7)
                    if do_b:
                        pe.wait_ge(s["f_at"], 2 * b_ + 1)
                        otrans(1)
                    if do_m:
                        pass1(28, 30)
                    if do_b:
                        atrans()
                    if do_m:
                        pass1(30, 32)
                    if do_b:
                        oproj()
                    if do_m:
                        pe.wait_ge(s["f_mm"], m_ + 1)
                        pe.transpose(obank[0:32, 0:64].bitcast(BF16), mm[:, 0:32], identb[:])
                        pe.transpose(obank[32:64, 0:64].bitcast(BF16), mm[:, 32:64], identb[:]).then_inc(s["f_mT"], 1)
                        pe.wait_ge(s["f_mr"], m_ + 1)
                    if do_b:
                        pe.wait_ge(s["f_rcy"], b_ + 1)
                    elif do_a and do_m:
                        pe.wait_ge(s["f_V"], a_ + 1)
                attention(pe, stage)

            @block.scalar
            def _(act):
                misc, obank = bank[7], bank[6]
                act.preload_act_table_set("natural_log_exp_and_others")

                def stage(k, r, do_a, do_m, do_b):
                    a_, m_, b_ = k + 2, k + 1, k
                    static = isinstance(k, int)

                    def rstd():
                        act.wait_ge(s["f_v2"], a_ + 1)
                        act.activation(rr[:, 0, :], mv3[:, :, 1], ACT.Ln, bias=eps_ln).then_inc(s["f_ln"], 1)
                        act.wait_ge(s["f_ln"], a_ + 1)
                        act.activation(rr[:, 1, :], rr[:, 0, :], ACT.Exp, scale=-0.5).then_inc(s["f_r2"], 1)

                    def exps(u):
                        for pr in range(2):
                            n = 2 * u + pr
                            act.wait_ge(s["f_sT"], 16 * b_ + n + 1)
                            if u >= 2:
                                act.wait_ge(s["f_pv"], 8 * b_ + u - 1)
                            src = wide[pr]
                            act.activation(pT[:, 4 * (u % 2) + 2 * pr:4 * (u % 2) + 2 * pr + 2, :], src, ACT.Exp).then_inc(s["f_exp"], 1)

                    def xevac():
                        act.wait_ge(s["f_tT"], a_ + 1)
                        for t in range(TPB):
                            w = D >> t
                            i = act.activation(xnT[0][0:w, P * t:P * t + P], misc[0:w, P * t:P * t + P], ACT.Identity,
                                               bias=cols[0:w, 1:2], scale=cols[0:w, 0:1])
                        i.then_inc(s["f_xnT"], 1)

                    def qkevac(kind):
                        if kind == 0:
                            act.wait_ge(s["f_q"], a_ + 1)
                            if not (static and k == -2):
                                act.wait_ge(s["f_split"], 2 * a_)
                            act.activation(qf, misc[:], ACT.Identity, bias=cols[:, 4:5], scale=scale).then_inc(s["f_qf"], 1)
                        else:
                            act.wait_ge(s["f_k"], a_ + 1)
                            act.activation(kf, misc[:], ACT.Identity, bias=cols[:, 3:4]).then_inc(s["f_kf"], 1)

                    def ocevac(g):
                        act.wait_ge(s["f_pv"], 8 * b_ + 4 * g + 4)
                        act.activation(oc[g], obank[:], ACT.Copy).then_inc(s["f_oc"], 1)

                    for u in range(8):
                        if do_b:
                            exps(u)
                            if u == 4:
                                ocevac(0)
                        if do_a and u == 0:
                            rstd()
                        if do_a and u == 1:
                            xevac()
                        if do_a and u in (2, 3):
                            qkevac(u - 2)
                    if do_b:
                        ocevac(1)
                        act.wait_ge(s["f_aT"], b_ + 1)
                        act.activation(attT, misc[:], ACT.Copy).then_inc(s["f_attT"], 1)
                    if do_m:
                        act.wait_ge(s["f_mT"], m_ + 1)
                        if not (static and k == -1):
                            act.wait_ge(s["f_mw"], 16 * m_)
                        act.activation(mT, obank[0:64, 0:64].bitcast(BF16), ACT.Copy).then_inc(s["f_mr"], 1)
                attention(act, stage)

            @block.gpsimd
            def _(pool):
                def batch(t, b, i=None):
                    if isinstance(b, int):
                        return t[:, b, i, :]
                    return t[:, bass.ds(b, 1), i, :].rearrange("p o d -> p (o d)")

                def stage(k, r, do_a, do_m, do_b):
                    a_, b_ = k + 2, k
                    static = isinstance(k, int)
                    h2 = h2buf[(r + 2) % 3]
                    link = lambda i, n: (i.then_inc(s["f_ob"], 1), pool.wait_ge(s["f_ob"], 9 * a_ + n))
                    if do_a:
                        v = lambda t: t.rearrange("p (t d) -> p t d", d=D)
                        pool.wait_ge(s["f_xh"], a_ + 1)
                        link(pool.tensor_tensor(v(xh2), v(xh2), bc(batch(modR, a_, 1), 1, TPB), ALU.mult), 1)
                        pool.tensor_tensor(v(h2), v(xh2), bc(batch(modR, a_, 0), 1, TPB), ALU.add).then_inc(s["f_h2"], 1)
                    if do_b:
                        if not do_a:
                            pool.wait_ge(s["f_y"], b_)
                        pool.tensor_tensor(t1, h2buf[r], slab[:, 1, 1152:1152 + T], ALU.add).then_inc(s["f_t1"], 1)
                    round_ = lambda dst, src: pool.tensor_tensor(dst, src, one1.broadcast_to([P, T]), ALU.mult)
                    if do_a:
                        for n, (src, parts, ready, written) in enumerate(((qf, qparts, "f_qf", "f_spq"), (kf, kparts, "f_kf", "f_spk"))):
                            pool.wait_ge(s[ready], a_ + 1)
                            if not (static and k == -2):
                                pool.wait_ge(s[written], 16 * a_)
                            o = 1 + 4 * n
                            link(round_(parts[:, 0, :], src), o + 1)
                            link(pool.tensor_tensor(res, src, parts[:, 0, :], ALU.subtract), o + 2)
                            link(round_(parts[:, 1, :], res), o + 3)
                            link(pool.tensor_tensor(res, res, parts[:, 1, :], ALU.subtract), o + 4)
                            round_(parts[:, 2, :], res).then_inc(s["f_split"], 1)
                attention(pool, stage)

            @block.vector
            def _(dve):
                misc = bank[7]

                def batch(t, b):
                    if isinstance(b, int):
                        return t[:, TPB * b:TPB * b + TPB, :]
                    return t[:, bass.ds(b * TPB, TPB), :]

                def gb(b):
                    if isinstance(b, int):
                        return modR[:, b, 2, :]
                    return modR[:, bass.ds(b, 1), 2, :].rearrange("p o d -> p (o d)")

                def stage(k, r, do_a, do_m, do_b):
                    a_, m_, b_ = k + 2, k + 1, k
                    static = isinstance(k, int)
                    h2 = h2buf[(r + 2) % 3]

                    def maxima(n0, n1):
                        for n in range(n0, n1):
                            dve.wait_ge(s["f_s1"], 32 * m_ + n + 1)
                            dve.tensor_reduce(mx[:, n:n + 1], bank[n % 2][:], AX, ALU.max).then_inc(s["f_max"], 1)

                    def statistics(src, st, mv, name, tag, between):
                        for t in range(TPB):
                            i = dve.bn_stats(st[:, t, :], src(t))
                        i.then_inc(s[tag], 1)
                        dve.wait_ge(s[tag], a_ + 1)
                        between()
                        for t in range(TPB):
                            i = dve.bn_aggr(mv[:, t, :], st[:, t, :])
                        i.then_inc(s[name], 1)

                    def x1tile(t):
                        if static:
                            return x1[:, TPB * a_ + t, :]
                        return x1[:, bass.ds(a_ * TPB + t, 1), :].rearrange("p o d -> p (o d)")

                    def normed(dst, src, mean, rstd, done):
                        for t in range(TPB):
                            i = dve.tensor_scalar(dst[:, P * t:P * t + P], src(t), mean(t), rstd(t), ALU.subtract, ALU.mult)
                        i.then_inc(s[done], 1)

                    def column(x, t):
                        if static:
                            return x[:, TPB * a_ + t:TPB * a_ + t + 1]
                        return x[:, bass.ds(a_ * TPB + t, 1)]

                    def onorm_(g):
                        dve.wait_ge(s["f_oT"], 2 * b_ + g + 1)
                        o = misc[:].rearrange("p (t h d) -> p t h d", t=TPB, h=4)
                        dve.reciprocal(rc[:, g, :, :], o[:, :, :, FD]).then_inc(s["f_rc"], 1)
                        dve.wait_ge(s["f_rc"], 2 * b_ + g + 1)
                        dst = att.rearrange("p (t h d) -> p t h d", t=TPB, h=FH)[:, :, 4 * g:4 * g + 4, :]
                        for t in range(TPB):
                            i = dve.tensor_tensor(dst[:, t], o[:, t, :, 0:FD], bc(rc[:, g, t, :], 2, FD), ALU.mult)
                        i.then_inc(s["f_at"], 1)

                    def final():
                        dve.wait_ge(s["f_t1"], b_ + 1)
                        dve.wait_ge(s["f_op"], b_ + 1)
                        for t in range(TPB):
                            w = D >> t
                            i = dve.tensor_tensor(t1[:, P * t:P * t + w], t1[:, P * t:P * t + w], misc[:, P * t:P * t + w], ALU.add)
                        i.then_inc(s["f_rcy"], 1)
                        dve.wait_ge(s["f_rcy"], b_ + 1)
                        v = lambda t: t.rearrange("p (t d) -> p t d", d=D)
                        dve.tensor_tensor(v(outbuf[0]), v(t1), bc(gb(b_), 1, TPB), ALU.mult).then_inc(s["f_y"], 1)
                        dve.wait_ge(s["f_y"], b_ + 1)
                        dve.tensor_tensor(batch(x1, b_), v(outbuf[0]), batch(x1, b_), ALU.add).then_inc(s["f_out"], 1)

                    if do_a:
                        normed(xh2, x1tile, lambda t: column(mvx[:, :, 0], t), lambda t: column(rx, t), "f_xh")
                    for u in range(8):
                        if do_m:
                            maxima((7 * u) // 2 + (u == 1 and do_a), (7 * u + 7) // 2)
                        if do_a and u == 0:
                            dve.wait_ge(s["f_h2"], a_ + 1)
                            tile = lambda t: h2[:, P * t:P * t + P]
                            statistics(tile, st3, mv3, "f_v2", "f_st3", lambda: do_m and maxima(3, 4))
                            dve.wait_ge(s["f_r2"], a_ + 1)
                            normed(xn2, tile, lambda t: mv3[:, t, 0:1], lambda t: rr[:, 1, t:t + 1], "f_xn")
                        if do_a and u == 5:
                            dve.wait_ge(s["f_v"], a_ + 1)
                            dst = vaug[(r + 2) % 3][:, :, :, 0:FD]
                            dve.tensor_tensor(dst, misc[:].rearrange("p (t h d) -> p t h d", t=TPB, h=FH),
                                              bc(vbR.rearrange("p (h d) -> p h d", h=FH), 1, TPB), ALU.add).then_inc(s["f_V"], 1)
                        if do_b and u == 7:
                            onorm_(0)
                    if do_b:
                        onorm_(1)
                    if do_m:
                        maxima(28, 32)
                        dve.wait_ge(s["f_max"], 32 * m_ + 32)
                        if not (static and k == -1):
                            dve.wait_ge(s["f_mT"], m_)
                        dve.tensor_scalar(mm[:, 0:32], mx, -1.0, None, ALU.mult).then_inc(s["f_mh"], 1)
                        dve.wait_ge(s["f_mh"], m_ + 1)
                        dve.scalar_tensor_tensor(mm[:, 32:64], mx, -1.0, mm[:, 0:32], ALU.mult, ALU.subtract).then_inc(s["f_mm"], 1)
                    if do_b:
                        final()
                attention(dve, stage)


def gate_sign(dve, link, dst, g, tmp):
    link(dve.tensor_scalar(dst, g, 0.0, 2.0, ALU.is_ge, ALU.mult))
    link(dve.scalar_tensor_tensor(tmp, g, -1.0, g, ALU.mult, ALU.max))
    link(dve.tensor_scalar(tmp, tmp, 0.25, None, ALU.max))
    link(dve.scalar_tensor_tensor(dst, dst, -1.0, tmp, ALU.add, ALU.mult))


def dump(nc, sem, out, slab, which):
    s = sem("s_dump")
    with nc.Block() as block:
        @block.sync
        def _(sp):
            for i, k in enumerate(which):
                sp.dma_start(out[i], slab[:, k, :]).then_inc(s, 16)
            sp.wait_ge(s, 16 * len(which))


def arrange(inputs):
    f = {k[3:]: np.asarray(v) for k, v in inputs.items()}
    d = {}
    d["x"] = f["attn_hidden_states"].reshape(NT, P, D)
    d["cT"] = f["c"].T
    wm = f["wmod"].reshape(D, 6, D)
    d["wmod1"] = wm[:, 0:2]
    d["wqkvT"] = np.stack([f["attn_W" + k].T for k in "qkv"], axis=1)
    d["convw"] = np.concatenate([f[f"attn_{k}conv_w"].T for k in "qkv"], axis=0)
    d["wbrep"] = np.repeat(f["attn_Wb"].T, DH, axis=1)
    i32 = np.arange(C)
    part = np.arange(P) % C
    cst = np.zeros((P, C_END), np.float32)
    cst[:, C_IDENT:C_IDENT + P] = np.eye(P)
    cst[:, C_BONES:C_BONES + P] = np.kron(np.eye(H), np.ones((DH, DH)))
    cst[:, C_NEGA:C_NEGA + C] = -1.0 * (i32[None] > part[:, None])
    cst[:, C_CAUSAL:C_CAUSAL + C] = i32[None] >= part[:, None]
    cst[:, C_EYE:C_EYE + C] = i32[None] == part[:, None]
    d["consts"] = cst
    d["zeros"] = np.zeros((LONG - 1, D), np.float32)
    toep = np.zeros((WIN, D, C), np.float32)
    wl = f["attn_fir_long_w"].reshape(D, LONG)
    for i in range(C):
        toep[i:i + LONG, :, i] = wl.T
    d["toep"] = toep
    d["fsw"] = f["attn_fir_short_w"].reshape(D, SHORT)
    w1 = f["attn_gate_w1"]
    d["w1T"], d["w1sT"] = w1[:, :D].T, w1[:, D:].T
    d["w2T"] = f["attn_gate_w2"].T.reshape(2, P, 4 * H).transpose(1, 0, 2)
    d["b1"] = f["attn_gate_b1"].reshape(2, P).T
    d["temp_bias"] = np.stack([np.repeat(f["attn_log_temp"], 4), f["attn_base_bias"].reshape(-1)], axis=1)
    d["floor"] = f["attn_floor_raw"].reshape(-1)
    d["woT"] = f["attn_Wo"].T
    d["onorm"] = np.tile(f["attn_onorm_w"], H).reshape(D, 1)
    d["wga"] = wm[:, 2]
    d["w2"] = np.stack([f[f"ffn_{k}_w"].T for k in "qkvo"], axis=1)
    d["wmod2"] = wm[:, 3:6].reshape(D, 3 * D)
    d["cols"] = np.stack([f["ffn_norm_w"], f["ffn_norm_b"], f["ffn_q_b"], f["ffn_k_b"]], axis=1)
    d["v_b"] = f["ffn_v_b"]
    ob = np.zeros((TPB, D), np.float32)
    for t in range(TPB):
        ob[t, :D >> t] = f["ffn_o_b"][:D >> t]
    d["obR"] = ob.reshape(-1)
    return {k: np.ascontiguousarray(v) for k, v in d.items()}


def kernel(**inputs):
    import numpy as _np
    import concourse.bacc as _bacc
    from concourse import mybir as _mybir
    from concourse.bass_utils import run_bass_kernel_spmd as _run

    nc = _bacc.Bacc("TRN2", target_bir_lowering=False, num_devices=1)
    arrays = {"in_" + k: v for k, v in arrange(inputs).items()}
    a = {k: nc.dram_tensor(k, v.shape, _mybir.dt.from_np(v.dtype), kind="ExternalInput").ap() for k, v in arrays.items()}
    out = nc.dram_tensor("out", (NT, P, D), F32, kind="ExternalOutput").ap()
    build(nc, {k[3:]: v for k, v in a.items()}, out)
    r = _run(nc, [arrays], core_ids=[0])
    return r.results[0]["out"].reshape(B, T, D)
```

```python
from contextlib import ExitStack

import numpy as np
import concourse.bass as bass
from concourse import mybir

F32 = mybir.dt.float32
BF16 = mybir.dt.bfloat16
ALU = mybir.AluOpType
ACT = mybir.ActivationFunctionType
AX = mybir.AxisListType.X

P = 128
B, T, D = 8, 512, 128
NT = B * T // P
TPB = T // P
H, DH = 4, 32
C = 32
NCH = B * T // C
CPB = T // C
TAPS = 4
SHORT, LONG = 3, 63
WIN = C + LONG - 1
FH, FD = 8, 16
LN_EPS = 1e-5
HID = 256
ROW = 4096

C_IDENT, C_BONES, C_NEGA, C_CAUSAL, C_EYE, C_QUARTER, C_END = 0, 128, 256, 288, 320, 352, 356


class Chain:

    def __init__(self, engine, sem):
        self.engine, self.sem, self.n = engine, sem, 0

    def link(self, ins):
        self.n += 1
        ins.then_inc(self.sem, 1)
        self.engine.wait_ge(self.sem, self.n)


def bc(ap, axis, n):
    ap = ap.unsqueeze(axis)
    shape = list(ap.shape)
    shape[axis] = n
    return ap.broadcast_to(shape)


def build(nc, a, out, stop=99):
    with ExitStack() as ctx:
        def sb(name, shape, dt=F32):
            return ctx.enter_context(nc.sbuf_tensor(name, shape, dt))

        def sem(name):
            return ctx.enter_context(nc.semaphore(name))

        psum = ctx.enter_context(nc.psum_tensor("psum", [P, 8, 512], F32))
        bank = [psum[:, i, :] for i in range(8)]
        wide = [psum[:, 2:4, :], psum[:, 4:6, :]]
        slab = sb("slab", [P, 11, ROW])
        hT = sb("hT", [P, B, T])
        cst = sb("cst", [P, C_END])
        ident = cst[:, C_IDENT:C_IDENT + P]
        bones = cst[:, C_BONES:C_BONES + P]
        neg_strict = cst[:, C_NEGA:C_NEGA + C]
        causal = cst[:, C_CAUSAL:C_CAUSAL + C]
        eye32 = cst[:, C_EYE:C_EYE + C]
        quarter = cst[:, C_QUARTER:C_QUARTER + 4]
        cT = sb("cT", [P, B])
        modF = sb("modF", [P, 2, B])
        scratch = sb("scratch", [P, 2048])
        eps = sb("eps", [P, 3])
        eps_ln, eps_l2, one1 = eps[:, 0:1], eps[:, 1:2], eps[:, 2:3]
        chain_act, chain_dve, chain_pool = sem("chain_act"), sem("chain_dve"), sem("chain_pool")
        order = {}

        def chain(engine, s):
            if s not in order:
                order[s] = [0]
            count = order[s]

            def link(ins):
                count[0] += 1
                ins.then_inc(s, 1)
                engine.wait_ge(s, count[0])
            return link

        v_dram = nc.dram_tensor("v_padded", (B, LONG - 1 + T, D), F32, kind="Internal")
        a_dram = nc.dram_tensor("a_scratch", (NT, P, P), F32, kind="Internal").ap()
        t_dram = nc.dram_tensor("t_scratch", (NT, P, P), F32, kind="Internal").ap()
        h_dram = nc.dram_tensor("h_kept", (P, B, T), F32, kind="Internal").ap()

        xN = slab[:, 0, :].rearrange("p (t d) -> p t d", d=D)
        wmodF = slab[:, 1, 0:2 * D].rearrange("p (k d) -> p k d", k=2)
        wT = slab[:, 7, 0:3 * D].rearrange("p (k d) -> p k d", k=3)
        wbrep = slab[:, 7, 384:384 + D]
        taps = slab[:, 7, 512:512 + 3 * TAPS]
        stats = slab[:, 10, 0:6 * NT].rearrange("p (t s) -> p t s", s=6)
        meanvar = slab[:, 10, 256:256 + 2 * NT].rearrange("p (t s) -> p t s", s=2)
        rstd = slab[:, 10, 384:384 + NT]
        lnv = slab[:, 10, 448:448 + NT]
        xh = xN
        s_x = [sem(f"s_x{g}") for g in range(4)]
        s_w, s_c, s_eps = sem("s_w"), sem("s_c"), sem("s_eps")
        s_silu, s_mod, s_modc, s_stats, s_rstd, s_xh = (
            sem(x) for x in ("s_silu", "s_mod", "s_modc", "s_stats", "s_rstd", "s_xh"))
        with nc.Block() as block:
            @block.sync
            def _(sp):
                for g in range(4):
                    sp.dma_start(xN[:, 8 * g:8 * g + 8, :],
                                 a["x"][8 * g:8 * g + 8].rearrange("t p d -> p t d")).then_inc(s_x[g], 16)

            @block.gpsimd
            def _(pool):
                pool.memset(eps[:, 0:1], LN_EPS).then_inc(s_eps, 1)
                pool.memset(eps[:, 1:2], 1e-6).then_inc(s_eps, 1)
                pool.memset(eps[:, 2:3], 1.0).then_inc(s_eps, 1)

            @block.scalar
            def _(act):
                act.dma_start(cT[:], a["cT"]).then_inc(s_c, 16)
                act.dma_start(wmodF, a["wmod1"]).then_inc(s_c, 16)
                act.dma_start(cst[:], a["consts"]).then_inc(s_w, 16)
                act.dma_start(wT, a["wqkvT"]).then_inc(s_w, 16)
                act.dma_start(taps, a["taps"]).then_inc(s_w, 16)
                act.dma_start(wbrep, a["wbrep"]).then_inc(s_w, 16)
                act.wait_ge(s_c, 32)
                act.activation(cT[:], cT[:], ACT.Silu).then_inc(s_silu, 1)
                act.wait_ge(s_eps, 3)
                act.preload_act_table_set("natural_log_exp_and_others")
                for g in range(4):
                    act.wait_ge(s_stats, g + 1)
                    link = chain(act, chain_act)
                    link(act.activation(lnv[:, 8 * g:8 * g + 8], meanvar[:, 8 * g:8 * g + 8, 1], ACT.Ln, bias=eps_ln))
                    act.activation(rstd[:, 8 * g:8 * g + 8], lnv[:, 8 * g:8 * g + 8], ACT.Exp, scale=-0.5).then_inc(s_rstd, 1)

            @block.tensor
            def _(pe):
                pe.wait_ge(s_silu, 1)
                for k in range(2):
                    m = pe.matmul(bank[0][:, k * B:(k + 1) * B], wmodF[:, k, :], cT[:], start=True, stop=True)
                m.then_inc(s_mod, 1)

            @block.vector
            def _(dve):
                link = chain(dve, chain_dve)
                for g in range(4):
                    dve.wait_ge(s_x[g], 16)
                    for t in range(8 * g, 8 * g + 8):
                        i = dve.bn_stats(stats[:, t, :], xN[:, t, :])
                    link(i)
                    for t in range(8 * g, 8 * g + 8):
                        i = dve.bn_aggr(meanvar[:, t, :], stats[:, t, :])
                    i.then_inc(s_stats, 1)
                dve.wait_ge(s_mod, 1)
                dve.tensor_copy(modF[:, 0, :], bank[0][:, 0:B]).then_inc(s_modc, 1)
                dve.tensor_scalar(modF[:, 1, :], bank[0][:, B:2 * B], 1.0, None, ALU.add).then_inc(s_modc, 1)
                dve.wait_ge(s_w, 64)
                for g in range(4):
                    dve.wait_ge(s_rstd, g + 1)
                    for t in range(8 * g, 8 * g + 8):
                        i = dve.tensor_scalar(xh[:, t, :], xN[:, t, :], meanvar[:, t, 0:1], rstd[:, t:t + 1],
                                              ALU.subtract, ALU.mult)
                    i.then_inc(s_xh, 1)

        qs, ks, vT, bt = (slab[:, s, :] for s in (1, 2, 3, 4))
        sqq, sqk = slab[:, 6, :], slab[:, 5, :]
        vb = slab[:, 9, :]
        vnat = slab[:, 10, :].rearrange("p (n t d) -> p n t d", n=B, t=TPB)
        s_pe, s_evac, s_tap, s_conv, s_act2, s_bt, s_pool2, s_vnat, s_vout = (
            sem(x) for x in ("s_pe", "s_evac", "s_tap", "s_conv", "s_act2", "s_bt", "s_pool2", "s_vnat", "s_vout"))
        outputs = [("t", 0)]
        for b in range(B):
            if b + 1 < B:
                outputs.append(("t", b + 1))
            outputs += [("q", b), ("k", b), ("v", b), ("beta", b)]
            if b >= 2:
                outputs.append(("vt", b - 2))
        outputs += [("vt", B - 2), ("vt", B - 1)]

        def evacuations(n):
            group = ("q", "k", "v") if outputs[n][0] in ("q", "k", "v") else ("t", "beta", "vt")
            return s_conv if "q" in group else s_evac, sum(kind in group for kind, _ in outputs[:n + 1])

        with nc.Block() as block:
            @block.tensor
            def _(pe):
                for n, (kind, b) in enumerate(outputs):
                    if n >= 8:
                        pe.wait_ge(*evacuations(n - 8))
                    o = bank[n % 8]
                    if kind == "t":
                        for t in range(TPB):
                            m = pe.transpose(o[:, P * t:P * t + P], xh[:, TPB * b + t, :], ident)
                    elif kind == "vt":
                        pe.wait_ge(s_act2, 3 * b + 3)
                        for t in range(TPB):
                            m = pe.transpose(o[:, P * t:P * t + P], vT[:, T * b + P * t:T * b + P * t + P], ident)
                    elif kind == "beta":
                        m = pe.matmul(o[:], wbrep, hT[:, b, :], start=True, stop=True)
                    else:
                        if kind == "q":
                            pe.wait_ge(*evacuations(outputs.index(("t", b))))
                        m = pe.matmul(o[:], wT[:, "qkv".index(kind), :], hT[:, b, :], start=True, stop=True)
                    m.then_inc(s_pe, 1)

            @block.scalar
            def _(act):
                def silus(b):
                    act.wait_ge(s_conv, 3 * b + 3)
                    cols = slice(T * b, T * b + T)
                    for y in (qs, ks, vT):
                        act.activation(y[:, cols], y[:, cols], ACT.Silu).then_inc(s_act2, 1)

                for n, (kind, b) in enumerate(outputs):
                    act.wait_ge(s_pe, n + 1)
                    o, cols = bank[n % 8][:], slice(T * b, T * b + T)
                    if kind == "t":
                        act.activation(hT[:, b, :], o, ACT.Identity,
                                       bias=modF[:, 0, b:b + 1], scale=modF[:, 1, b:b + 1]).then_inc(s_evac, 1)
                    elif kind == "vt":
                        act.activation(vnat[:, b, :, :], o.rearrange("p (t d) -> p t d", d=D), ACT.Copy).then_inc(s_evac, 1)
                    elif kind == "beta":
                        act.activation(bt[:, cols], o, ACT.Tanh, scale=0.5).then_inc(s_evac, 1)
                        if b:
                            silus(b - 1)
                        if b == B - 1:
                            silus(b)
                    else:
                        k = "qkv".index(kind)
                        act.activation((qs, ks, vT)[k][:, cols], o, ACT.Identity,
                                       scale=taps[:, TAPS * k + TAPS - 1:TAPS * k + TAPS]).then_inc(s_tap, 1)

            @block.vector
            def _(dve):
                link = chain(dve, chain_dve)
                for b in range(B):
                    dve.wait_ge(s_tap, 3 * b + 3)
                    for d in range(1, TAPS):
                        for k, y in enumerate((qs, ks, vT)):
                            o = bank[outputs.index(("qkv"[k], b)) % 8]
                            j = TAPS * k + TAPS - 1 - d
                            y_ = y[:, T * b + d:T * b + T]
                            i = dve.scalar_tensor_tensor(y_, o[:, 0:T - d], taps[:, j:j + 1], y_, ALU.mult, ALU.add)
                            if d == TAPS - 1:
                                i.then_inc(s_conv, 1)
                        if d < TAPS - 1:
                            link(i)
                    dve.wait_ge(*evacuations(outputs.index(("beta", b))))
                    cols = slice(T * b, T * b + T)
                    dve.tensor_scalar(bt[:, cols], bt[:, cols], 0.5, 0.5, ALU.mult, ALU.add).then_inc(s_bt, 1)

            @block.gpsimd
            def _(pool):
                for b in range(B):
                    cols = slice(T * b, T * b + T)
                    pool.wait_ge(s_act2, 3 * b + 3)
                    pool.tensor_tensor(sqk[:, cols], ks[:, cols], ks[:, cols], ALU.mult)
                    pool.tensor_tensor(sqq[:, cols], qs[:, cols], qs[:, cols], ALU.mult)
                    pool.wait_ge(s_bt, b + 1)
                    pool.tensor_tensor(vb[:, cols], vT[:, cols], bt[:, cols], ALU.mult).then_inc(s_pool2, 1)

            @block.sync
            def _(sp):
                for b in range(B):
                    sp.dma_start(v_dram.ap()[b, 0:LONG - 1, :], a["zeros"]).then_inc(s_vout, 16)
                for b in range(B):
                    sp.wait_ge(*evacuations(outputs.index(("vt", b))))
                    sp.dma_start(v_dram.ap()[b, LONG - 1:, :].rearrange("(t p) d -> p t d", p=P), vnat[:, b, :, :]).then_inc(s_vout, 16)
                sp.wait_ge(s_vout, 32 * B)
        if stop == 2:
            return dump(nc, sem, out, slab, [1, 2, 3, 4])

        kbq = slab[:, 5:7, :].rearrange("p k (c i) -> p k c i", i=C)
        vk = slab[:, 0:2, :].rearrange("p s (t h k d) -> p (s t) h k d", h=H, k=2, d=DH)
        ak = slab[:, 7:9, :].rearrange("p s (t h k d) -> p (s t) h k d", h=H, k=2, d=DH)
        kn = ks
        a_nat = slab[:, 0, :].rearrange("p (t h i) -> p t h i", h=H, i=C)
        X = slab[:, 10, :]
        s_ss, s_ln, s_rs, s_qn, s_knorm, s_kb, s_g, s_ga, s_adma, s_xdma = (
            sem(x) for x in ("s_ss", "s_ln", "s_rs", "s_qn", "s_knorm", "s_kb", "s_g", "s_ga", "s_adma", "s_xdma"))
        TG = 8
        s_hout, s_hin = sem("s_hout"), sem("s_hin")
        with nc.Block() as block:
            @block.tensor
            def _(pe):
                def products(g):
                    pe.wait_ge(s_kb, 2 * g + 2)
                    pe.wait_ge(s_qn, 2 * g + 2)
                    for h in range(H):
                        if g:
                            pe.wait_ge(s_ga, H * (g - 1) + h + 1)
                        o = bank[4 + h][:].rearrange("p (t k i) -> p t k i", k=2, i=C)
                        for t in range(TG):
                            for c in range(4):
                                chunk = 4 * (TG * g + t) + c
                                m = pe.matmul(o[C * c:C * c + C, t, :, :],
                                              kn[DH * h:DH * h + DH, C * chunk:C * chunk + C],
                                              kbq[DH * h:DH * h + DH, :, chunk, :], start=True, stop=True)
                        m.then_inc(s_g, 1)

                for n in range(2 * B):
                    b, src = n // 2, (sqk, sqq)[n % 2]
                    if n >= 4:
                        pe.wait_ge(s_ln, n - 3)
                    pe.matmul(bank[n % 4][:], bones, src[:, T * b:T * b + T], start=True, stop=True).then_inc(s_ss, 1)
                    if n >= 8 and n % 4 == 3:
                        products((n - 8) // 4)
                products(2)
                products(3)

            @block.scalar
            def _(act):
                act.preload_act_table_set("natural_log_exp_and_others")

                def exponent(n):
                    b, f = n // 2, (sqk, sqq)[n % 2]
                    act.wait_ge(s_ln, n + 1)
                    act.activation(f[:, T * b:T * b + T], f[:, T * b:T * b + T], ACT.Exp, scale=-0.5).then_inc(s_rs, 1)

                for n in range(2 * B):
                    b, f = n // 2, (sqk, sqq)[n % 2]
                    act.wait_ge(s_ss, n + 1)
                    act.activation(f[:, T * b:T * b + T], bank[n % 4][:], ACT.Ln, bias=eps_l2).then_inc(s_ln, 1)
                    if n:
                        exponent(n - 1)
                exponent(2 * B - 1)

            @block.gpsimd
            def _(pool):
                for b in range(B):
                    cols = slice(T * b, T * b + T)
                    pool.wait_ge(s_rs, 2 * b + 2)
                    pool.tensor_tensor(sqq[:, cols], qs[:, cols], sqq[:, cols], ALU.mult).then_inc(s_qn, 1)

            @block.vector
            def _(dve):
                def masked(g):
                    tiles = slice(TG * g, TG * g + TG)
                    for h in range(H):
                        dve.wait_ge(s_g, H * g + h + 1)
                        o = bank[4 + h][:].rearrange("p (t k i) -> p t k i", k=2, i=C)
                        dve.tensor_tensor(a_nat[:, tiles, h, :], o[:, :, 0, :], bc(neg_strict, 1, TG), ALU.mult)
                        dve.tensor_tensor(ak[:, tiles, h, 0, :], o[:, :, 1, :], bc(causal, 1, TG), ALU.mult).then_inc(s_ga, 1)

                for b in range(B):
                    cols = slice(T * b, T * b + T)
                    dve.wait_ge(s_rs, 2 * b + 1)
                    dve.tensor_tensor(kn[:, cols], ks[:, cols], sqk[:, cols], ALU.mult).then_inc(s_knorm, 1)
                    dve.wait_ge(s_knorm, b + 1)
                    dve.tensor_tensor(sqk[:, cols], kn[:, cols], bt[:, cols], ALU.mult).then_inc(s_kb, 1)
                    if b == 6:
                        masked(0)
                for g in range(1, NT // TG):
                    masked(g)

            @block.sync
            def _(sp):
                sp.dma_start(h_dram, hT[:]).then_inc(s_hout, 16)
                for g in range(NT // TG):
                    sp.wait_ge(s_ga, H * (g + 1))
                    sp.dma_start(a_dram[TG * g:TG * g + TG].rearrange("t p x -> p t x"),
                                 slab[:, 0, TG * P * g:TG * P * g + TG * P].rearrange("p (t x) -> p t x", x=P)).then_inc(s_adma, 16)
                    sp.wait_ge(s_adma, 16 * (g + 1))
                    sp.dma_start(X[4 * TG * g:4 * TG * (g + 1), :],
                                 a_dram[TG * g:TG * g + TG].rearrange("t (c j) x -> (t c) (j x)", c=4)).then_inc(s_xdma, 16)
                sp.wait_ge(s_xdma, 16 * (NT // TG))
                sp.wait_ge(s_hout, 16)

        X4 = X.rearrange("p (j h i) -> p j h i", h=H, i=C)
        s_xd, s_xp, s_tdma, s_ttdma = sem("s_xd"), sem("s_xp"), sem("s_tdma"), sem("s_ttdma")
        HD = 3
        MAXW = max(m * (C - 1 - m) for m in range(C))
        toep = slab[0:WIN, 4, :].rearrange("p (d i) -> p d i", i=C)
        fo = slab[:, 2, :].rearrange("p (g c) -> p g c", c=NCH)
        win = [slab[0:WIN, 9, 2048 * k:2048 * k + 2048].rearrange("p (c d) -> p c d", d=2 * DH) for k in range(2)]
        WC = 2 * CPB
        FIR = 2 * (B // 2)
        s_toep, s_fpe, s_fev, s_wused, s_xpose, s_xevac = (
            sem(x) for x in ("s_toep", "s_fpe", "s_fev", "s_wused", "s_xpose", "s_xevac"))
        s_win = [sem(f"s_win{i}") for i in range(2)]
        copies = [(src, b) for src in ("vb", "kn", "kb") for b in range(B)]

        def invert(engine, s, h0, h1):
            link = chain(engine, s)
            nh = h1 - h0
            tmp = scratch[:, MAXW * h0:MAXW * h1]
            for m in range(1, C - 1):
                w = C - 1 - m
                prod = tmp[:, 0:m * nh * w].rearrange("p (k h i) -> p k h i", h=nh, i=w)
                link(engine.tensor_tensor(prod, bc(X4[:, m, h0:h1, m + 1:], 1, m),
                                          X4[:, 0:m, h0:h1, m:m + 1].broadcast_to([P, m, nh, w]), ALU.mult))
                link(engine.tensor_tensor(X4[:, 0:m, h0:h1, m + 1:], X4[:, 0:m, h0:h1, m + 1:], prod, ALU.add))
            for h in range(h0, h1):
                i = engine.memset(X[:, C * h:C * h + (P + 1) * (C - 1) + 1:P + 1], 1.0)
            return i

        with nc.Block() as block:
            @block.vector
            def _(dve):
                invert(dve, chain_dve, 0, HD).then_inc(s_xd, 1)

            @block.gpsimd
            def _(pool):
                invert(pool, chain_pool, HD, H).then_inc(s_xp, 1)

            @block.tensor
            def _(pe):
                for n, (src, b) in enumerate(copies):
                    if n >= 2:
                        pe.wait_ge(s_xevac, n - 1)
                    rows = {"vb": vb, "kn": kn, "kb": sqk}[src]
                    for t in range(TPB):
                        m = pe.transpose(bank[6 + n % 2][:, P * t:P * t + P], rows[:, T * b + P * t:T * b + P * t + P], ident)
                    m.then_inc(s_xpose, 1)
                pe.wait_ge(s_toep, 16)
                for p in range(B // 2):
                    if p >= 2:
                        pe.wait_ge(s_fev, 2 * (p - 1))
                    for hp in range(2):
                        n = 2 * p + hp
                        pe.wait_ge(s_win[hp], 32 * (p + 1))
                        for j in range(DH):
                            o = bank[2 * (p % 2) + j // 16]
                            cols = slice(WC * (j % 16), WC * (j % 16) + WC)
                            for h in (2 * hp, 2 * hp + 1):
                                m = pe.matmul(o[DH * h:DH * h + DH, cols], toep[:, DH * h + j, :],
                                              win[hp][:, :, DH * (h % 2) + j], start=True, stop=True)
                        m.then_inc(s_fpe, 1)

            @block.scalar
            def _(act):
                for n, (src, b) in enumerate(copies):
                    act.wait_ge(s_xpose, n + 1)
                    tiles = slice(TPB * b, TPB * b + TPB)
                    dst = {"vb": vk[:, tiles, :, 0, :], "kn": ak[:, tiles, :, 1, :], "kb": vk[:, tiles, :, 1, :]}[src]
                    act.activation(dst, bank[6 + n % 2][:].rearrange("p (t h d) -> p t h d", h=H, d=DH), ACT.Copy).then_inc(s_xevac, 1)
                for p in range(B // 2):
                    act.wait_ge(s_fpe, 2 * p + 2)
                    for k in range(2):
                        act.activation(fo[:, 16 * k:16 * k + 16, WC * p:WC * p + WC],
                                       bank[2 * (p % 2) + k][:].rearrange("p (g c) -> p g c", c=WC), ACT.Copy).then_inc(s_fev, 1)

            @block.sync
            def _(sp):
                sp.dma_start(toep, a["toep"]).then_inc(s_toep, 16)
                sp.wait_ge(s_xpose, B)
                for n in range(FIR):
                    p, hp = n // 2, n % 2
                    if n >= 2:
                        sp.wait_ge(s_fpe, n - 1)
                    for b in (2 * p, 2 * p + 1):
                        src = bass.AP(v_dram, b * (LONG - 1 + T) * D + 2 * DH * hp, [[D, WIN], [C * D, CPB], [1, 2 * DH]])
                        c0 = CPB * (b % 2)
                        sp.dma_start(win[hp][:, c0:c0 + CPB, :], src).then_inc(s_win[hp], 16)
                sp.wait_ge(s_xd, 1)
                sp.wait_ge(s_xp, 1)
                sp.dma_start(t_dram.rearrange("t (c j) x -> (t c) (j x)", c=4), X).then_inc(s_tdma, 16)
                sp.wait_ge(s_fpe, FIR)
                sp.wait_ge(s_tdma, 16)
                sp.dma_start(slab[:, 9, :].rearrange("p (t x) -> p t x", x=P), t_dram.rearrange("t p x -> p t x")).then_inc(s_ttdma, 16)
                sp.wait_ge(s_ttdma, 16)
        if stop == 5:
            return dump(nc, sem, out, slab, [7, 8, 9, 10])

        tt = slab[:, 9, :].rearrange("p (t h i) -> p t h i", h=H, i=C)
        uw = vk
        au = slab[:, 4, :].rearrange("p (c i) -> p c i", i=C)
        N = slab[:, 10, :].rearrange("p (c d) -> p c d", d=DH)
        NG = NT // 2
        ak_spread = [hT[:].rearrange("p b t -> p (b t)")[:, 2048 * k:2048 * k + 2048].rearrange(
            "p (n c x) -> p n c x", c=4, x=C) for k in range(2)]
        u_spread = [scratch[:, 1024 * k:1024 * k + 1024].rearrange("p (n c x) -> p n c x", c=4, x=DH) for k in range(2)]
        s_u, s_uw, s_us, s_akd, s_akp, s_pb, s_ed, s_ea = (
            sem(x) for x in ("s_u", "s_uw", "s_us", "s_akd", "s_akp", "s_pb", "s_ed", "s_ea"))

        def spread(engine, dst, src, n):
            return engine.tensor_tensor(dst, bc(src, 2, 4), bc(bc(quarter, 1, n), 3, C), ALU.mult)

        def spread_ak(engine, g):
            src = ak[:, 2 * g:2 * g + 2, :, :, :].rearrange("p t h k d -> p (t h k) d")
            return spread(engine, ak_spread[g % 2], src, 4 * H)

        with nc.Block() as block:
            @block.tensor
            def _(pe):
                def solve(g):
                    if g >= 2:
                        pe.wait_ge(s_uw, g - 1)
                    for t in range(2 * g, 2 * g + 2):
                        for h in range(H):
                            for c in range(4):
                                q = slice(C * c, C * c + C)
                                col = 2 * DH * (H * (t % 2) + h)
                                m = pe.matmul(bank[g % 2][q, col:col + 2 * DH], tt[q, t, h, :], vk[q, t, h, :, :],
                                              start=True, stop=True)
                    m.then_inc(s_u, 1)

                solve(0)
                for g in range(NG):
                    if g + 1 < NG:
                        solve(g + 1)
                    quad = g // 2
                    pe.wait_ge(s_uw, g + 1)
                    pe.wait_ge(s_us, g + 1)
                    pe.wait_ge(s_akd if g % 2 == 0 else s_akp, g // 2 + 1)
                    if g >= 2:
                        pe.wait_ge(s_ed, g - 1)
                    if quad >= 2:
                        pe.wait_ge(s_ea, quad - 1)
                    for i in range(2):
                        tile = 2 * g + i
                        for h in range(H):
                            q = slice(DH * h, DH * h + DH)
                            n = 2 * (H * i + h)
                            cols = slice(P * (tile % 4), P * (tile % 4) + P)
                            pe.matmul(bank[2 + g % 2][q, 2 * P * i:2 * P * i + 2 * P], uw[:, tile, h, 1, :],
                                      ak_spread[g % 2][:, n:n + 2, :, :], start=True, stop=True)
                            pe.matmul(bank[4 + quad % 2][q, cols], uw[:, tile, h, 0, :], ak_spread[g % 2][:, n, :, :],
                                      start=True, stop=True)
                            m = pe.matmul(bank[6 + quad % 2][q, cols], ak[:, tile, h, 1, :], u_spread[g % 2][:, H * i + h, :, :],
                                          start=True, stop=True)
                    m.then_inc(s_pb, 1)

            @block.scalar
            def _(act):
                def gathered(quad):
                    act.wait_ge(s_pb, 2 * quad + 2)
                    chunks = slice(16 * quad, 16 * quad + 16)
                    act.activation(au[:, chunks, :], bank[4 + quad % 2][:].rearrange("p (c i) -> p c i", i=C), ACT.Copy)
                    act.activation(N[:, chunks, :], bank[6 + quad % 2][:].rearrange("p (c i) -> p c i", i=C), ACT.Copy).then_inc(s_ea, 1)

                for g in range(NG):
                    act.wait_ge(s_u, g + 1)
                    act.activation(uw[:, 2 * g:2 * g + 2].rearrange("p t h k d -> p (t h k d)"), bank[g % 2][:], ACT.Copy).then_inc(s_uw, 1)
                    if g >= 3 and g % 2:
                        gathered((g - 3) // 2)
                gathered(NG // 2 - 1)

            @block.gpsimd
            def _(pool):
                for g in range(1, NG, 2):
                    if g >= 2:
                        pool.wait_ge(s_pb, g - 1)
                    spread_ak(pool, g).then_inc(s_akp, 1)

            @block.vector
            def _(dve):
                def subtract(g):
                    dve.wait_ge(s_pb, g + 1)
                    o = bank[2 + g % 2][:].rearrange("p (t k c i) -> p t k c i", t=2, k=2, i=C)
                    for i in range(2):
                        chunks = slice(4 * (2 * g + i), 4 * (2 * g + i) + 4)
                        dve.tensor_tensor(kbq[:, 1, chunks, :], kbq[:, 1, chunks, :], o[:, i, 0, :, :], ALU.subtract)
                        m = dve.tensor_tensor(kbq[:, 0, chunks, :], bc(eye32, 1, 4), o[:, i, 1, :, :], ALU.subtract)
                    m.then_inc(s_ed, 1)

                spread_ak(dve, 0).then_inc(s_akd, 1)
                for g in range(NG):
                    dve.wait_ge(s_uw, g + 1)
                    if g >= 2:
                        dve.wait_ge(s_pb, g - 1)
                    spread(dve, u_spread[g % 2], uw[:, 2 * g:2 * g + 2, :, 0, :].rearrange("p t h d -> p (t h) d"), 2 * H).then_inc(s_us, 1)
                    if g >= 1:
                        subtract(g - 1)
                        if g % 2 and g + 1 < NG:
                            spread_ak(dve, g + 1).then_inc(s_akd, 1)
                subtract(NG - 1)

        Nb = N.rearrange("p (b c) d -> p b c d", c=CPB)
        s_r, s_s, s_o, s_oe = sem("s_r"), sem("s_s"), sem("s_o"), sem("s_oe")
        with nc.Block() as block:
            @block.tensor
            def _(pe):
                for c in range(1, CPB - 1):
                    for half in range(2):
                        if c > 1:
                            pe.wait_ge(s_s, 2 * (c - 2) + half + 1)
                        for b in range(4 * half, 4 * half + 4):
                            for h in range(H):
                                q = slice(DH * h, DH * h + DH)
                                m = pe.matmul(bank[half][q, DH * (b % 4):DH * (b % 4) + DH], kbq[q, 0, CPB * b + c, :],
                                              Nb[q, b, c - 1, :], start=True, stop=True)
                        m.then_inc(s_r, 1)
                pe.wait_ge(s_s, 2 * (CPB - 2))
                for b in range(B):
                    if b >= 4:
                        pe.wait_ge(s_oe, b - 3)
                    for c in range(1, CPB):
                        for h in range(H):
                            q = slice(DH * h, DH * h + DH)
                            m = pe.matmul(bank[2 + b % 4][q, C * c:C * c + C], Nb[q, b, c - 1, :], kbq[q, 1, CPB * b + c, :],
                                          start=True, stop=True)
                    m.then_inc(s_o, 1)

            @block.vector
            def _(dve):
                for c in range(1, CPB - 1):
                    for half in range(2):
                        dve.wait_ge(s_r, 2 * (c - 1) + half + 1)
                        bs = slice(4 * half, 4 * half + 4)
                        dve.tensor_tensor(Nb[:, bs, c, :], Nb[:, bs, c, :],
                                          bank[half][:, 0:4 * DH].rearrange("p (b d) -> p b d", d=DH), ALU.add).then_inc(s_s, 1)
                for b in range(B):
                    dve.wait_ge(s_o, b + 1)
                    cols = slice(T * b + C, T * b + T)
                    dve.tensor_tensor(slab[:, 4, cols], slab[:, 4, cols], bank[2 + b % 4][:, C:], ALU.add).then_inc(s_oe, 1)
        if stop == 7:
            return dump(nc, sem, out, slab, [4, 2, 5, 6])

        fsw = sb("fsw", [P, SHORT])
        short_f, short_c, long_c, delta_c, v_c = (slab[:, s, :] for s in (10, 3, 1, 9, 4))
        s_fw, s_sf, s_cp, s_ca, s_cd, s_vc = (sem(x) for x in ("s_fw", "s_sf", "s_cp", "s_ca", "s_cd", "s_vc"))
        with nc.Block() as block:
            jobs = [(k, g) for k in ("delta", "long", "short") for g in range(8)]

            def evacuated(engine, n):
                engine.wait_ge(s_ca if n % 2 == 0 else s_cd, n // 2 + 1)

            @block.sync
            def _(sp):
                sp.dma_start(hT[:], h_dram).then_inc(s_hin, 16)
                for n in (6, 7):
                    evacuated(sp, n)
                for b in range(B):
                    sp.dma_start(v_c[CPB * b:CPB * b + CPB, :],
                                 v_dram.ap()[b, LONG - 1:, :].rearrange("(c j) d -> c (j d)", j=C)).then_inc(s_vc, 16)
                sp.wait_ge(s_vc, 16 * B)
                sp.wait_ge(s_hin, 16)

            @block.gpsimd
            def _(pool):
                pool.dma_start(fsw[:], a["fsw"]).then_inc(s_fw, 16)

            @block.tensor
            def _(pe):
                for n, (kind, g) in enumerate(jobs):
                    o = bank[n % 8]
                    if n >= 8:
                        evacuated(pe, n - 8)
                    if kind == "short" and g == 0:
                        pe.wait_ge(s_sf, 1)
                    for i in range(4):
                        j = 4 * g + i
                        cols = slice(P * i, P * i + P)
                        if kind == "long":
                            m = pe.transpose(o[:, cols], fo[:, j, :], ident)
                        else:
                            src = slab[:, 4, :] if kind == "delta" else short_f
                            m = pe.transpose(o[:, cols], src[:, j:C * (NCH - 1) + j + 1:C], ident)
                    m.then_inc(s_cp, 1)

            def evacuate(engine, copy, parity, s, jobs_of_call):
                for n, (kind, g) in enumerate(jobs):
                    if n % 2 != parity or n not in jobs_of_call:
                        continue
                    engine.wait_ge(s_cp, n + 1)
                    o = bank[n % 8][:]
                    if kind == "long":
                        dst = long_c.rearrange("p (i h d) -> p h i d", h=H, d=DH)[:, :, :, 4 * g:4 * g + 4]
                        for h in range(H):
                            i = copy(dst[:, h, :, :], o.rearrange("p (d h i) -> p h i d", h=H, i=C)[:, h, :, :])
                        i.then_inc(s, 1)
                    else:
                        dst = {"delta": delta_c, "short": short_c}[kind][:, 512 * g:512 * g + 512]
                        copy(dst, o).then_inc(s, 1)

            @block.scalar
            def _(act):
                evacuate(act, lambda d, s: act.activation(d, s, ACT.Copy), 0, s_ca, range(len(jobs)))

            @block.vector
            def _(dve):
                evacuate(dve, dve.tensor_copy, 1, s_cd, range(0, 8))
                link = chain(dve, chain_dve)
                r, v = (x.rearrange("p (b t) -> p b t", t=T) for x in (short_f, vT))
                dve.wait_ge(s_fw, 16)
                link(dve.tensor_scalar(r, v, fsw[:, 2:3], None, ALU.mult))
                link(dve.scalar_tensor_tensor(r[:, :, 1:], v[:, :, :T - 1], fsw[:, 1:2], r[:, :, 1:], ALU.mult, ALU.add))
                dve.scalar_tensor_tensor(r[:, :, 2:], v[:, :, :T - 2], fsw[:, 0:1], r[:, :, 2:], ALU.mult, ALU.add).then_inc(s_sf, 1)
                evacuate(dve, dve.tensor_copy, 1, s_cd, range(8, len(jobs)))
        if stop == 8:
            return dump(nc, sem, out, slab, [3, 1, 9, 4])

        paths = [short_c, long_c, delta_c, v_c]
        NP_ = len(paths)
        K16 = H * NP_
        st = slab[:, 10, 0:1024].rearrange("p (j w h k) -> p j w h k", w=NP_, h=H, k=2)
        sums = slab[:, 10, 1024:1536].rearrange("p (w n) -> p w n", w=NP_)
        sqs = slab[:, 10, 1536:2048].rearrange("p (w n) -> p w n", w=NP_)
        m2 = slab[:, 10, 2048:2560].rearrange("p (w n) -> p w n", w=NP_)
        stT = slab[0:C, 2, :]
        small = slab[:, 10, 2560:4096]
        w1T, w2T = small[:, 0:HID], small[:, 256:288].rearrange("p (m k) -> p m k", m=2)
        b1 = small[:, 288:290]
        w1sT = small[0:C, 290:290 + HID]
        tmp16 = small[0:K16, 546:554]
        fl = small[:, 554:570]
        flt = small[:, 570:586]
        s_sqr, s_red, s_gw, s_st, s_stp, s_sta, s_std, s_tmp, s_tv = (
            sem(x) for x in ("s_sqr", "s_red", "s_gw", "s_st", "s_stp", "s_sta", "s_std", "s_tmp", "s_tv"))
        with nc.Block() as block:
            @block.sync
            def _(sp):
                for dst, name in ((w1T, "w1T"), (w2T, "w2T"), (b1, "b1"), (w1sT, "w1sT"), (tmp16[:, 0:2], "temp_bias")):
                    sp.dma_start(dst, a[name]).then_inc(s_gw, 16)
                sp.dma_start(fl, a["floor"].partition_broadcast(P)).then_inc(s_gw, 16)
                sp.wait_ge(s_gw, 96)

            @block.scalar
            def _(act):
                act.preload_act_table_set("natural_log_exp_and_others")
                link = chain(act, chain_act)
                for w in range(NP_):
                    act.activation(slab[:, 5 + w, :], paths[w], ACT.Square).then_inc(s_sqr, 1)
                act.wait_ge(s_gw, 96)
                link(act.activation(tmp16[:, 2:3], tmp16[:, 0:1], ACT.Abs))
                link(act.activation(tmp16[:, 3:4], tmp16[:, 2:3], ACT.Exp, scale=-1.0))
                act.activation(tmp16[:, 4:5], tmp16[:, 3:4], ACT.Ln, bias=one1[0:K16]).then_inc(s_tmp, 1)
                act.activation(flt, fl, ACT.Exp, scale=-1.0).then_inc(s_tmp, 1)
                for g in range(0, 8, 2):
                    act.wait_ge(s_stp, g + 1)
                    for i in range(4):
                        k = act.activation(stT[:, 4 * g + i:C * (NCH - 1) + 4 * g + i + 1:C],
                                           bank[g][C * i:C * i + C, 0:P], ACT.Copy)
                    k.then_inc(s_sta, 1)

            @block.vector
            def _(dve):
                link = chain(dve, chain_dve)
                for w in range(NP_):
                    dve.tensor_reduce(sums[:, w, :], paths[w].rearrange("p (n d) -> p n d", d=DH), AX, ALU.add).then_inc(s_red, 1)
                    dve.wait_ge(s_sqr, w + 1)
                    dve.tensor_reduce(sqs[:, w, :], slab[:, 5 + w, :].rearrange("p (n d) -> p n d", d=DH), AX, ALU.add).then_inc(s_red, 1)
                dve.wait_ge(s_red, 2 * NP_)
                for w in range(NP_):
                    i = dve.tensor_scalar(st[:, :, w, :, 0], sums[:, w, :].rearrange("p (j h) -> p j h", h=H), 1.0 / DH, None, ALU.mult)
                link(i)
                for w in range(NP_):
                    i = dve.tensor_tensor(m2[:, w, :].rearrange("p (j h) -> p j h", h=H), st[:, :, w, :, 0], st[:, :, w, :, 0], ALU.mult)
                link(i)
                for w in range(NP_):
                    i = dve.scalar_tensor_tensor(st[:, :, w, :, 1], sqs[:, w, :].rearrange("p (j h) -> p j h", h=H), 1.0 / DH,
                                                 m2[:, w, :].rearrange("p (j h) -> p j h", h=H), ALU.mult, ALU.subtract)
                i.then_inc(s_st, 1)
                dve.wait_ge(s_tmp, 2)
                link(dve.tensor_scalar(tmp16[:, 5:6], tmp16[:, 0:1], 0.0, 1e-4, ALU.max, ALU.add))
                link(dve.tensor_tensor(tmp16[:, 6:7], tmp16[:, 5:6], tmp16[:, 4:5], ALU.add))
                link(dve.reciprocal(tmp16[:, 7:8], tmp16[:, 6:7]))
                link(dve.tensor_scalar(flt, flt, 1.0, None, ALU.add))
                link(dve.reciprocal(fl, flt))
                link(dve.tensor_scalar(fl, fl, 0.05, None, ALU.mult))
                for g in range(1, 8, 2):
                    dve.wait_ge(s_stp, g + 1)
                    for i in range(4):
                        k = dve.tensor_copy(stT[:, 4 * g + i:C * (NCH - 1) + 4 * g + i + 1:C], bank[g][C * i:C * i + C, 0:P])
                    k.then_inc(s_std, 1)

            @block.tensor
            def _(pe):
                pe.wait_ge(s_st, 1)
                for g in range(8):
                    pe.transpose(bank[g][:, 0:P], slab[:, 10, P * g:P * g + P], ident).then_inc(s_stp, 1)

        hm = slab[:, 6:8, 0:2048].rearrange("p n (m t) -> p n m t", m=4)
        lT = slab[0:K16, 8, :]
        probs = slab[:, 7, 2048:2560].rearrange("p (n w) -> p n w", w=NP_)
        s_hm, s_gel, s_lg, s_lt, s_ltt = (sem(x) for x in ("s_hm", "s_gel", "s_lg", "s_lt", "s_ltt"))
        with nc.Block() as block:
            @block.tensor
            def _(pe):
                def logits(b):
                    pe.wait_ge(s_gel, 2 * b + 2)
                    if b >= 2:
                        pe.wait_ge(s_lt, b - 1)
                    for k in range(2):
                        m = pe.matmul(bank[4 + b % 2][0:K16, :], w2T[:, k, :], hm[:, b % 2, k, :], start=k == 0, stop=k == 1)
                    m.then_inc(s_lg, 1)

                for b in range(B):
                    for k in range(2):
                        n = 2 * b + k
                        if n >= 4:
                            pe.wait_ge(s_gel, n - 3)
                        o = bank[n % 4]
                        pe.matmul(o[:], w1T[:, P * k:P * k + P], hT[:, b, :], start=True, stop=False)
                        pe.matmul(o[:], w1sT[:, P * k:P * k + P], stT[:, T * b:T * b + T], start=False, stop=True).then_inc(s_hm, 1)
                    if b:
                        logits(b - 1)
                logits(B - 1)
                pe.wait_ge(s_lt, B)
                for j in range(C):
                    m = pe.transpose(bank[6][:, K16 * j:K16 * j + K16], lT[:, j:C * (NCH - 1) + j + 1:C], ident[0:K16, 0:K16])
                m.then_inc(s_ltt, 1)

            @block.scalar
            def _(act):
                for b in range(B):
                    for k in range(2):
                        n = 2 * b + k
                        act.wait_ge(s_hm, n + 1)
                        if b >= 2:
                            act.wait_ge(s_lg, b - 1)
                        act.activation(hm[:, b % 2, k, :], bank[n % 4][:], ACT.Gelu, bias=b1[:, k:k + 1]).then_inc(s_gel, 1)

            @block.vector
            def _(dve):
                for b in range(B):
                    dve.wait_ge(s_lg, b + 1)
                    dve.tensor_scalar(lT[:, T * b:T * b + T], bank[4 + b % 2][0:K16, :], tmp16[:, 1:2], tmp16[:, 7:8],
                                      ALU.add, ALU.mult).then_inc(s_lt, 1)

        mixT = slab[:, 2, :]
        x1 = slab[:, 0, :].rearrange("p (t d) -> p t d", d=D)
        gt = slab[:, 10, 0:1024].rearrange("p (s n) -> p s n", n=P)
        e = slab[:, 7, 2560:3072].rearrange("p (n w) -> p n w", w=NP_)
        woT = slab[:, 7, 3072:3072 + D]
        onorm = slab[:, 7, 3200:3201]
        wga = slab[:, 7, 3328:3328 + D]
        crep = slab[:, 10, 1024:2048].rearrange("p (b n) -> p b n", b=B)
        gaR = slab[:, 10, 2048:3072].rearrange("p (b n) -> p b n", b=B)
        gab = slab[:, 10, 3072:4096].rearrange("p (b n) -> p b n", b=B)
        stx = slab[:, 10, 3200:3200 + 6 * NT].rearrange("p (t s) -> p t s", s=6)
        s_vp = sem("s_vp")
        s_xagain, s_wo, s_mx, s_ex, s_pr, s_crep, s_ga2, s_wog, s_m1, s_mix, s_ms, s_rr, s_mixn, s_mt, s_mte, s_wp, s_x1 = (
            sem(x) for x in ("s_xagain", "s_wo", "s_mx", "s_ex", "s_pr", "s_crep", "s_ga2", "s_wog", "s_m1", "s_mix", "s_ms", "s_rr",
                             "s_mixn", "s_mt", "s_mte", "s_wp", "s_x1done"))
        JQ = 4
        with nc.Block() as block:
            @block.sync
            def _(sp):
                sp.dma_start(woT, a["woT"]).then_inc(s_wo, 16)
                sp.dma_start(onorm, a["onorm"]).then_inc(s_wo, 16)
                sp.dma_start(wga, a["wga"]).then_inc(s_wo, 16)
                sp.dma_start(x1, a["x"].rearrange("t p d -> p t d")).then_inc(s_xagain, 16)

            @block.tensor
            def _(pe):
                pe.wait_ge(s_crep, 1)
                pe.wait_ge(s_wo, 48)
                for b in range(B):
                    m = pe.matmul(bank[4 + b // 4][:, P * (b % 4):P * (b % 4) + P], crep[:, b, :], wga, start=True, stop=True)
                m.then_inc(s_ga2, 1)
                for q in range(JQ):
                    pe.wait_ge(s_mixn, q + 1)
                    for g in range(2):
                        n = 2 * q + g
                        if n >= 4:
                            pe.wait_ge(s_mte, n - 3)
                        for i in range(4):
                            j = 4 * n + i
                            m = pe.transpose(bank[n % 4][:, P * i:P * i + P], slab[:, 5, P * j:P * j + P], ident)
                        m.then_inc(s_mt, 1)
                pe.wait_ge(s_mte, 8)
                pe.wait_ge(s_wog, B)
                for b in range(B):
                    if b >= 4:
                        pe.wait_ge(s_x1, b - 3)
                    for t in range(TPB):
                        m = pe.matmul(bank[b % 4][:, P * t:P * t + P], mixT[:, T * b + P * t:T * b + P * t + P], gaR[:, b, :],
                                      start=True, stop=True)
                    m.then_inc(s_wp, 1)

            @block.scalar
            def _(act):
                act.preload_act_table_set("natural_log_exp_and_others")
                act.wait_ge(s_mx, 1)
                act.activation(e, e, ACT.Exp).then_inc(s_ex, 1)
                link = chain(act, chain_act)
                for q in range(JQ):
                    part = slice(1024 * q, 1024 * q + 1024)
                    act.wait_ge(s_mix, q + 1)
                    act.activation(slab[:, 6, part], slab[:, 5, part], ACT.Square).then_inc(s_m1, 1)
                    act.wait_ge(s_ms, q + 1)
                    n = slice(32 * q, 32 * q + 32)
                    link(act.activation(gt[:, 5, n], gt[:, 4, n], ACT.Ln, bias=eps_ln, scale=1.0 / DH))
                    act.activation(gt[:, 6, n], gt[:, 5, n], ACT.Exp, scale=-0.5).then_inc(s_rr, 1)
                for n in range(8):
                    act.wait_ge(s_mt, n + 1)
                    dst = mixT.rearrange("p (c j) -> p c j", j=C)[:, :, 4 * n:4 * n + 4]
                    act.activation(dst, bank[n % 4][:].rearrange("p (j c) -> p c j", j=4), ACT.Copy).then_inc(s_mte, 1)

            @block.gpsimd
            def _(pool):
                pool.tensor_copy(crep, bc(cT[:], 2, P)).then_inc(s_crep, 1)
                pool.wait_ge(s_pr, 1)
                for q in range(JQ):
                    link = chain(pool, chain_pool)
                    part, n = slice(1024 * q, 1024 * q + 1024), slice(32 * q, 32 * q + 32)
                    v3 = lambda t: t[:, part].rearrange("p (n d) -> p n d", d=DH)
                    pool.tensor_tensor(v3(v_c), v3(v_c), bc(probs[:, n, 3], 2, DH), ALU.mult).then_inc(s_vp, 1)

            @block.vector
            def _(dve):
                link = chain(dve, chain_dve)
                logit = bank[6][:].rearrange("p (n w) -> p n w", w=NP_)
                link(dve.tensor_reduce(gt[:, 0, :], logit, AX, ALU.max))
                dve.tensor_tensor(e, logit, bc(gt[:, 0, :], 2, NP_), ALU.subtract).then_inc(s_mx, 1)
                dve.wait_ge(s_ex, 1)
                link(dve.tensor_reduce(gt[:, 1, :], e, AX, ALU.add))
                link(dve.reciprocal(gt[:, 2, :], gt[:, 1, :]))
                link(dve.tensor_tensor(e, e, bc(gt[:, 2, :], 2, NP_), ALU.mult))
                link(dve.tensor_tensor(e.rearrange("p (j h) w -> p j (h w)", h=H), e.rearrange("p (j h) w -> p j (h w)", h=H),
                                       bc(fl, 1, C), ALU.max))
                link(dve.tensor_reduce(gt[:, 1, :], e, AX, ALU.add))
                link(dve.reciprocal(gt[:, 2, :], gt[:, 1, :]))
                dve.tensor_tensor(probs, e, bc(gt[:, 2, :], 2, NP_), ALU.mult).then_inc(s_pr, 1)
                dve.wait_ge(s_pr, 1)
                for q in range(JQ):
                    part, n = slice(1024 * q, 1024 * q + 1024), slice(32 * q, 32 * q + 32)
                    v3 = lambda t: t[:, part].rearrange("p (n d) -> p n d", d=DH)
                    mixed = slab[:, 5, :]
                    dve.tensor_tensor(v3(mixed), v3(short_c), bc(probs[:, n, 0], 2, DH), ALU.mult)
                    dve.tensor_tensor(v3(long_c), v3(long_c), bc(probs[:, n, 1], 2, DH), ALU.mult)
                    link(dve.tensor_tensor(v3(delta_c), v3(delta_c), bc(probs[:, n, 2], 2, DH), ALU.mult))
                    link(dve.tensor_tensor(mixed[:, part], mixed[:, part], long_c[:, part], ALU.add))
                    link(dve.tensor_tensor(mixed[:, part], mixed[:, part], delta_c[:, part], ALU.add))
                    dve.wait_ge(s_vp, q + 1)
                    dve.tensor_tensor(mixed[:, part], mixed[:, part], v_c[:, part], ALU.add).then_inc(s_mix, 1)
                    dve.wait_ge(s_m1, q + 1)
                    dve.tensor_reduce(gt[:, 4, n], slab[:, 6, part].rearrange("p (n d) -> p n d", d=DH), AX, ALU.add).then_inc(s_ms, 1)
                    dve.wait_ge(s_rr, q + 1)
                    dve.tensor_tensor(v3(mixed), v3(mixed), bc(gt[:, 6, n], 2, DH), ALU.mult).then_inc(s_mixn, 1)
                dve.wait_ge(s_ga2, 1)
                for k in range(2):
                    half = slice(4 * k, 4 * k + 4)
                    o = bank[4 + k][:].rearrange("p (b n) -> p b n", b=4)
                    i = dve.tensor_copy(gab[:, half, :], o)
                link(i)
                gate_sign(dve, link, gaR, gab, gab)
                link(dve.tensor_scalar(woT, woT, onorm, None, ALU.mult))
                for b in range(B):
                    dve.tensor_tensor(gaR[:, b, :], gaR[:, b, :], woT, ALU.mult).then_inc(s_wog, 1)
                dve.wait_ge(s_xagain, 16)
                for b in range(B):
                    dve.wait_ge(s_wp, b + 1)
                    tiles = slice(TPB * b, TPB * b + TPB)
                    link(dve.tensor_tensor(x1[:, tiles, :], x1[:, tiles, :], bank[b % 4][:].rearrange("p (t d) -> p t d", d=D),
                                           ALU.add))
                    for t in range(TPB * b, TPB * b + TPB):
                        i = dve.bn_stats(stx[:, t, :], x1[:, t, :])
                    i.then_inc(s_x1, 1)
        if stop == 11:
            return dump(nc, sem, out, slab, [0, 5, 1, 7])

        w2 = slab[:, 1, 0:4 * D].rearrange("p (k d) -> p k d", k=4)
        wmod2 = slab[:, 1, 512:896]
        cols = slab[:, 1, 896:902]
        vbR = slab[:, 1, 1024:1024 + D]
        obR = slab[:, 1, 1152:1152 + T].rearrange("p (t d) -> p t d", d=D)
        modR = slab[:, 2, 0:3 * B * D].rearrange("p (b k d) -> p b k d", b=B, k=3)
        gtmp = slab[:, 2, 3 * B * D:].rearrange("p (b d) -> p b d", b=B)
        gtmp2 = slab[:, 3, 0:B * D].rearrange("p (b d) -> p b d", b=B)
        identb = sb("identb", [P, P], BF16)
        nb = slab[:, 3, :].rearrange("p (n t) -> p n t", t=T)
        h2buf = [nb[:, k, :] for k in range(3)]
        xh2, xn2 = nb[:, 3, :], nb[:, 4, :]
        outbuf = [nb[:, 5 + k, :] for k in range(2)]
        fb = slab[:, 4, :].rearrange("p (n t) -> p n t", t=T)
        xnT = [fb[:, k, :] for k in range(2)]
        qf, kf, att, attT = fb[:, 2, :], fb[:, 3, :], fb[:, 4, :], fb[:, 5, :]
        t1 = fb[:, 6, :]
        half = lambda k, n: slab[:, k, :].bitcast(BF16)[:, n * 4096:n * 4096 + 4096].rearrange("p (h t) -> p h t", h=FH)
        qstack = [half(5 + k, 0) for k in range(3)]
        kstack = [half(5 + k, 1) for k in range(3)]
        vaug = [slab[:, 8, 1024 * k:1024 * k + 1024].rearrange("p (t h d) -> p t h d", t=TPB, h=FH) for k in range(3)]
        oc = [slab[:, 8, 3072 + T * k:3072 + T * k + T] for k in range(2)]
        pT = slab[:, 9, :].rearrange("p (n t) -> p n t", t=T)
        sp10 = slab[:, 10, :]
        qparts = sp10[:, 0:768].bitcast(BF16).rearrange("p (n t) -> p n t", n=3)
        kparts = sp10[:, 768:1536].bitcast(BF16).rearrange("p (n t) -> p n t", n=3)
        res = sp10[:, 1536:2048]
        mx = sp10[:, 2048:2080]
        mm = sp10[:, 2080:2112].bitcast(BF16)
        mT = sp10[0:2 * 32, 2112:2176].bitcast(BF16)
        st3 = sp10[:, 2208:2232].rearrange("p (t s) -> p t s", s=6)
        mv3 = sp10[:, 2232:2240].rearrange("p (t s) -> p t s", s=2)
        rr = sp10[:, 2240:2256].rearrange("p (n t) -> p n t", t=TPB)
        rc = sp10[:, 2256:2288].rearrange("p (g t h) -> p g t h", g=2, t=TPB)
        mvx = slab[:, 10, 3072:3072 + 2 * NT].rearrange("p (t s) -> p t s", s=2)
        lnx = slab[:, 10, 3136:3136 + NT]
        rx = slab[:, 10, 3168:3168 + NT]
        s_mvx, s_lnx, s_rx = sem("s_mvx"), sem("s_lnx"), sem("s_rx")
        crep8 = slab[:, 10, 0:1024].rearrange("p (b n) -> p b n", b=B)
        scale = float(D) ** -0.5
        s_w2, s_cr, s_mr2, s_ms2, s_me2 = (sem(x) for x in ("s_w2", "s_cr", "s_mr2", "s_ms2", "s_me2"))
        with nc.Block() as block:
            @block.sync
            def _(sp):
                sp.dma_start(w2, a["w2"]).then_inc(s_w2, 16)
                sp.dma_start(wmod2, a["wmod2"]).then_inc(s_w2, 16)
                sp.dma_start(cols[:, 0:4], a["cols"]).then_inc(s_w2, 16)
                sp.dma_start(vbR, a["v_b"].partition_broadcast(P)).then_inc(s_w2, 16)
                sp.dma_start(slab[:, 1, 1152:1152 + T], a["obR"].partition_broadcast(P)).then_inc(s_w2, 16)

            @block.gpsimd
            def _(pool):
                link = chain(pool, chain_pool)
                link(pool.tensor_copy(identb[:], ident))
                link(pool.memset(xnT[0], 0.0))
                for k in range(3):
                    link(pool.memset(kstack[k][96:98, :, :], 1.0))
                    link(pool.memset(vaug[k][:, :, :, FD:FD + 1], 1.0))
                    link(pool.memset(vaug[k][:, :, :, FD + 1:], 0.0))

            @block.tensor
            def _(pe):
                pe.wait_ge(s_w2, 80)
                for b in range(B):
                    pe.wait_ge(s_cr, b + 1)
                    pe.matmul(bank[b][:, 0:3 * D], crep8[:, b, :], wmod2, start=True, stop=True).then_inc(s_mr2, 1)

            @block.scalar
            def _(act):
                act.preload_act_table_set("natural_log_exp_and_others")
                act.wait_ge(s_mvx, 1)
                act.activation(lnx, mvx[:, :, 1], ACT.Ln, bias=eps_ln).then_inc(s_lnx, 1)
                act.wait_ge(s_lnx, 1)
                act.activation(rx, lnx, ACT.Exp, scale=-0.5).then_inc(s_rx, 1)
                act.wait_ge(s_rx, 1)

            @block.vector
            def _(dve):
                link = chain(dve, chain_dve)
                for t in range(NT):
                    i = dve.bn_aggr(mvx[:, t, :], stx[:, t, :])
                i.then_inc(s_mvx, 1)
                for b in range(B):
                    dve.tensor_copy(crep8[:, b, :], cT[:, b:b + 1].broadcast_to([P, P])).then_inc(s_cr, 1)
                dve.wait_ge(s_w2, 80)
                link(dve.tensor_scalar(cols[:, 4:5], cols[:, 2:3], scale, None, ALU.mult))
                for b in range(B):
                    dve.wait_ge(s_mr2, b + 1)
                    o = bank[b][:, 0:3 * D].rearrange("p (k d) -> p k d", k=3)
                    dve.tensor_copy(modR[:, b, 0, :], o[:, 0, :])
                    dve.tensor_scalar(modR[:, b, 1, :], o[:, 1, :], 1.0, None, ALU.add)
                    i = dve.tensor_copy(gtmp[:, b, :], o[:, 2, :])
                link(i)
                gate_sign(dve, link, modR[:, :, 2, :], gtmp, gtmp2)

        QP = (0, 0, 1, 1, 0, 2)
        KP = (0, 1, 0, 1, 2, 0)
        part_dram = nc.dram_tensor("qk_parts", (2, FH, FD, 3, T), BF16, kind="Internal").ap()
        m_dram = nc.dram_tensor("neg_max", (64, P), BF16, kind="Internal").ap()
        names = ("f_v1 f_r1 f_xh f_h2 f_v2 f_r2 f_xn f_tT f_xnT f_q f_qf f_k f_kf f_v f_V f_split f_spq f_spk f_stack "
                 "f_s1 f_max f_mm f_mT f_mr f_mw f_mq f_sT f_exp f_pv f_oc f_oT f_rc f_at f_aT f_attT f_op f_t1 f_y "
                 "f_out f_store f_ln f_ob f_st2 f_st3 f_rcy f_mh").split()
        s = {n: sem(n) for n in names}

        def attention(engine, stage):
            for k in (-2, -1):
                stage(k, k % 3, k + 2 < B, k + 1 >= 0, k >= 0)
            with engine.Fori(0, 2) as trip:
                for r in range(3):
                    stage(trip * 3 + r, r, True, True, True)
            for k in (6, 7):
                stage(k, k % 3, False, k + 1 < B, True)

        with nc.Block() as block:
            @block.sync
            def _(sp):
                def stage(k, r, do_a, do_m, do_b):
                    if do_a:
                        b, rb = k + 2, (r + 2) % 3
                        for n, (parts, stack, which, written) in enumerate(((qparts, qstack[rb], QP, "f_spq"),
                                                                            (kparts, kstack[rb], KP, "f_spk"))):
                            sp.wait_ge(s["f_split"], 2 * b + n + 1)
                            sp.dma_start(part_dram[n].rearrange("h d n t -> (h d) n t"), parts).then_inc(s[written], 16)
                            sp.wait_ge(s[written], 16 * b + 16)
                            for g in range(6):
                                sp.dma_start(stack[FD * g:FD * g + FD, :, :],
                                             part_dram[n, :, :, which[g], :].rearrange("h d t -> d h t")).then_inc(s["f_stack"], 16)
                    if do_m:
                        b, rb = k + 1, (r + 1) % 3
                        sp.wait_ge(s["f_mr"], b + 1)
                        sp.dma_start(m_dram, mT).then_inc(s["f_mw"], 16)
                        sp.wait_ge(s["f_mw"], 16 * b + 16)
                        sp.dma_start(qstack[rb][96:98, :, :], m_dram.rearrange("(n h t) q -> n h (t q)", n=2, h=FH)).then_inc(s["f_mq"], 16)
                    if do_b:
                        b = k
                        sp.wait_ge(s["f_out"], b + 1)
                        if isinstance(b, int):
                            dst, src = out[TPB * b:TPB * b + TPB], x1[:, TPB * b:TPB * b + TPB, :]
                        else:
                            dst, src = out[bass.ds(b * TPB, TPB)], x1[:, bass.ds(b * TPB, TPB), :]
                        sp.dma_start(dst.rearrange("t p d -> p t d"), src).then_inc(s["f_store"], 16)
                attention(sp, stage)
                sp.wait_ge(s["f_store"], 16 * B)

            @block.tensor
            def _(pe):
                misc, obank = bank[7], bank[6]

                def share(i):
                    return (28 * i) // 16, (28 * (i + 1)) // 16

                def stage(k, r, do_a, do_m, do_b):
                    a_, m_, b_ = k + 2, k + 1, k
                    ra, rm, rb = (r + 2) % 3, (r + 1) % 3, r
                    pa = {}

                    def pass1(n0, n1):
                        for n in range(n0, n1):
                            h, t = n // TPB, n % TPB
                            if n == 0:
                                pe.wait_ge(s["f_stack"], 192 * m_ + 192)
                            if not (n < 2 and isinstance(k, int) and k == -1):
                                pe.wait_ge(s["f_max"], 32 * m_ + n - 1)
                            pe.matmul(bank[n % 2][:], qstack[rm][0:96, h, P * t:P * t + P], kstack[rm][0:96, h, :],
                                      start=True, stop=True).then_inc(s["f_s1"], 1)

                    def scoresT(u, pr):
                        g, kt = u // 4, u % 4
                        n = 2 * u + pr
                        if n == 0:
                            pe.wait_ge(s["f_mq"], 16 * b_ + 16)
                        if n >= 2:
                            pe.wait_ge(s["f_exp"], 16 * b_ + n - 1)
                        for i in range(2):
                            h = 4 * g + 2 * pr + i
                            m = pe.matmul(bank[2 + 2 * pr + i][:], kstack[rb][0:98, h, P * kt:P * kt + P],
                                          qstack[rb][0:98, h, :], start=True, stop=True)
                        m.then_inc(s["f_sT"], 1)

                    def pv(u):
                        g, kt = u // 4, u % 4
                        if u == 0:
                            pe.wait_ge(s["f_V"], b_ + 1)
                        if kt == 0 and g == 1:
                            pe.wait_ge(s["f_oc"], 2 * b_ + 1)
                        pe.wait_ge(s["f_exp"], 16 * b_ + 2 * u + 2)
                        for i in range(4):
                            m = pe.matmul(obank[32 * i:32 * i + 32, :], vaug[rb][:, kt, 4 * g + i, :], pT[:, 4 * (u % 2) + i, :],
                                          start=kt == 0, stop=kt == 3)
                        m.then_inc(s["f_pv"], 1)

                    def otrans(g):
                        pe.wait_ge(s["f_oc"], 2 * b_ + g + 1)
                        for t in range(TPB):
                            m = pe.transpose(misc[:, P * t:P * t + P], oc[g][:, P * t:P * t + P], ident)
                        m.then_inc(s["f_oT"], 1)

                    def xtrans():
                        pe.wait_ge(s["f_xn"], a_ + 1)
                        for t in range(TPB):
                            m = pe.transpose(misc[:, P * t:P * t + P], xn2[:, P * t:P * t + P], ident)
                        m.then_inc(s["f_tT"], 1)

                    def proj(kind):
                        if kind == 0:
                            pe.wait_ge(s["f_xnT"], a_ + 1)
                            pe.matmul(misc[:], w2[:, 0, :], xnT[0], start=True, stop=True).then_inc(s["f_q"], 1)
                        elif kind == 1:
                            pe.wait_ge(s["f_qf"], a_ + 1)
                            pe.matmul(misc[:], w2[:, 1, :], xnT[0], start=True, stop=True).then_inc(s["f_k"], 1)
                        else:
                            pe.wait_ge(s["f_kf"], a_ + 1)
                            for t in range(TPB):
                                m = pe.matmul(misc[:, P * t:P * t + P], xnT[0][:, P * t:P * t + P], w2[:, 2, :], start=True, stop=True)
                            m.then_inc(s["f_v"], 1)

                    def atrans():
                        pe.wait_ge(s["f_at"], 2 * b_ + 2)
                        for t in range(TPB):
                            m = pe.transpose(misc[:, P * t:P * t + P], att[:, P * t:P * t + P], ident)
                        m.then_inc(s["f_aT"], 1)

                    def oproj():
                        pe.wait_ge(s["f_attT"], b_ + 1)
                        for t in range(TPB):
                            w = D >> t
                            m = pe.matmul(misc[:, P * t:P * t + w], attT[0:w, P * t:P * t + P], w2[0:w, 3, 0:w], start=True, stop=True)
                        m.then_inc(s["f_op"], 1)

                    for u in range(8):
                        for pr in range(2):
                            if do_b:
                                scoresT(u, pr)
                            if do_m:
                                pass1(*share(2 * u + pr))
                        if do_b and u:
                            pv(u - 1)
                        if do_a and u == 1:
                            xtrans()
                        if do_a and u in (2, 3, 4):
                            proj(u - 2)
                        if do_b and u == 6:
                            if do_a:
                                pe.wait_ge(s["f_V"], a_ + 1)
                            otrans(0)
                    if do_b:
                        pv(7)
                    if do_b:
                        pe.wait_ge(s["f_at"], 2 * b_ + 1)
                        otrans(1)
                    if do_m:
                        pass1(28, 30)
                    if do_b:
                        atrans()
                    if do_m:
                        pass1(30, 32)
                    if do_b:
                        oproj()
                    if do_m:
                        pe.wait_ge(s["f_mm"], m_ + 1)
                        pe.transpose(obank[0:32, 0:64].bitcast(BF16), mm[:, 0:32], identb[:])
                        pe.transpose(obank[32:64, 0:64].bitcast(BF16), mm[:, 32:64], identb[:]).then_inc(s["f_mT"], 1)
                        pe.wait_ge(s["f_mr"], m_ + 1)
                    if do_b:
                        pe.wait_ge(s["f_rcy"], b_ + 1)
                    elif do_a and do_m:
                        pe.wait_ge(s["f_V"], a_ + 1)
                attention(pe, stage)

            @block.scalar
            def _(act):
                misc, obank = bank[7], bank[6]
                act.preload_act_table_set("natural_log_exp_and_others")

                def stage(k, r, do_a, do_m, do_b):
                    a_, m_, b_ = k + 2, k + 1, k
                    static = isinstance(k, int)

                    def rstd():
                        act.wait_ge(s["f_v2"], a_ + 1)
                        act.activation(rr[:, 0, :], mv3[:, :, 1], ACT.Ln, bias=eps_ln).then_inc(s["f_ln"], 1)
                        act.wait_ge(s["f_ln"], a_ + 1)
                        act.activation(rr[:, 1, :], rr[:, 0, :], ACT.Exp, scale=-0.5).then_inc(s["f_r2"], 1)

                    def exps(u):
                        for pr in range(2):
                            n = 2 * u + pr
                            act.wait_ge(s["f_sT"], 16 * b_ + n + 1)
                            if u >= 2:
                                act.wait_ge(s["f_pv"], 8 * b_ + u - 1)
                            src = wide[pr]
                            act.activation(pT[:, 4 * (u % 2) + 2 * pr:4 * (u % 2) + 2 * pr + 2, :], src, ACT.Exp).then_inc(s["f_exp"], 1)

                    def xevac():
                        act.wait_ge(s["f_tT"], a_ + 1)
                        for t in range(TPB):
                            w = D >> t
                            i = act.activation(xnT[0][0:w, P * t:P * t + P], misc[0:w, P * t:P * t + P], ACT.Identity,
                                               bias=cols[0:w, 1:2], scale=cols[0:w, 0:1])
                        i.then_inc(s["f_xnT"], 1)

                    def qkevac(kind):
                        if kind == 0:
                            act.wait_ge(s["f_q"], a_ + 1)
                            if not (static and k == -2):
                                act.wait_ge(s["f_split"], 2 * a_)
                            act.activation(qf, misc[:], ACT.Identity, bias=cols[:, 4:5], scale=scale).then_inc(s["f_qf"], 1)
                        else:
                            act.wait_ge(s["f_k"], a_ + 1)
                            act.activation(kf, misc[:], ACT.Identity, bias=cols[:, 3:4]).then_inc(s["f_kf"], 1)

                    def ocevac(g):
                        act.wait_ge(s["f_pv"], 8 * b_ + 4 * g + 4)
                        act.activation(oc[g], obank[:], ACT.Copy).then_inc(s["f_oc"], 1)

                    for u in range(8):
                        if do_b:
                            exps(u)
                            if u == 4:
                                ocevac(0)
                        if do_a and u == 0:
                            rstd()
                        if do_a and u == 1:
                            xevac()
                        if do_a and u in (2, 3):
                            qkevac(u - 2)
                    if do_b:
                        ocevac(1)
                        act.wait_ge(s["f_aT"], b_ + 1)
                        act.activation(attT, misc[:], ACT.Copy).then_inc(s["f_attT"], 1)
                    if do_m:
                        act.wait_ge(s["f_mT"], m_ + 1)
                        if not (static and k == -1):
                            act.wait_ge(s["f_mw"], 16 * m_)
                        act.activation(mT, obank[0:64, 0:64].bitcast(BF16), ACT.Copy).then_inc(s["f_mr"], 1)
                attention(act, stage)

            @block.gpsimd
            def _(pool):
                def batch(t, b, i=None):
                    if isinstance(b, int):
                        return t[:, b, i, :]
                    return t[:, bass.ds(b, 1), i, :].rearrange("p o d -> p (o d)")

                def stage(k, r, do_a, do_m, do_b):
                    a_, b_ = k + 2, k
                    static = isinstance(k, int)
                    h2 = h2buf[(r + 2) % 3]
                    link = lambda i, n: (i.then_inc(s["f_ob"], 1), pool.wait_ge(s["f_ob"], 9 * a_ + n))
                    if do_a:
                        v = lambda t: t.rearrange("p (t d) -> p t d", d=D)
                        pool.wait_ge(s["f_xh"], a_ + 1)
                        link(pool.tensor_tensor(v(xh2), v(xh2), bc(batch(modR, a_, 1), 1, TPB), ALU.mult), 1)
                        pool.tensor_tensor(v(h2), v(xh2), bc(batch(modR, a_, 0), 1, TPB), ALU.add).then_inc(s["f_h2"], 1)
                    if do_b:
                        if not do_a:
                            pool.wait_ge(s["f_y"], b_)
                        pool.tensor_tensor(t1, h2buf[r], slab[:, 1, 1152:1152 + T], ALU.add).then_inc(s["f_t1"], 1)
                    round_ = lambda dst, src: pool.tensor_tensor(dst, src, one1.broadcast_to([P, T]), ALU.mult)
                    if do_a:
                        for n, (src, parts, ready, written) in enumerate(((qf, qparts, "f_qf", "f_spq"), (kf, kparts, "f_kf", "f_spk"))):
                            pool.wait_ge(s[ready], a_ + 1)
                            if not (static and k == -2):
                                pool.wait_ge(s[written], 16 * a_)
                            o = 1 + 4 * n
                            link(round_(parts[:, 0, :], src), o + 1)
                            link(pool.tensor_tensor(res, src, parts[:, 0, :], ALU.subtract), o + 2)
                            link(round_(parts[:, 1, :], res), o + 3)
                            link(pool.tensor_tensor(res, res, parts[:, 1, :], ALU.subtract), o + 4)
                            round_(parts[:, 2, :], res).then_inc(s["f_split"], 1)
                attention(pool, stage)

            @block.vector
            def _(dve):
                misc = bank[7]

                def batch(t, b):
                    if isinstance(b, int):
                        return t[:, TPB * b:TPB * b + TPB, :]
                    return t[:, bass.ds(b * TPB, TPB), :]

                def gb(b):
                    if isinstance(b, int):
                        return modR[:, b, 2, :]
                    return modR[:, bass.ds(b, 1), 2, :].rearrange("p o d -> p (o d)")

                def stage(k, r, do_a, do_m, do_b):
                    a_, m_, b_ = k + 2, k + 1, k
                    static = isinstance(k, int)
                    h2 = h2buf[(r + 2) % 3]

                    def maxima(n0, n1):
                        for n in range(n0, n1):
                            dve.wait_ge(s["f_s1"], 32 * m_ + n + 1)
                            dve.tensor_reduce(mx[:, n:n + 1], bank[n % 2][:], AX, ALU.max).then_inc(s["f_max"], 1)

                    def statistics(src, st, mv, name, tag, between):
                        for t in range(TPB):
                            i = dve.bn_stats(st[:, t, :], src(t))
                        i.then_inc(s[tag], 1)
                        dve.wait_ge(s[tag], a_ + 1)
                        between()
                        for t in range(TPB):
                            i = dve.bn_aggr(mv[:, t, :], st[:, t, :])
                        i.then_inc(s[name], 1)

                    def x1tile(t):
                        if static:
                            return x1[:, TPB * a_ + t, :]
                        return x1[:, bass.ds(a_ * TPB + t, 1), :].rearrange("p o d -> p (o d)")

                    def normed(dst, src, mean, rstd, done):
                        for t in range(TPB):
                            i = dve.tensor_scalar(dst[:, P * t:P * t + P], src(t), mean(t), rstd(t), ALU.subtract, ALU.mult)
                        i.then_inc(s[done], 1)

                    def column(x, t):
                        if static:
                            return x[:, TPB * a_ + t:TPB * a_ + t + 1]
                        return x[:, bass.ds(a_ * TPB + t, 1)]

                    def onorm_(g):
                        dve.wait_ge(s["f_oT"], 2 * b_ + g + 1)
                        o = misc[:].rearrange("p (t h d) -> p t h d", t=TPB, h=4)
                        dve.reciprocal(rc[:, g, :, :], o[:, :, :, FD]).then_inc(s["f_rc"], 1)
                        dve.wait_ge(s["f_rc"], 2 * b_ + g + 1)
                        dst = att.rearrange("p (t h d) -> p t h d", t=TPB, h=FH)[:, :, 4 * g:4 * g + 4, :]
                        for t in range(TPB):
                            i = dve.tensor_tensor(dst[:, t], o[:, t, :, 0:FD], bc(rc[:, g, t, :], 2, FD), ALU.mult)
                        i.then_inc(s["f_at"], 1)

                    def final():
                        dve.wait_ge(s["f_t1"], b_ + 1)
                        dve.wait_ge(s["f_op"], b_ + 1)
                        for t in range(TPB):
                            w = D >> t
                            i = dve.tensor_tensor(t1[:, P * t:P * t + w], t1[:, P * t:P * t + w], misc[:, P * t:P * t + w], ALU.add)
                        i.then_inc(s["f_rcy"], 1)
                        dve.wait_ge(s["f_rcy"], b_ + 1)
                        v = lambda t: t.rearrange("p (t d) -> p t d", d=D)
                        dve.tensor_tensor(v(outbuf[0]), v(t1), bc(gb(b_), 1, TPB), ALU.mult).then_inc(s["f_y"], 1)
                        dve.wait_ge(s["f_y"], b_ + 1)
                        dve.tensor_tensor(batch(x1, b_), v(outbuf[0]), batch(x1, b_), ALU.add).then_inc(s["f_out"], 1)

                    if do_a:
                        normed(xh2, x1tile, lambda t: column(mvx[:, :, 0], t), lambda t: column(rx, t), "f_xh")
                    for u in range(8):
                        if do_m:
                            maxima((7 * u) // 2 + (u == 1 and do_a), (7 * u + 7) // 2)
                        if do_a and u == 0:
                            dve.wait_ge(s["f_h2"], a_ + 1)
                            tile = lambda t: h2[:, P * t:P * t + P]
                            statistics(tile, st3, mv3, "f_v2", "f_st3", lambda: do_m and maxima(3, 4))
                            dve.wait_ge(s["f_r2"], a_ + 1)
                            normed(xn2, tile, lambda t: mv3[:, t, 0:1], lambda t: rr[:, 1, t:t + 1], "f_xn")
                        if do_a and u == 5:
                            dve.wait_ge(s["f_v"], a_ + 1)
                            dst = vaug[(r + 2) % 3][:, :, :, 0:FD]
                            dve.tensor_tensor(dst, misc[:].rearrange("p (t h d) -> p t h d", t=TPB, h=FH),
                                              bc(vbR.rearrange("p (h d) -> p h d", h=FH), 1, TPB), ALU.add).then_inc(s["f_V"], 1)
                        if do_b and u == 7:
                            onorm_(0)
                    if do_b:
                        onorm_(1)
                    if do_m:
                        maxima(28, 32)
                        dve.wait_ge(s["f_max"], 32 * m_ + 32)
                        if not (static and k == -1):
                            dve.wait_ge(s["f_mT"], m_)
                        dve.tensor_scalar(mm[:, 0:32], mx, -1.0, None, ALU.mult).then_inc(s["f_mh"], 1)
                        dve.wait_ge(s["f_mh"], m_ + 1)
                        dve.scalar_tensor_tensor(mm[:, 32:64], mx, -1.0, mm[:, 0:32], ALU.mult, ALU.subtract).then_inc(s["f_mm"], 1)
                    if do_b:
                        final()
                attention(dve, stage)


def gate_sign(dve, link, dst, g, tmp):
    link(dve.tensor_scalar(dst, g, 0.0, 2.0, ALU.is_ge, ALU.mult))
    link(dve.scalar_tensor_tensor(tmp, g, -1.0, g, ALU.mult, ALU.max))
    link(dve.tensor_scalar(tmp, tmp, 0.25, None, ALU.max))
    link(dve.scalar_tensor_tensor(dst, dst, -1.0, tmp, ALU.add, ALU.mult))


def dump(nc, sem, out, slab, which):
    s = sem("s_dump")
    with nc.Block() as block:
        @block.sync
        def _(sp):
            for i, k in enumerate(which):
                sp.dma_start(out[i], slab[:, k, :]).then_inc(s, 16)
            sp.wait_ge(s, 16 * len(which))


def arrange(inputs):
    f = {k[3:]: np.asarray(v) for k, v in inputs.items()}
    d = {}
    d["x"] = f["attn_hidden_states"].reshape(NT, P, D)
    d["cT"] = f["c"].T
    wm = f["wmod"].reshape(D, 6, D)
    d["wmod1"] = wm[:, 0:2]
    d["wqkvT"] = np.stack([f["attn_W" + k].T for k in "qkv"], axis=1)
    d["taps"] = np.concatenate([f[f"attn_{k}conv_w"] for k in "qkv"], axis=1)
    d["wbrep"] = np.repeat(f["attn_Wb"].T, DH, axis=1)
    i32 = np.arange(C)
    part = np.arange(P) % C
    cst = np.zeros((P, C_END), np.float32)
    cst[:, C_IDENT:C_IDENT + P] = np.eye(P)
    cst[:, C_BONES:C_BONES + P] = np.kron(np.eye(H), np.ones((DH, DH)))
    cst[:, C_NEGA:C_NEGA + C] = -1.0 * (i32[None] > part[:, None])
    cst[:, C_CAUSAL:C_CAUSAL + C] = i32[None] >= part[:, None]
    cst[:, C_EYE:C_EYE + C] = i32[None] == part[:, None]
    cst[:, C_QUARTER:C_QUARTER + 4] = np.arange(P)[:, None] // C == np.arange(4)[None]
    d["consts"] = cst
    d["zeros"] = np.zeros((LONG - 1, D), np.float32)
    toep = np.zeros((WIN, D, C), np.float32)
    wl = f["attn_fir_long_w"].reshape(D, LONG)
    for i in range(C):
        toep[i:i + LONG, :, i] = wl.T
    d["toep"] = toep
    d["fsw"] = f["attn_fir_short_w"].reshape(D, SHORT)
    w1 = f["attn_gate_w1"]
    d["w1T"], d["w1sT"] = w1[:, :D].T, w1[:, D:].T
    d["w2T"] = f["attn_gate_w2"].T.reshape(2, P, 4 * H).transpose(1, 0, 2)
    d["b1"] = f["attn_gate_b1"].reshape(2, P).T
    d["temp_bias"] = np.stack([np.repeat(f["attn_log_temp"], 4), f["attn_base_bias"].reshape(-1)], axis=1)
    d["floor"] = f["attn_floor_raw"].reshape(-1)
    d["woT"] = f["attn_Wo"].T
    d["onorm"] = np.tile(f["attn_onorm_w"], H).reshape(D, 1)
    d["wga"] = wm[:, 2]
    d["w2"] = np.stack([f[f"ffn_{k}_w"].T for k in "qkvo"], axis=1)
    d["wmod2"] = wm[:, 3:6].reshape(D, 3 * D)
    d["cols"] = np.stack([f["ffn_norm_w"], f["ffn_norm_b"], f["ffn_q_b"], f["ffn_k_b"]], axis=1)
    d["v_b"] = f["ffn_v_b"]
    ob = np.zeros((TPB, D), np.float32)
    for t in range(TPB):
        ob[t, :D >> t] = f["ffn_o_b"][:D >> t]
    d["obR"] = ob.reshape(-1)
    return {k: np.ascontiguousarray(v) for k, v in d.items()}


def kernel(**inputs):
    import numpy as _np
    import concourse.bacc as _bacc
    from concourse import mybir as _mybir
    from concourse.bass_utils import run_bass_kernel_spmd as _run

    nc = _bacc.Bacc("TRN2", target_bir_lowering=False, num_devices=1)
    arrays = {"in_" + k: v for k, v in arrange(inputs).items()}
    a = {k: nc.dram_tensor(k, v.shape, _mybir.dt.from_np(v.dtype), kind="ExternalInput").ap() for k, v in arrays.items()}
    out = nc.dram_tensor("out", (NT, P, D), F32, kind="ExternalOutput").ap()
    build(nc, {k[3:]: v for k, v in a.items()}, out)
    r = _run(nc, [arrays], core_ids=[0])
    return r.results[0]["out"].reshape(B, T, D)
```

```python
from contextlib import ExitStack

import numpy as np
import concourse.bass as bass
from concourse import mybir

F32 = mybir.dt.float32
BF16 = mybir.dt.bfloat16
ALU = mybir.AluOpType
ACT = mybir.ActivationFunctionType
AX = mybir.AxisListType.X

P = 128
B, T, D = 8, 512, 128
NT = B * T // P
TPB = T // P
H, DH = 4, 32
C = 32
NCH = B * T // C
CPB = T // C
TAPS = 4
SHORT, LONG = 3, 63
WIN = C + LONG - 1
FH, FD = 8, 16
LN_EPS = 1e-5
HID = 256
ROW = 4096

C_IDENT, C_BONES, C_NEGA, C_CAUSAL, C_EYE, C_QUARTER, C_END = 0, 128, 256, 288, 320, 352, 356


class Chain:

    def __init__(self, engine, sem):
        self.engine, self.sem, self.n = engine, sem, 0

    def link(self, ins):
        self.n += 1
        ins.then_inc(self.sem, 1)
        self.engine.wait_ge(self.sem, self.n)


def bc(ap, axis, n):
    ap = ap.unsqueeze(axis)
    shape = list(ap.shape)
    shape[axis] = n
    return ap.broadcast_to(shape)


def build(nc, a, out, stop=99):
    with ExitStack() as ctx:
        def sb(name, shape, dt=F32):
            return ctx.enter_context(nc.sbuf_tensor(name, shape, dt))

        def sem(name):
            return ctx.enter_context(nc.semaphore(name))

        psum = ctx.enter_context(nc.psum_tensor("psum", [P, 8, 512], F32))
        bank = [psum[:, i, :] for i in range(8)]
        wide = [psum[:, 2:4, :], psum[:, 4:6, :]]
        slab = sb("slab", [P, 11, ROW])
        hT = sb("hT", [P, B, T])
        cst = sb("cst", [P, C_END])
        ident = cst[:, C_IDENT:C_IDENT + P]
        bones = cst[:, C_BONES:C_BONES + P]
        neg_strict = cst[:, C_NEGA:C_NEGA + C]
        causal = cst[:, C_CAUSAL:C_CAUSAL + C]
        eye32 = cst[:, C_EYE:C_EYE + C]
        quarter = cst[:, C_QUARTER:C_QUARTER + 4]
        cT = sb("cT", [P, B])
        modF = sb("modF", [P, 2, B])
        scratch = sb("scratch", [P, 2048])
        eps = sb("eps", [P, 3])
        eps_ln, eps_l2, one1 = eps[:, 0:1], eps[:, 1:2], eps[:, 2:3]
        chain_act, chain_dve, chain_pool = sem("chain_act"), sem("chain_dve"), sem("chain_pool")
        order = {}

        def chain(engine, s):
            if s not in order:
                order[s] = [0]
            count = order[s]

            def link(ins):
                count[0] += 1
                ins.then_inc(s, 1)
                engine.wait_ge(s, count[0])
            return link

        v_dram = nc.dram_tensor("v_padded", (B, LONG - 1 + T, D), F32, kind="Internal")
        a_dram = nc.dram_tensor("a_scratch", (NT, P, P), F32, kind="Internal").ap()
        t_dram = nc.dram_tensor("t_scratch", (NT, P, P), F32, kind="Internal").ap()
        h_dram = nc.dram_tensor("h_kept", (P, B, T), F32, kind="Internal").ap()

        xN = slab[:, 0, :].rearrange("p (t d) -> p t d", d=D)
        wmodF = slab[:, 1, 0:2 * D].rearrange("p (k d) -> p k d", k=2)
        wT = slab[:, 7, 0:3 * D].rearrange("p (k d) -> p k d", k=3)
        wbrep = slab[:, 7, 384:384 + D]
        taps = slab[:, 7, 512:512 + 3 * TAPS]
        stats = slab[:, 10, 0:6 * NT].rearrange("p (t s) -> p t s", s=6)
        meanvar = slab[:, 10, 256:256 + 2 * NT].rearrange("p (t s) -> p t s", s=2)
        rstd = slab[:, 10, 384:384 + NT]
        lnv = slab[:, 10, 448:448 + NT]
        xh = xN
        s_x = [sem(f"s_x{g}") for g in range(4)]
        s_w, s_c, s_eps = sem("s_w"), sem("s_c"), sem("s_eps")
        s_silu, s_mod, s_modc, s_stats, s_rstd, s_xh = (
            sem(x) for x in ("s_silu", "s_mod", "s_modc", "s_stats", "s_rstd", "s_xh"))
        with nc.Block() as block:
            @block.sync
            def _(sp):
                for g in range(4):
                    sp.dma_start(xN[:, 8 * g:8 * g + 8, :],
                                 a["x"][8 * g:8 * g + 8].rearrange("t p d -> p t d")).then_inc(s_x[g], 16)

            @block.gpsimd
            def _(pool):
                pool.memset(eps[:, 0:1], LN_EPS).then_inc(s_eps, 1)
                pool.memset(eps[:, 1:2], 1e-6).then_inc(s_eps, 1)
                pool.memset(eps[:, 2:3], 1.0).then_inc(s_eps, 1)

            @block.scalar
            def _(act):
                act.dma_start(cT[:], a["cT"]).then_inc(s_c, 16)
                act.dma_start(wmodF, a["wmod1"]).then_inc(s_c, 16)
                act.dma_start(cst[:], a["consts"]).then_inc(s_w, 16)
                act.dma_start(wT, a["wqkvT"]).then_inc(s_w, 16)
                act.dma_start(taps, a["taps"]).then_inc(s_w, 16)
                act.dma_start(wbrep, a["wbrep"]).then_inc(s_w, 16)
                act.wait_ge(s_c, 32)
                act.activation(cT[:], cT[:], ACT.Silu).then_inc(s_silu, 1)
                act.wait_ge(s_eps, 3)
                act.preload_act_table_set("natural_log_exp_and_others")
                for g in range(4):
                    act.wait_ge(s_stats, g + 1)
                    link = chain(act, chain_act)
                    link(act.activation(lnv[:, 8 * g:8 * g + 8], meanvar[:, 8 * g:8 * g + 8, 1], ACT.Ln, bias=eps_ln))
                    act.activation(rstd[:, 8 * g:8 * g + 8], lnv[:, 8 * g:8 * g + 8], ACT.Exp, scale=-0.5).then_inc(s_rstd, 1)

            @block.tensor
            def _(pe):
                pe.wait_ge(s_silu, 1)
                for k in range(2):
                    m = pe.matmul(bank[0][:, k * B:(k + 1) * B], wmodF[:, k, :], cT[:], start=True, stop=True)
                m.then_inc(s_mod, 1)

            @block.vector
            def _(dve):
                link = chain(dve, chain_dve)
                for g in range(4):
                    dve.wait_ge(s_x[g], 16)
                    for t in range(8 * g, 8 * g + 8):
                        i = dve.bn_stats(stats[:, t, :], xN[:, t, :])
                    link(i)
                    for t in range(8 * g, 8 * g + 8):
                        i = dve.bn_aggr(meanvar[:, t, :], stats[:, t, :])
                    i.then_inc(s_stats, 1)
                dve.wait_ge(s_mod, 1)
                dve.tensor_copy(modF[:, 0, :], bank[0][:, 0:B]).then_inc(s_modc, 1)
                dve.tensor_scalar(modF[:, 1, :], bank[0][:, B:2 * B], 1.0, None, ALU.add).then_inc(s_modc, 1)
                dve.wait_ge(s_w, 64)
                for g in range(4):
                    dve.wait_ge(s_rstd, g + 1)
                    for t in range(8 * g, 8 * g + 8):
                        i = dve.tensor_scalar(xh[:, t, :], xN[:, t, :], meanvar[:, t, 0:1], rstd[:, t:t + 1],
                                              ALU.subtract, ALU.mult)
                    i.then_inc(s_xh, 1)

        qs, ks, vT, bt = (slab[:, s, :] for s in (1, 2, 3, 4))
        sqq, sqk = slab[:, 6, :], slab[:, 5, :]
        vb = slab[:, 9, :]
        vnat = slab[:, 10, :].rearrange("p (n t d) -> p n t d", n=B, t=TPB)
        s_pe, s_evac, s_tap, s_conv, s_act2, s_bt, s_pool2, s_vnat, s_vout = (
            sem(x) for x in ("s_pe", "s_evac", "s_tap", "s_conv", "s_act2", "s_bt", "s_pool2", "s_vnat", "s_vout"))
        outputs = [("t", 0)]
        for b in range(B):
            if b + 1 < B:
                outputs.append(("t", b + 1))
            outputs += [("q", b), ("k", b), ("v", b), ("beta", b)]
            if b >= 2:
                outputs.append(("vt", b - 2))
        outputs += [("vt", B - 2), ("vt", B - 1)]

        def evacuations(n):
            group = ("q", "k", "v") if outputs[n][0] in ("q", "k", "v") else ("t", "beta", "vt")
            return s_conv if "q" in group else s_evac, sum(kind in group for kind, _ in outputs[:n + 1])

        with nc.Block() as block:
            @block.tensor
            def _(pe):
                for n, (kind, b) in enumerate(outputs):
                    if n >= 8:
                        pe.wait_ge(*evacuations(n - 8))
                    o = bank[n % 8]
                    if kind == "t":
                        for t in range(TPB):
                            m = pe.transpose(o[:, P * t:P * t + P], xh[:, TPB * b + t, :], ident)
                    elif kind == "vt":
                        pe.wait_ge(s_act2, 3 * b + 3)
                        for t in range(TPB):
                            m = pe.transpose(o[:, P * t:P * t + P], vT[:, T * b + P * t:T * b + P * t + P], ident)
                    elif kind == "beta":
                        m = pe.matmul(o[:], wbrep, hT[:, b, :], start=True, stop=True)
                    else:
                        if kind == "q":
                            pe.wait_ge(*evacuations(outputs.index(("t", b))))
                        m = pe.matmul(o[:], wT[:, "qkv".index(kind), :], hT[:, b, :], start=True, stop=True)
                    m.then_inc(s_pe, 1)

            @block.scalar
            def _(act):
                def silus(b):
                    act.wait_ge(s_conv, 3 * b + 3)
                    cols = slice(T * b, T * b + T)
                    for y in (qs, ks, vT):
                        act.activation(y[:, cols], y[:, cols], ACT.Silu).then_inc(s_act2, 1)

                for n, (kind, b) in enumerate(outputs):
                    act.wait_ge(s_pe, n + 1)
                    o, cols = bank[n % 8][:], slice(T * b, T * b + T)
                    if kind == "t":
                        act.activation(hT[:, b, :], o, ACT.Identity,
                                       bias=modF[:, 0, b:b + 1], scale=modF[:, 1, b:b + 1]).then_inc(s_evac, 1)
                    elif kind == "vt":
                        act.activation(vnat[:, b, :, :], o.rearrange("p (t d) -> p t d", d=D), ACT.Copy).then_inc(s_evac, 1)
                    elif kind == "beta":
                        act.activation(bt[:, cols], o, ACT.Tanh, scale=0.5).then_inc(s_evac, 1)
                        if b:
                            silus(b - 1)
                        if b == B - 1:
                            silus(b)
                    else:
                        k = "qkv".index(kind)
                        act.activation((qs, ks, vT)[k][:, cols], o, ACT.Identity,
                                       scale=taps[:, TAPS * k + TAPS - 1:TAPS * k + TAPS]).then_inc(s_tap, 1)

            @block.vector
            def _(dve):
                link = chain(dve, chain_dve)
                for b in range(B):
                    dve.wait_ge(s_tap, 3 * b + 3)
                    for d in range(1, TAPS):
                        for k, y in enumerate((qs, ks, vT)):
                            o = bank[outputs.index(("qkv"[k], b)) % 8]
                            j = TAPS * k + TAPS - 1 - d
                            y_ = y[:, T * b + d:T * b + T]
                            i = dve.scalar_tensor_tensor(y_, o[:, 0:T - d], taps[:, j:j + 1], y_, ALU.mult, ALU.add)
                            if d == TAPS - 1:
                                i.then_inc(s_conv, 1)
                        if d < TAPS - 1:
                            link(i)
                    dve.wait_ge(*evacuations(outputs.index(("beta", b))))
                    cols = slice(T * b, T * b + T)
                    dve.tensor_scalar(bt[:, cols], bt[:, cols], 0.5, 0.5, ALU.mult, ALU.add).then_inc(s_bt, 1)

            @block.gpsimd
            def _(pool):
                for b in range(B):
                    cols = slice(T * b, T * b + T)
                    pool.wait_ge(s_act2, 3 * b + 3)
                    pool.tensor_tensor(sqk[:, cols], ks[:, cols], ks[:, cols], ALU.mult)
                    pool.tensor_tensor(sqq[:, cols], qs[:, cols], qs[:, cols], ALU.mult)
                    pool.wait_ge(s_bt, b + 1)
                    pool.tensor_tensor(vb[:, cols], vT[:, cols], bt[:, cols], ALU.mult).then_inc(s_pool2, 1)

            @block.sync
            def _(sp):
                for b in range(B):
                    sp.dma_start(v_dram.ap()[b, 0:LONG - 1, :], a["zeros"]).then_inc(s_vout, 16)
                for b in range(B):
                    sp.wait_ge(*evacuations(outputs.index(("vt", b))))
                    sp.dma_start(v_dram.ap()[b, LONG - 1:, :].rearrange("(t p) d -> p t d", p=P), vnat[:, b, :, :]).then_inc(s_vout, 16)
                sp.wait_ge(s_vout, 32 * B)
        if stop == 2:
            return dump(nc, sem, out, slab, [1, 2, 3, 4])

        kbq = slab[:, 5:7, :].rearrange("p k (c i) -> p k c i", i=C)
        vk = slab[:, 0:2, :].rearrange("p s (t h k d) -> p (s t) h k d", h=H, k=2, d=DH)
        ak = slab[:, 7:9, :].rearrange("p s (t h k d) -> p (s t) h k d", h=H, k=2, d=DH)
        kn = ks
        a_nat = slab[:, 0, :].rearrange("p (t h i) -> p t h i", h=H, i=C)
        X = slab[:, 10, :]
        s_ss, s_ln, s_rs, s_qn, s_knorm, s_kb, s_g, s_ga, s_adma, s_xdma = (
            sem(x) for x in ("s_ss", "s_ln", "s_rs", "s_qn", "s_knorm", "s_kb", "s_g", "s_ga", "s_adma", "s_xdma"))
        TG = 8
        s_hout, s_hin = sem("s_hout"), sem("s_hin")
        with nc.Block() as block:
            @block.tensor
            def _(pe):
                def products(g):
                    pe.wait_ge(s_kb, 2 * g + 2)
                    pe.wait_ge(s_qn, 2 * g + 2)
                    for h in range(H):
                        if g:
                            pe.wait_ge(s_ga, H * (g - 1) + h + 1)
                        o = bank[4 + h][:].rearrange("p (t k i) -> p t k i", k=2, i=C)
                        for t in range(TG):
                            for c in range(4):
                                chunk = 4 * (TG * g + t) + c
                                m = pe.matmul(o[C * c:C * c + C, t, :, :],
                                              kn[DH * h:DH * h + DH, C * chunk:C * chunk + C],
                                              kbq[DH * h:DH * h + DH, :, chunk, :], start=True, stop=True)
                        m.then_inc(s_g, 1)

                for n in range(2 * B):
                    b, src = n // 2, (sqk, sqq)[n % 2]
                    if n >= 4:
                        pe.wait_ge(s_ln, n - 3)
                    pe.matmul(bank[n % 4][:], bones, src[:, T * b:T * b + T], start=True, stop=True).then_inc(s_ss, 1)
                    if n >= 8 and n % 4 == 3:
                        products((n - 8) // 4)
                products(2)
                products(3)

            @block.scalar
            def _(act):
                act.preload_act_table_set("natural_log_exp_and_others")

                def exponent(n):
                    b, f = n // 2, (sqk, sqq)[n % 2]
                    act.wait_ge(s_ln, n + 1)
                    act.activation(f[:, T * b:T * b + T], f[:, T * b:T * b + T], ACT.Exp, scale=-0.5).then_inc(s_rs, 1)

                for n in range(2 * B):
                    b, f = n // 2, (sqk, sqq)[n % 2]
                    act.wait_ge(s_ss, n + 1)
                    act.activation(f[:, T * b:T * b + T], bank[n % 4][:], ACT.Ln, bias=eps_l2).then_inc(s_ln, 1)
                    if n:
                        exponent(n - 1)
                exponent(2 * B - 1)

            @block.gpsimd
            def _(pool):
                for b in range(B):
                    cols = slice(T * b, T * b + T)
                    pool.wait_ge(s_rs, 2 * b + 2)
                    pool.tensor_tensor(sqq[:, cols], qs[:, cols], sqq[:, cols], ALU.mult).then_inc(s_qn, 1)

            @block.vector
            def _(dve):
                def masked(g):
                    tiles = slice(TG * g, TG * g + TG)
                    for h in range(H):
                        dve.wait_ge(s_g, H * g + h + 1)
                        o = bank[4 + h][:].rearrange("p (t k i) -> p t k i", k=2, i=C)
                        dve.tensor_tensor(a_nat[:, tiles, h, :], o[:, :, 0, :], bc(neg_strict, 1, TG), ALU.mult)
                        dve.tensor_tensor(ak[:, tiles, h, 0, :], o[:, :, 1, :], bc(causal, 1, TG), ALU.mult).then_inc(s_ga, 1)

                for b in range(B):
                    cols = slice(T * b, T * b + T)
                    dve.wait_ge(s_rs, 2 * b + 1)
                    dve.tensor_tensor(kn[:, cols], ks[:, cols], sqk[:, cols], ALU.mult).then_inc(s_knorm, 1)
                    dve.wait_ge(s_knorm, b + 1)
                    dve.tensor_tensor(sqk[:, cols], kn[:, cols], bt[:, cols], ALU.mult).then_inc(s_kb, 1)
                    if b == 6:
                        masked(0)
                for g in range(1, NT // TG):
                    masked(g)

            @block.sync
            def _(sp):
                sp.dma_start(h_dram, hT[:]).then_inc(s_hout, 16)
                for g in range(NT // TG):
                    sp.wait_ge(s_ga, H * (g + 1))
                    sp.dma_start(a_dram[TG * g:TG * g + TG].rearrange("t p x -> p t x"),
                                 slab[:, 0, TG * P * g:TG * P * g + TG * P].rearrange("p (t x) -> p t x", x=P)).then_inc(s_adma, 16)
                    sp.wait_ge(s_adma, 16 * (g + 1))
                    sp.dma_start(X[4 * TG * g:4 * TG * (g + 1), :],
                                 a_dram[TG * g:TG * g + TG].rearrange("t (c j) x -> (t c) (j x)", c=4)).then_inc(s_xdma, 16)
                sp.wait_ge(s_xdma, 16 * (NT // TG))
                sp.wait_ge(s_hout, 16)

        X4 = X.rearrange("p (j h i) -> p j h i", h=H, i=C)
        s_xd, s_xp, s_tdma, s_ttdma = sem("s_xd"), sem("s_xp"), sem("s_tdma"), sem("s_ttdma")
        HD = 3
        MAXW = max(m * (C - 1 - m) for m in range(C))
        toep = slab[0:WIN, 4, :].rearrange("p (d i) -> p d i", i=C)
        fo = slab[:, 2, :].rearrange("p (g c) -> p g c", c=NCH)
        win = [hT[0:WIN].rearrange("p b t -> p (b t)").rearrange("p (c d) -> p c d", d=D),
               slab[0:WIN, 9, :].rearrange("p (c d) -> p c d", d=D)]
        WC = 2 * CPB
        s_toep, s_fpe, s_fev, s_wused, s_xpose, s_xevac = (
            sem(x) for x in ("s_toep", "s_fpe", "s_fev", "s_wused", "s_xpose", "s_xevac"))
        s_win = [sem(f"s_win{i}") for i in range(2)]
        copies = [(src, b) for src in ("vb", "kn", "kb") for b in range(B)]

        def invert(engine, s, h0, h1):
            link = chain(engine, s)
            nh = h1 - h0
            tmp = scratch[:, MAXW * h0:MAXW * h1]
            for m in range(1, C - 1):
                w = C - 1 - m
                prod = tmp[:, 0:m * nh * w].rearrange("p (k h i) -> p k h i", h=nh, i=w)
                link(engine.tensor_tensor(prod, bc(X4[:, m, h0:h1, m + 1:], 1, m),
                                          X4[:, 0:m, h0:h1, m:m + 1].broadcast_to([P, m, nh, w]), ALU.mult))
                link(engine.tensor_tensor(X4[:, 0:m, h0:h1, m + 1:], X4[:, 0:m, h0:h1, m + 1:], prod, ALU.add))
            for h in range(h0, h1):
                i = engine.memset(X[:, C * h:C * h + (P + 1) * (C - 1) + 1:P + 1], 1.0)
            return i

        with nc.Block() as block:
            @block.vector
            def _(dve):
                invert(dve, chain_dve, 0, HD).then_inc(s_xd, 1)

            @block.gpsimd
            def _(pool):
                invert(pool, chain_pool, HD, H).then_inc(s_xp, 1)

            @block.tensor
            def _(pe):
                for n, (src, b) in enumerate(copies):
                    if n >= 2:
                        pe.wait_ge(s_xevac, n - 1)
                    rows = {"vb": vb, "kn": kn, "kb": sqk}[src]
                    for t in range(TPB):
                        m = pe.transpose(bank[6 + n % 2][:, P * t:P * t + P], rows[:, T * b + P * t:T * b + P * t + P], ident)
                    m.then_inc(s_xpose, 1)
                pe.wait_ge(s_toep, 16)
                for p in range(B // 2):
                    if p >= 2:
                        pe.wait_ge(s_fev, 2 * (p - 1))
                    pe.wait_ge(s_win[p % 2], 32 * (p // 2 + 1))
                    for k in range(2):
                        for j in range(16 * k, 16 * k + 16):
                            cols = slice(WC * (j % 16), WC * (j % 16) + WC)
                            for h in range(H):
                                m = pe.matmul(bank[2 * (p % 2) + k][DH * h:DH * h + DH, cols], toep[:, DH * h + j, :],
                                              win[p % 2][:, :, DH * h + j], start=True, stop=True)
                        m.then_inc(s_fpe, 1)

            @block.scalar
            def _(act):
                for n, (src, b) in enumerate(copies):
                    act.wait_ge(s_xpose, n + 1)
                    tiles = slice(TPB * b, TPB * b + TPB)
                    dst = {"vb": vk[:, tiles, :, 0, :], "kn": ak[:, tiles, :, 1, :], "kb": vk[:, tiles, :, 1, :]}[src]
                    act.activation(dst, bank[6 + n % 2][:].rearrange("p (t h d) -> p t h d", h=H, d=DH), ACT.Copy).then_inc(s_xevac, 1)
                for p in range(B // 2):
                    for k in range(2):
                        act.wait_ge(s_fpe, 2 * p + k + 1)
                        act.activation(fo[:, 16 * k:16 * k + 16, WC * p:WC * p + WC],
                                       bank[2 * (p % 2) + k][:].rearrange("p (g c) -> p g c", c=WC), ACT.Copy).then_inc(s_fev, 1)

            @block.sync
            def _(sp):
                sp.dma_start(toep, a["toep"]).then_inc(s_toep, 16)
                for p in range(B // 2):
                    if p == 1:
                        sp.wait_ge(s_xpose, B)
                    if p >= 2:
                        sp.wait_ge(s_fpe, 2 * (p - 1))
                    for b in (2 * p, 2 * p + 1):
                        src = bass.AP(v_dram, b * (LONG - 1 + T) * D, [[D, WIN], [C * D, CPB], [1, D]])
                        c0 = CPB * (b % 2)
                        sp.dma_start(win[p % 2][:, c0:c0 + CPB, :], src).then_inc(s_win[p % 2], 16)
                sp.wait_ge(s_xd, 1)
                sp.wait_ge(s_xp, 1)
                sp.dma_start(t_dram.rearrange("t (c j) x -> (t c) (j x)", c=4), X).then_inc(s_tdma, 16)
                sp.wait_ge(s_fpe, B)
                sp.wait_ge(s_tdma, 16)
                sp.dma_start(slab[:, 9, :].rearrange("p (t x) -> p t x", x=P), t_dram.rearrange("t p x -> p t x")).then_inc(s_ttdma, 16)
                sp.wait_ge(s_ttdma, 16)
        if stop == 5:
            return dump(nc, sem, out, slab, [7, 8, 9, 10])

        tt = slab[:, 9, :].rearrange("p (t h i) -> p t h i", h=H, i=C)
        uw = vk
        au = slab[:, 4, :].rearrange("p (c i) -> p c i", i=C)
        N = slab[:, 10, :].rearrange("p (c d) -> p c d", d=DH)
        NG = NT // 2
        ak_spread = [hT[:].rearrange("p b t -> p (b t)")[:, 2048 * k:2048 * k + 2048].rearrange(
            "p (n c x) -> p n c x", c=4, x=C) for k in range(2)]
        u_spread = [scratch[:, 1024 * k:1024 * k + 1024].rearrange("p (n c x) -> p n c x", c=4, x=DH) for k in range(2)]
        s_u, s_uw, s_us, s_akd, s_akp, s_pb, s_ed, s_ea = (
            sem(x) for x in ("s_u", "s_uw", "s_us", "s_akd", "s_akp", "s_pb", "s_ed", "s_ea"))

        def spread(engine, dst, src, n):
            return engine.tensor_tensor(dst, bc(src, 2, 4), bc(bc(quarter, 1, n), 3, C), ALU.mult)

        def spread_ak(engine, g):
            src = ak[:, 2 * g:2 * g + 2, :, :, :].rearrange("p t h k d -> p (t h k) d")
            return spread(engine, ak_spread[g % 2], src, 4 * H)

        with nc.Block() as block:
            @block.tensor
            def _(pe):
                def solve(g):
                    if g >= 2:
                        pe.wait_ge(s_uw, g - 1)
                    for t in range(2 * g, 2 * g + 2):
                        for h in range(H):
                            for c in range(4):
                                q = slice(C * c, C * c + C)
                                col = 2 * DH * (H * (t % 2) + h)
                                m = pe.matmul(bank[g % 2][q, col:col + 2 * DH], tt[q, t, h, :], vk[q, t, h, :, :],
                                              start=True, stop=True)
                    m.then_inc(s_u, 1)

                solve(0)
                for g in range(NG):
                    if g + 1 < NG:
                        solve(g + 1)
                    quad = g // 2
                    pe.wait_ge(s_uw, g + 1)
                    pe.wait_ge(s_us, g + 1)
                    pe.wait_ge(s_akd if g % 2 == 0 else s_akp, g // 2 + 1)
                    if g >= 2:
                        pe.wait_ge(s_ed, g - 1)
                    if quad >= 2:
                        pe.wait_ge(s_ea, quad - 1)
                    for i in range(2):
                        tile = 2 * g + i
                        for h in range(H):
                            q = slice(DH * h, DH * h + DH)
                            n = 2 * (H * i + h)
                            cols = slice(P * (tile % 4), P * (tile % 4) + P)
                            pe.matmul(bank[2 + g % 2][q, 2 * P * i:2 * P * i + 2 * P], uw[:, tile, h, 1, :],
                                      ak_spread[g % 2][:, n:n + 2, :, :], start=True, stop=True)
                            pe.matmul(bank[4 + quad % 2][q, cols], uw[:, tile, h, 0, :], ak_spread[g % 2][:, n, :, :],
                                      start=True, stop=True)
                            m = pe.matmul(bank[6 + quad % 2][q, cols], ak[:, tile, h, 1, :], u_spread[g % 2][:, H * i + h, :, :],
                                          start=True, stop=True)
                    m.then_inc(s_pb, 1)

            @block.scalar
            def _(act):
                def gathered(quad):
                    act.wait_ge(s_pb, 2 * quad + 2)
                    chunks = slice(16 * quad, 16 * quad + 16)
                    act.activation(au[:, chunks, :], bank[4 + quad % 2][:].rearrange("p (c i) -> p c i", i=C), ACT.Copy)
                    act.activation(N[:, chunks, :], bank[6 + quad % 2][:].rearrange("p (c i) -> p c i", i=C), ACT.Copy).then_inc(s_ea, 1)

                for g in range(NG):
                    act.wait_ge(s_u, g + 1)
                    act.activation(uw[:, 2 * g:2 * g + 2].rearrange("p t h k d -> p (t h k d)"), bank[g % 2][:], ACT.Copy).then_inc(s_uw, 1)
                    if g >= 3 and g % 2:
                        gathered((g - 3) // 2)
                gathered(NG // 2 - 1)

            @block.gpsimd
            def _(pool):
                for g in range(1, NG, 2):
                    if g >= 2:
                        pool.wait_ge(s_pb, g - 1)
                    spread_ak(pool, g).then_inc(s_akp, 1)

            @block.vector
            def _(dve):
                def subtract(g):
                    dve.wait_ge(s_pb, g + 1)
                    o = bank[2 + g % 2][:].rearrange("p (t k c i) -> p t k c i", t=2, k=2, i=C)
                    for i in range(2):
                        chunks = slice(4 * (2 * g + i), 4 * (2 * g + i) + 4)
                        dve.tensor_tensor(kbq[:, 1, chunks, :], kbq[:, 1, chunks, :], o[:, i, 0, :, :], ALU.subtract)
                        m = dve.tensor_tensor(kbq[:, 0, chunks, :], bc(eye32, 1, 4), o[:, i, 1, :, :], ALU.subtract)
                    m.then_inc(s_ed, 1)

                spread_ak(dve, 0).then_inc(s_akd, 1)
                for g in range(NG):
                    dve.wait_ge(s_uw, g + 1)
                    if g >= 2:
                        dve.wait_ge(s_pb, g - 1)
                    spread(dve, u_spread[g % 2], uw[:, 2 * g:2 * g + 2, :, 0, :].rearrange("p t h d -> p (t h) d"), 2 * H).then_inc(s_us, 1)
                    if g >= 1:
                        subtract(g - 1)
                        if g % 2 and g + 1 < NG:
                            spread_ak(dve, g + 1).then_inc(s_akd, 1)
                subtract(NG - 1)

        Nb = N.rearrange("p (b c) d -> p b c d", c=CPB)
        fsw = sb("fsw", [P, SHORT])
        NP_ = 4
        short_c, long_c, delta_c, v_c = (slab[:, s, :] for s in (3, 1, 5, 9))
        short_f, tap1, tap0 = (slab[:, s, :] for s in (7, 0, 8))
        sq_short, sq_long, sq_v = slab[:, 8, :], slab[:, 0, :], hT[:].rearrange("p b t -> p (b t)")
        sums = scratch[:, 0:512].rearrange("p (w n) -> p w n", w=NP_)
        sqs = scratch[:, 512:1024].rearrange("p (w n) -> p w n", w=NP_)
        m2 = scratch[:, 1024:1536].rearrange("p (w n) -> p w n", w=NP_)
        s_r, s_s, s_o, s_oe, s_fw, s_vc, s_prod, s_pl, s_cp, s_ce, s_vsq, s_lsq, s_ssq = (
            sem(x) for x in ("s_r", "s_s", "s_o", "s_oe", "s_fw", "s_vc", "s_prod", "s_pl", "s_cp", "s_ce", "s_vsq", "s_lsq", "s_ssq"))
        PIECE = 1024

        def reduce_piece(dve, w, path, squares, i):
            src, dst = (squares, sqs) if i >= 4 else (path, sums)
            part, n = slice(PIECE * (i % 4), PIECE * (i % 4 + 1)), slice(32 * (i % 4), 32 * (i % 4) + 32)
            return dve.tensor_reduce(dst[:, w, n], src[:, part].rearrange("p (n d) -> p n d", d=DH), AX, ALU.add)

        with nc.Block() as block:
            @block.sync
            def _(sp):
                sp.dma_start(fsw[:], a["fsw"]).then_inc(s_fw, 16)
                for b in range(B):
                    sp.dma_start(v_c[CPB * b:CPB * b + CPB, :],
                                 v_dram.ap()[b, LONG - 1:, :].rearrange("(c j) d -> c (j d)", j=C)).then_inc(s_vc, 16)

            @block.tensor
            def _(pe):
                def to_chunks(n):
                    if n >= 2:
                        pe.wait_ge(s_ce, n - 1)
                    for i in range(4):
                        j = 4 * (n % 8) + i
                        src = fo[:, j, :] if n < 8 else short_f[:, j:C * (NCH - 1) + j + 1:C]
                        m = pe.transpose(bank[6 + n % 2][:, P * i:P * i + P], src, ident)
                    m.then_inc(s_cp, 1)

                for c in range(1, CPB - 1):
                    for half in range(2):
                        if c > 1:
                            pe.wait_ge(s_s, 2 * (c - 2) + half + 1)
                        for b in range(4 * half, 4 * half + 4):
                            for h in range(H):
                                q = slice(DH * h, DH * h + DH)
                                m = pe.matmul(bank[half][q, DH * (b % 4):DH * (b % 4) + DH], kbq[q, 0, CPB * b + c, :],
                                              Nb[q, b, c - 1, :], start=True, stop=True)
                        m.then_inc(s_r, 1)
                    if c >= 7:
                        to_chunks(c - 7)
                pe.wait_ge(s_s, 2 * (CPB - 2))
                for b in range(B):
                    if b >= 4:
                        pe.wait_ge(s_oe, b - 3)
                    for c in range(1, CPB):
                        for h in range(H):
                            q = slice(DH * h, DH * h + DH)
                            m = pe.matmul(bank[2 + b % 4][q, C * c:C * c + C], Nb[q, b, c - 1, :], kbq[q, 1, CPB * b + c, :],
                                          start=True, stop=True)
                    m.then_inc(s_o, 1)
                    if b == 0:
                        pe.wait_ge(s_pl, 2)
                    to_chunks(8 + b)

            @block.scalar
            def _(act):
                act.wait_ge(s_fw, 16)
                for tap, dst in enumerate((short_f, tap1, tap0)):
                    act.activation(dst, vT, ACT.Identity, scale=fsw[:, SHORT - 1 - tap:SHORT - tap]).then_inc(s_prod, 1)
                act.wait_ge(s_vc, 16 * B)
                act.activation(sq_v, v_c, ACT.Square).then_inc(s_vsq, 1)
                for n in range(8):
                    act.wait_ge(s_cp, n + 1)
                    o = bank[6 + n % 2][:].rearrange("p (d h i) -> p h i d", h=H, i=C)
                    dst = long_c.rearrange("p (i h d) -> p h i d", h=H, d=DH)[:, :, :, 4 * n:4 * n + 4]
                    for h in range(H):
                        i = act.activation(dst[:, h, :, :], o[:, h, :, :], ACT.Copy)
                    i.then_inc(s_ce, 1)
                act.wait_ge(s_ce, 8)
                act.wait_ge(s_pl, 1)
                act.activation(sq_long, long_c, ACT.Square).then_inc(s_lsq, 1)
                act.wait_ge(s_pl, 2)
                for n in range(8, 16):
                    act.wait_ge(s_cp, n + 1)
                    part = slice(512 * (n - 8), 512 * (n - 8) + 512)
                    act.activation(short_c[:, part], bank[6 + n % 2][:], ACT.Copy)
                    act.activation(sq_short[:, part], bank[6 + n % 2][:], ACT.Square).then_inc(s_ce, 1)

            @block.gpsimd
            def _(pool):
                r, t1_, t0_ = (x.rearrange("p (b t) -> p b t", t=T) for x in (short_f, tap1, tap0))
                pool.wait_ge(s_prod, 2)
                pool.tensor_tensor(r[:, :, 1:], r[:, :, 1:], t1_[:, :, :T - 1], ALU.add).then_inc(s_pl, 1)
                pool.wait_ge(s_prod, 3)
                pool.wait_ge(s_pl, 1)
                pool.tensor_tensor(r[:, :, 2:], r[:, :, 2:], t0_[:, :, :T - 2], ALU.add).then_inc(s_pl, 1)

            @block.vector
            def _(dve):
                for c in range(1, CPB - 1):
                    for half in range(2):
                        dve.wait_ge(s_r, 2 * (c - 1) + half + 1)
                        bs = slice(4 * half, 4 * half + 4)
                        dve.tensor_tensor(Nb[:, bs, c, :], Nb[:, bs, c, :],
                                          bank[half][:, 0:4 * DH].rearrange("p (b d) -> p b d", d=DH), ALU.add).then_inc(s_s, 1)
                    if c >= 7:
                        if c == 7:
                            dve.wait_ge(s_vsq, 1)
                            dve.wait_ge(s_vc, 16 * B)
                        reduce_piece(dve, 3, v_c, sq_v, c - 7)
                for b in range(B):
                    dve.wait_ge(s_o, b + 1)
                    cols = slice(T * b + C, T * b + T)
                    dve.tensor_tensor(slab[:, 4, cols], slab[:, 4, cols], bank[2 + b % 4][:, C:], ALU.add).then_inc(s_oe, 1)
                    if b < 4:
                        if b == 0:
                            dve.wait_ge(s_lsq, 1)
                        for i in (2 * b, 2 * b + 1):
                            reduce_piece(dve, 1, long_c, sq_long, i)
                    else:
                        dve.wait_ge(s_ce, 8 + 2 * (b - 4) + 2)
                        reduce_piece(dve, 0, short_c, sq_short, b - 4)
                        reduce_piece(dve, 0, short_c, sq_short, b)
        if stop == 7:
            return dump(nc, sem, out, slab, [4, 2, 5, 6])

        paths = [short_c, long_c, delta_c, v_c]
        K16 = H * NP_
        st = slab[:, 10, 0:1024].rearrange("p (j w h k) -> p j w h k", w=NP_, h=H, k=2)
        sq_delta = slab[:, 8, :]
        stT = slab[:, 2, 0:1024]
        small = slab[:, 10, 2560:4096]
        w1T, w2T = small[:, 0:HID], small[:, 256:320].rearrange("p (m k) -> p m k", m=2)
        b1 = small[:, 320:322]
        tb = small[:, 322:418].rearrange("p (n k) -> p n k", k=K16)
        fl = small[:, 418:434]
        flt = small[:, 434:450]
        w1s = slab[:, 2, 1024:2048].rearrange("p (i m) -> p i m", i=4)
        s_dp, s_dc, s_sqr, s_red, s_gw, s_st, s_stp, s_sta, s_std, s_tmp, s_tv = (
            sem(x) for x in ("s_dp", "s_dc", "s_sqr", "s_red", "s_gw", "s_st", "s_stp", "s_sta", "s_std", "s_tmp", "s_tv"))
        with nc.Block() as block:
            @block.sync
            def _(sp):
                sp.dma_start(hT[:], h_dram).then_inc(s_hin, 16)
                for dst, name in ((w1T, "w1T"), (w2T, "w2T"), (b1, "b1"), (w1s, "w1s")):
                    sp.dma_start(dst, a[name]).then_inc(s_gw, 16)
                sp.dma_start(tb[:, 0:2, :], a["temp_bias"].partition_broadcast(P)).then_inc(s_gw, 16)
                sp.dma_start(fl, a["floor"].partition_broadcast(P)).then_inc(s_gw, 16)
                sp.wait_ge(s_gw, 96)
                sp.wait_ge(s_hin, 16)

            @block.scalar
            def _(act):
                act.preload_act_table_set("natural_log_exp_and_others")
                link = chain(act, chain_act)
                for g in range(8):
                    act.wait_ge(s_dp, g + 1)
                    part = slice(512 * g, 512 * g + 512)
                    act.activation(delta_c[:, part], bank[g][:], ACT.Copy).then_inc(s_dc, 1)
                    act.activation(sq_delta[:, part], bank[g][:], ACT.Square).then_inc(s_sqr, 1)
                act.wait_ge(s_gw, 96)
                link(act.activation(tb[:, 2, :], tb[:, 0, :], ACT.Abs))
                link(act.activation(tb[:, 3, :], tb[:, 2, :], ACT.Exp, scale=-1.0))
                act.activation(tb[:, 4, :], tb[:, 3, :], ACT.Ln, bias=one1).then_inc(s_tmp, 1)
                act.activation(flt, fl, ACT.Exp, scale=-1.0).then_inc(s_tmp, 1)
                act.wait_ge(s_stp, 1)
                act.activation(stT[:, 0:512], bank[0][:], ACT.Copy).then_inc(s_sta, 1)

            @block.vector
            def _(dve):
                link = chain(dve, chain_dve)
                for i in range(4):
                    dve.wait_ge(s_sqr, 2 * i + 2)
                    dve.wait_ge(s_dc, 2 * i + 2)
                    reduce_piece(dve, 2, delta_c, sq_delta, i).then_inc(s_red, 1)
                    reduce_piece(dve, 2, delta_c, sq_delta, i + 4).then_inc(s_red, 1)
                dve.wait_ge(s_red, 8)
                for w in range(NP_):
                    i = dve.tensor_scalar(st[:, :, w, :, 0], sums[:, w, :].rearrange("p (j h) -> p j h", h=H), 1.0 / DH, None, ALU.mult)
                link(i)
                for w in range(NP_):
                    i = dve.tensor_tensor(m2[:, w, :].rearrange("p (j h) -> p j h", h=H), st[:, :, w, :, 0], st[:, :, w, :, 0], ALU.mult)
                link(i)
                for w in range(NP_):
                    i = dve.scalar_tensor_tensor(st[:, :, w, :, 1], sqs[:, w, :].rearrange("p (j h) -> p j h", h=H), 1.0 / DH,
                                                 m2[:, w, :].rearrange("p (j h) -> p j h", h=H), ALU.mult, ALU.subtract)
                i.then_inc(s_st, 1)
                dve.wait_ge(s_tmp, 2)
                link(dve.tensor_scalar(tb[:, 5, :], tb[:, 0, :], 0.0, 1e-4, ALU.max, ALU.add))
                link(dve.tensor_tensor(tb[:, 2, :], tb[:, 5, :], tb[:, 4, :], ALU.add))
                link(dve.reciprocal(tb[:, 3, :], tb[:, 2, :]))
                link(dve.tensor_scalar(flt, flt, 1.0, None, ALU.add))
                link(dve.reciprocal(fl, flt))
                link(dve.tensor_scalar(fl, fl, 0.05, None, ALU.mult))
                dve.wait_ge(s_stp, 2)
                dve.tensor_copy(stT[:, 512:1024], bank[1][:]).then_inc(s_std, 1)

            @block.tensor
            def _(pe):
                for g in range(8):
                    for i in range(4):
                        j = 4 * g + i
                        m = pe.transpose(bank[g][:, P * i:P * i + P], slab[:, 4, j:C * (NCH - 1) + j + 1:C], ident)
                    m.then_inc(s_dp, 1)
                pe.wait_ge(s_st, 1)
                for k in range(2):
                    for i in range(4):
                        g = 4 * k + i
                        m = pe.transpose(bank[k][:, P * i:P * i + P], slab[:, 10, P * g:P * g + P], ident)
                    m.then_inc(s_stp, 1)

        hm = slab[:, 6:8, 0:2048].rearrange("p n (m t) -> p n m t", m=4)
        lT = slab[:, 8, 1024:2048]
        hc = hT[:].rearrange("p b (c j) -> p (b c) j", j=C)
        probs = slab[:, 7, 2048:2560].rearrange("p (n w) -> p n w", w=NP_)
        s_hm, s_gel, s_lg, s_lt, s_ltt = (sem(x) for x in ("s_hm", "s_gel", "s_lg", "s_lt", "s_ltt"))
        with nc.Block() as block:
            @block.tensor
            def _(pe):
                def logits(g):
                    pe.wait_ge(s_gel, 2 * g + 2)
                    q = slice(C * (g % 4), C * (g % 4) + C)
                    for k in range(2):
                        m = pe.matmul(bank[4 + g // 4][q, :], w2T[:, k, :], hm[:, g % 2, k, :], start=k == 0, stop=k == 1)
                    m.then_inc(s_lg, 1)

                def transposed(G):
                    pe.wait_ge(s_lt, G + 1)
                    for i in range(4):
                        m = pe.transpose(bank[6 + G][:, P * i:P * i + P], lT[:, 512 * G + P * i:512 * G + P * i + P], ident)
                    m.then_inc(s_ltt, 1)

                for g in range(8):
                    for k in range(2):
                        n = 2 * g + k
                        if n >= 4:
                            pe.wait_ge(s_gel, n - 3)
                        o = bank[n % 4]
                        pe.matmul(o[:], w1T[:, P * k:P * k + P], hc[:, :, 4 * g:4 * g + 4].rearrange("p c i -> p i c"),
                                  start=True, stop=False)
                        for i in range(4):
                            m = pe.matmul(o[:, P * i:P * i + P], w1s[:, i, P * k:P * k + P], stT[:, P * g:P * g + P],
                                          start=False, stop=i == 3)
                        m.then_inc(s_hm, 1)
                    if g:
                        logits(g - 1)
                    if g == 6:
                        transposed(0)
                logits(7)
                transposed(1)

            @block.scalar
            def _(act):
                for g in range(8):
                    for k in range(2):
                        n = 2 * g + k
                        act.wait_ge(s_hm, n + 1)
                        if g >= 2:
                            act.wait_ge(s_lg, g - 1)
                        act.activation(hm[:, g % 2, k, :], bank[n % 4][:], ACT.Gelu, bias=b1[:, k:k + 1]).then_inc(s_gel, 1)

            @block.vector
            def _(dve):
                link = chain(dve, chain_dve)
                for G in range(2):
                    dve.wait_ge(s_lg, 4 * G + 4)
                    dve.tensor_copy(lT[:, 512 * G:512 * G + 512], bank[4 + G][:]).then_inc(s_lt, 1)
                logit = slab[:, 8, 0:512].rearrange("p (G q i k) -> p G q i k", G=2, q=4, i=4)
                for G in range(2):
                    dve.wait_ge(s_ltt, G + 1)
                    o = bank[6 + G][:].rearrange("p (i q k) -> p q i k", i=4, q=4)
                    for q in range(4):
                        m = dve.tensor_tensor(logit[:, G, q], o[:, q, :, 0:K16], bc(tb[:, 1, :], 1, 4), ALU.add)
                link(m)
                flat = slab[:, 8, 0:512].rearrange("p (j k) -> p j k", k=K16)
                link(dve.tensor_tensor(flat, flat, bc(tb[:, 3, :], 1, C), ALU.mult))

        w2 = slab[:, 8, 3072:3584].rearrange("p (k d) -> p k d", k=4)
        wmod2 = slab[:, 7, 3584:3968]
        free = hT[:].rearrange("p b t -> p (b t)")
        cols = free[:, 3072:3084]
        vbR = free[:, 3200:3200 + D]
        obR = slab[:, 8, 3584:3584 + T]
        modR = free[:, 0:3 * B * D].rearrange("p (b k d) -> p b k d", b=B, k=3)
        gtmp = scratch[:, 0:B * D].rearrange("p (b d) -> p b d", b=B)
        gtmp2 = scratch[:, B * D:].rearrange("p (b d) -> p b d", b=B)
        identb = sb("identb", [P, P], BF16)
        by_batch = lambda k: slab[:, k, :].rearrange("p (b t) -> p b t", t=T)
        h2o, xnT_all, work = by_batch(1), by_batch(3), by_batch(6)
        fb = slab[:, 4, :].rearrange("p (n t) -> p n t", t=T)
        xnT = fb[:, 0, :]
        qf, kf, att, attT = fb[:, 2, :], fb[:, 3, :], fb[:, 4, :], fb[:, 5, :]
        outbuf = fb[:, 6, :]
        half = lambda k, n: slab[:, k, :].bitcast(BF16)[:, n * 4096:n * 4096 + 4096].rearrange("p (h t) -> p h t", h=FH)
        qstack = [half(5 + k, 0) for k in range(3)]
        kstack = [half(5 + k, 1) for k in range(3)]
        vaug = [slab[:, 8, 1024 * k:1024 * k + 1024].rearrange("p (t h d) -> p t h d", t=TPB, h=FH) for k in range(3)]
        oc = [slab[:, 2, T * k:T * k + T] for k in range(2)]
        pT = slab[:, 9, :].rearrange("p (n t) -> p n t", t=T)
        sp10 = slab[:, 10, :]
        qparts = sp10[:, 0:768].bitcast(BF16).rearrange("p (n t) -> p n t", n=3)
        kparts = sp10[:, 768:1536].bitcast(BF16).rearrange("p (n t) -> p n t", n=3)
        res = sp10[:, 1536:2048]
        kres = slab[:, 2, 2 * T:3 * T]
        mx = sp10[:, 2048:2080]
        mm = sp10[:, 2080:2112].bitcast(BF16)
        mT = sp10[0:2 * 32, 2112:2176].bitcast(BF16)
        rc = sp10[:, 2256:2288].rearrange("p (g t h) -> p g t h", g=2, t=TPB)

        mixT = slab[:, 2, :]
        x1 = slab[:, 0, :].rearrange("p (t d) -> p t d", d=D)
        gt = slab[:, 10, 0:1024].rearrange("p (s n) -> p s n", n=P)
        e = slab[:, 7, 2560:3072].rearrange("p (n w) -> p n w", w=NP_)
        woT = slab[:, 7, 3072:3072 + D]
        onorm = slab[:, 7, 3200:3201]
        wga = slab[:, 7, 3328:3328 + D]
        crep = slab[:, 10, 1024:2048].rearrange("p (b n) -> p b n", b=B)
        gaR = slab[:, 10, 2048:3072].rearrange("p (b n) -> p b n", b=B)
        gab = slab[:, 10, 3072:4096].rearrange("p (b n) -> p b n", b=B)
        stx = slab[:, 10, 3200:3200 + 6 * NT].rearrange("p (t s) -> p t s", s=6)
        s_vp = sem("s_vp")
        s_xagain, s_wo, s_mx, s_ex, s_pr, s_crep, s_ga2, s_wog, s_m1, s_mix, s_ms, s_rr, s_mixn, s_mt, s_mte, s_wp, s_x1 = (
            sem(x) for x in ("s_xagain", "s_wo", "s_mx", "s_ex", "s_pr", "s_crep", "s_ga2", "s_wog", "s_m1", "s_mix", "s_ms", "s_rr",
                             "s_mixn", "s_mt", "s_mte", "s_wp", "s_x1done"))
        s_w2, s_mr2, s_me2 = (sem(x) for x in ("s_w2", "s_mr2", "s_me2"))
        mvx = slab[:, 10, 3072:3072 + 2 * NT].rearrange("p (t s) -> p t s", s=2)
        JQ = 4
        with nc.Block() as block:
            @block.sync
            def _(sp):
                sp.dma_start(woT, a["woT"]).then_inc(s_wo, 16)
                sp.dma_start(onorm, a["onorm"]).then_inc(s_wo, 16)
                sp.dma_start(wga, a["wga"]).then_inc(s_wo, 16)
                sp.dma_start(wmod2, a["wmod2"]).then_inc(s_wo, 16)
                sp.dma_start(x1, a["x"].rearrange("t p d -> p t d")).then_inc(s_xagain, 16)
                sp.dma_start(w2, a["w2"]).then_inc(s_w2, 16)
                sp.dma_start(cols, a["cols"]).then_inc(s_w2, 16)
                sp.dma_start(vbR, a["v_b"].partition_broadcast(P)).then_inc(s_w2, 16)
                sp.dma_start(obR, a["obR"].partition_broadcast(P)).then_inc(s_w2, 16)
                sp.wait_ge(s_w2, 64)

            @block.tensor
            def _(pe):
                pe.wait_ge(s_crep, 1)
                pe.wait_ge(s_wo, 64)
                for b in range(B):
                    m = pe.matmul(bank[4 + b // 4][:, P * (b % 4):P * (b % 4) + P], crep[:, b, :], wga, start=True, stop=True)
                m.then_inc(s_ga2, 1)
                for b in range(B):
                    if b >= 2:
                        pe.wait_ge(s_me2, b - 1)
                    pe.matmul(bank[6 + b % 2][:, 0:3 * D], crep[:, b, :], wmod2, start=True, stop=True).then_inc(s_mr2, 1)
                for q in range(JQ):
                    pe.wait_ge(s_mixn, q + 1)
                    for g in range(2):
                        n = 2 * q + g
                        if n >= 4:
                            pe.wait_ge(s_mte, n - 3)
                        for i in range(4):
                            j = 4 * n + i
                            m = pe.transpose(bank[n % 4][:, P * i:P * i + P], slab[:, 4, P * j:P * j + P], ident)
                        m.then_inc(s_mt, 1)
                pe.wait_ge(s_mte, 8)
                pe.wait_ge(s_wog, B)
                for b in range(B):
                    if b >= 4:
                        pe.wait_ge(s_x1, b - 3)
                    for t in range(TPB):
                        m = pe.matmul(bank[b % 4][:, P * t:P * t + P], mixT[:, T * b + P * t:T * b + P * t + P], gaR[:, b, :],
                                      start=True, stop=True)
                    m.then_inc(s_wp, 1)

            @block.scalar
            def _(act):
                act.preload_act_table_set("natural_log_exp_and_others")
                act.wait_ge(s_mx, 1)
                act.activation(e, e, ACT.Exp).then_inc(s_ex, 1)
                for b in range(B):
                    act.wait_ge(s_mr2, b + 1)
                    o = bank[6 + b % 2][:, 0:3 * D].rearrange("p (k d) -> p k d", k=3)
                    act.activation(modR[:, b, 0, :], o[:, 0, :], ACT.Copy)
                    act.activation(modR[:, b, 1, :], o[:, 1, :], ACT.Identity, bias=one1)
                    act.activation(gtmp[:, b, :], o[:, 2, :], ACT.Copy).then_inc(s_me2, 1)
                link = chain(act, chain_act)
                for q in range(JQ):
                    part = slice(1024 * q, 1024 * q + 1024)
                    act.wait_ge(s_mix, q + 1)
                    act.activation(slab[:, 6, part], slab[:, 4, part], ACT.Square).then_inc(s_m1, 1)
                    act.wait_ge(s_ms, q + 1)
                    n = slice(32 * q, 32 * q + 32)
                    link(act.activation(gt[:, 5, n], gt[:, 4, n], ACT.Ln, bias=eps_ln, scale=1.0 / DH))
                    act.activation(gt[:, 6, n], gt[:, 5, n], ACT.Exp, scale=-0.5).then_inc(s_rr, 1)
                for n in range(8):
                    act.wait_ge(s_mt, n + 1)
                    dst = mixT.rearrange("p (c j) -> p c j", j=C)[:, :, 4 * n:4 * n + 4]
                    act.activation(dst, bank[n % 4][:].rearrange("p (j c) -> p c j", j=4), ACT.Copy).then_inc(s_mte, 1)

            @block.gpsimd
            def _(pool):
                pool.tensor_copy(crep, bc(cT[:], 2, P)).then_inc(s_crep, 1)
                pool.wait_ge(s_pr, 1)
                for q in range(JQ):
                    link = chain(pool, chain_pool)
                    part, n = slice(1024 * q, 1024 * q + 1024), slice(32 * q, 32 * q + 32)
                    v3 = lambda t: t[:, part].rearrange("p (n d) -> p n d", d=DH)
                    pool.tensor_tensor(v3(delta_c), v3(delta_c), bc(probs[:, n, 2], 2, DH), ALU.mult).then_inc(s_vp, 1)
                    pool.tensor_tensor(v3(v_c), v3(v_c), bc(probs[:, n, 3], 2, DH), ALU.mult).then_inc(s_vp, 1)
                pool.tensor_copy(identb[:], ident)
                for k in (1, 2):
                    pool.memset(vaug[k][:, :, :, FD:FD + 1], 1.0)
                    pool.memset(vaug[k][:, :, :, FD + 1:], 0.0)

            @block.vector
            def _(dve):
                link = chain(dve, chain_dve)
                logit = slab[:, 8, 0:512].rearrange("p (n w) -> p n w", w=NP_)
                link(dve.tensor_reduce(gt[:, 0, :], logit, AX, ALU.max))
                dve.tensor_tensor(e, logit, bc(gt[:, 0, :], 2, NP_), ALU.subtract).then_inc(s_mx, 1)
                dve.wait_ge(s_ex, 1)
                link(dve.tensor_reduce(gt[:, 1, :], e, AX, ALU.add))
                link(dve.reciprocal(gt[:, 2, :], gt[:, 1, :]))
                link(dve.tensor_tensor(e, e, bc(gt[:, 2, :], 2, NP_), ALU.mult))
                link(dve.tensor_tensor(e.rearrange("p (j h) w -> p j (h w)", h=H), e.rearrange("p (j h) w -> p j (h w)", h=H),
                                       bc(fl, 1, C), ALU.max))
                link(dve.tensor_reduce(gt[:, 1, :], e, AX, ALU.add))
                link(dve.reciprocal(gt[:, 2, :], gt[:, 1, :]))
                dve.tensor_tensor(probs, e, bc(gt[:, 2, :], 2, NP_), ALU.mult).then_inc(s_pr, 1)
                dve.wait_ge(s_pr, 1)
                mixed = slab[:, 4, :]

                def normalise(q):
                    part, n = slice(1024 * q, 1024 * q + 1024), slice(32 * q, 32 * q + 32)
                    v3 = lambda t: t[:, part].rearrange("p (n d) -> p n d", d=DH)
                    dve.wait_ge(s_rr, q + 1)
                    dve.tensor_tensor(v3(mixed), v3(mixed), bc(gt[:, 6, n], 2, DH), ALU.mult).then_inc(s_mixn, 1)

                def square_sums(q):
                    part, n = slice(1024 * q, 1024 * q + 1024), slice(32 * q, 32 * q + 32)
                    dve.wait_ge(s_m1, q + 1)
                    dve.tensor_reduce(gt[:, 4, n], slab[:, 6, part].rearrange("p (n d) -> p n d", d=DH), AX, ALU.add).then_inc(s_ms, 1)

                for q in range(JQ):
                    part, n = slice(1024 * q, 1024 * q + 1024), slice(32 * q, 32 * q + 32)
                    v3 = lambda t: t[:, part].rearrange("p (n d) -> p n d", d=DH)
                    dve.tensor_tensor(v3(mixed), v3(short_c), bc(probs[:, n, 0], 2, DH), ALU.mult)
                    link(dve.tensor_tensor(v3(long_c), v3(long_c), bc(probs[:, n, 1], 2, DH), ALU.mult))
                    link(dve.tensor_tensor(mixed[:, part], mixed[:, part], long_c[:, part], ALU.add))
                    if q:
                        square_sums(q - 1)
                    dve.wait_ge(s_vp, 2 * q + 1)
                    link(dve.tensor_tensor(mixed[:, part], mixed[:, part], delta_c[:, part], ALU.add))
                    if q:
                        normalise(q - 1)
                    dve.wait_ge(s_vp, 2 * q + 2)
                    dve.tensor_tensor(mixed[:, part], mixed[:, part], v_c[:, part], ALU.add).then_inc(s_mix, 1)
                square_sums(JQ - 1)
                normalise(JQ - 1)
                dve.wait_ge(s_ga2, 1)
                for k in range(2):
                    half = slice(4 * k, 4 * k + 4)
                    o = bank[4 + k][:].rearrange("p (b n) -> p b n", b=4)
                    i = dve.tensor_copy(gab[:, half, :], o)
                link(i)
                gate_sign(dve, link, gaR, gab, gab)
                link(dve.tensor_scalar(woT, woT, onorm, None, ALU.mult))
                for b in range(B):
                    dve.tensor_tensor(gaR[:, b, :], gaR[:, b, :], woT, ALU.mult).then_inc(s_wog, 1)
                dve.wait_ge(s_me2, B)
                gate_sign(dve, link, modR[:, :, 2, :], gtmp, gtmp2)

                def aggregate(b):
                    dve.wait_ge(s_x1, b + 1)
                    for t in range(TPB * b, TPB * b + TPB):
                        i = dve.bn_aggr(mvx[:, t, :], stx[:, t, :])
                    return i

                dve.wait_ge(s_xagain, 16)
                for b in range(B):
                    dve.wait_ge(s_wp, b + 1)
                    tiles = slice(TPB * b, TPB * b + TPB)
                    link(dve.tensor_tensor(x1[:, tiles, :], x1[:, tiles, :], bank[b % 4][:].rearrange("p (t d) -> p t d", d=D),
                                           ALU.add))
                    for t in range(TPB * b, TPB * b + TPB):
                        i = dve.bn_stats(stx[:, t, :], x1[:, t, :])
                    i.then_inc(s_x1, 1)
                    if b:
                        aggregate(b - 1)
                link(aggregate(B - 1))
        if stop == 11:
            return dump(nc, sem, out, slab, [0, 5, 1, 7])

        s10 = lambda c, n: slab[:, 10, c:c + n]
        lnx, rx, nmr = s10(3136, NT), s10(3168, NT), s10(3520, NT)
        mv2, ln2, r2 = s10(3392, 2 * NT).rearrange("p (t s) -> p t s", s=2), s10(3456, NT), s10(3488, NT)
        s_lnx, s_rx, s_nmr, s_xh2, s_mod2, s_h2, s_h2o, s_v2, s_ln2, s_r2, s_xn2, s_xt2, s_xe2 = (
            sem(x) for x in ("s_lnx", "s_rx", "s_nmr", "s_xh2", "s_mod2", "s_h2", "s_h2o", "s_v2", "s_ln2", "s_r2", "s_xn2", "s_xt2", "s_xe2"))
        scale = float(D) ** -0.5
        v3 = lambda t: t.rearrange("p (t d) -> p t d", d=D)
        with nc.Block() as block:
            @block.scalar
            def _(act):
                act.preload_act_table_set("natural_log_exp_and_others")
                act.activation(lnx, mvx[:, :, 1], ACT.Ln, bias=eps_ln).then_inc(s_lnx, 1)
                act.wait_ge(s_lnx, 1)
                act.activation(rx, lnx, ACT.Exp, scale=-0.5).then_inc(s_rx, 1)
                act.wait_ge(s_nmr, 1)

                def rstd(b):
                    tiles = slice(TPB * b, TPB * b + TPB)
                    act.wait_ge(s_v2, b + 1)
                    act.activation(ln2[:, tiles], mv2[:, tiles, 1], ACT.Ln, bias=eps_ln).then_inc(s_ln2, 1)
                    act.wait_ge(s_ln2, b + 1)
                    act.activation(r2[:, tiles], ln2[:, tiles], ACT.Exp, scale=-0.5).then_inc(s_r2, 1)

                def operand(half):
                    act.wait_ge(s_xt2, 4 * half + 4)
                    for t in range(TPB):
                        act.activation(xnT_all[:, 4 * half:4 * half + 4, P * t:P * t + P],
                                       bank[t + 4 * half][:].rearrange("p (b i) -> p b i", b=4), ACT.Identity,
                                       bias=cols[:, 8 + t:9 + t], scale=cols[:, 4 + t:5 + t]).then_inc(s_xe2, 1)

                for b in range(B):
                    for t in range(TPB * b, TPB * b + TPB):
                        i = act.activation(work[:, b, P * (t % 4):P * (t % 4) + P], x1[:, t, :], ACT.Identity,
                                           bias=nmr[:, t:t + 1], scale=rx[:, t:t + 1])
                    i.then_inc(s_xh2, 1)
                    if b >= 3:
                        rstd(b - 3)
                for b in range(B - 3, B):
                    rstd(b)
                    if b == B - 3:
                        operand(0)
                operand(1)

            @block.gpsimd
            def _(pool):
                link = chain(pool, chain_pool)
                for b in range(B):
                    pool.wait_ge(s_mod2, b + 1)
                    pool.tensor_tensor(v3(work[:, b, :]), v3(work[:, b, :]), bc(modR[:, b, 0, :], 1, TPB), ALU.add).then_inc(s_h2, 1)
                    pool.wait_ge(s_h2, b + 1)
                    pool.tensor_tensor(h2o[:, b, :], work[:, b, :], obR, ALU.add).then_inc(s_h2o, 1)
                link(pool.memset(mx, 0.0))
                pool.memset(vaug[0][:, :, :, FD:FD + 1], 1.0)
                pool.memset(vaug[0][:, :, :, FD + 1:], 0.0).then_inc(s_me2, 1)
                pool.wait_ge(s_me2, B + 1)

            @block.tensor
            def _(pe):
                for b in range(B):
                    pe.wait_ge(s_xn2, b + 1)
                    for t in range(TPB):
                        m = pe.transpose(bank[t + 4 * (b // 4)][:, P * (b % 4):P * (b % 4) + P], work[:, b, P * t:P * t + P], ident)
                    m.then_inc(s_xt2, 1)

            @block.vector
            def _(dve):
                link = chain(dve, chain_dve)
                dve.wait_ge(s_rx, 1)
                dve.scalar_tensor_tensor(nmr, mvx[:, :, 0], -1.0, rx, ALU.mult, ALU.mult).then_inc(s_nmr, 1)

                def statistics(b):
                    dve.wait_ge(s_h2, b + 1)
                    for t in range(TPB):
                        i = dve.bn_stats(stx[:, TPB * b + t, :], work[:, b, P * t:P * t + P])
                    link(i)
                    for t in range(TPB * b, TPB * b + TPB):
                        i = dve.bn_aggr(mv2[:, t, :], stx[:, t, :])
                    i.then_inc(s_v2, 1)

                def normed(b):
                    dve.wait_ge(s_r2, b + 1)
                    dve.wait_ge(s_h2o, b + 1)
                    for t in range(TPB * b, TPB * b + TPB):
                        w_ = work[:, b, P * (t % 4):P * (t % 4) + P]
                        i = dve.tensor_scalar(w_, w_, mv2[:, t, 0:1], r2[:, t:t + 1], ALU.subtract, ALU.mult)
                    i.then_inc(s_xn2, 1)

                for b in range(B + 3):
                    if b < B:
                        dve.wait_ge(s_xh2, b + 1)
                        dve.tensor_tensor(v3(work[:, b, :]), v3(work[:, b, :]), bc(modR[:, b, 1, :], 1, TPB), ALU.mult).then_inc(s_mod2, 1)
                    if 1 <= b <= B:
                        statistics(b - 1)
                    if b >= 3:
                        normed(b - 3)
                    if b == 2:
                        dve.memset(att, 0.0)
                        dve.memset(oc[0], 1.0)
                    if b == B:
                        dve.memset(kstack[0][96:98, :, :], 1.0)
                link(dve.tensor_scalar(cols[:, 2:3], cols[:, 0:1], scale, None, ALU.mult))

        QT = [sum(FD * h < D >> t for t in range(TPB)) for h in range(FH)]
        wanted = [(h, t) for h in range(FH) for t in range(QT[h])]
        NW = len(wanted)
        TAIL = 2
        STEPS = 1 + TPB
        share = lambda i: ((NW - TAIL) * i // (2 * STEPS), (NW - TAIL) * (i + 1) // (2 * STEPS))
        QP = (0, 0, 1, 1, 0, 2)
        KP = (0, 1, 0, 1, 2, 0)
        part_dram = nc.dram_tensor("qk_parts", (2, FH, FD, 3, T), BF16, kind="Internal").ap()
        m_dram = nc.dram_tensor("neg_max", (64, P), BF16, kind="Internal").ap()
        names = ("f_xnT f_q f_qf f_k f_kf f_v f_V f_qsplit f_ksplit f_spq f_spk f_stack "
                 "f_s1 f_max f_mm f_mT f_mr f_mw f_mq f_sT f_exp f_pv f_oc f_oT f_rc f_at f_aT f_attT f_op f_y "
                 "f_out f_store f_ob f_rcy f_mh f_kl").split()
        s = {n: sem(n) for n in names}

        def split(engine, src, parts, res, ready, written, links, per_batch, first, a_, fresh, round_, done):
            def link(i, n):
                i.then_inc(s[links], 1)
                engine.wait_ge(s[links], per_batch * a_ + n)
            engine.wait_ge(s[ready], a_ + 1)
            if not fresh:
                engine.wait_ge(s[written], 16 * a_)
            link(round_(parts[:, 0, :], src), first)
            link(engine.tensor_tensor(res, src, parts[:, 0, :], ALU.subtract), first + 1)
            link(round_(parts[:, 1, :], res), first + 2)
            link(engine.tensor_tensor(res, res, parts[:, 1, :], ALU.subtract), first + 3)
            round_(parts[:, 2, :], res).then_inc(s[done], 1)

        def attention(engine, stage):
            for k in (-2, -1):
                stage(k, k % 3, k + 2 < B, k + 1 >= 0, k >= 0)
            with engine.Fori(0, 2) as trip:
                for r in range(3):
                    stage(trip * 3 + r, r, True, True, True)
            for k in (6, 7):
                stage(k, k % 3, False, k + 1 < B, True)

        with nc.Block() as block:
            @block.sync
            def _(sp):
                def stage(k, r, do_a, do_m, do_b):
                    if do_a:
                        b, rb = k + 2, (r + 2) % 3
                        for n, (parts, split, written) in enumerate(((qparts, "f_qsplit", "f_spq"), (kparts, "f_ksplit", "f_spk"))):
                            sp.wait_ge(s[split], b + 1)
                            sp.dma_start(part_dram[n].rearrange("h d n t -> (h d) n t"), parts).then_inc(s[written], 16)
                        for n, (stack, which, written) in enumerate(((qstack[rb], QP, "f_spq"), (kstack[rb], KP, "f_spk"))):
                            sp.wait_ge(s[written], 16 * b + 16)
                            for g in range(6):
                                sp.dma_start(stack[FD * g:FD * g + FD, :, :],
                                             part_dram[n, :, :, which[g], :].rearrange("h d t -> d h t")).then_inc(s["f_stack"], 16)
                    if do_m:
                        b, rb = k + 1, (r + 1) % 3
                        sp.wait_ge(s["f_mr"], b + 1)
                        sp.dma_start(m_dram, mT).then_inc(s["f_mw"], 16)
                        sp.wait_ge(s["f_mw"], 16 * b + 16)
                        sp.dma_start(qstack[rb][96:98, :, :], m_dram.rearrange("(n h t) q -> n h (t q)", n=2, h=FH)).then_inc(s["f_mq"], 16)
                    if do_b:
                        b = k
                        sp.wait_ge(s["f_out"], b + 1)
                        if isinstance(b, int):
                            dst, src = out[TPB * b:TPB * b + TPB], x1[:, TPB * b:TPB * b + TPB, :]
                        else:
                            dst, src = out[bass.ds(b * TPB, TPB)], x1[:, bass.ds(b * TPB, TPB), :]
                        sp.dma_start(dst.rearrange("t p d -> p t d"), src).then_inc(s["f_store"], 16)
                attention(sp, stage)
                sp.wait_ge(s["f_store"], 16 * B)

            @block.tensor
            def _(pe):
                misc, obank = bank[7], bank[6]

                def stage(k, r, do_a, do_m, do_b):
                    a_, m_, b_ = k + 2, k + 1, k
                    ra, rm, rb = (r + 2) % 3, (r + 1) % 3, r
                    pa = {}

                    def pass1(n0, n1):
                        for n in range(n0, n1):
                            h, t = wanted[n]
                            if n == 0:
                                pe.wait_ge(s["f_stack"], 192 * m_ + 192)
                            if not (n < 2 and isinstance(k, int) and k == -1):
                                pe.wait_ge(s["f_max"], NW * m_ + n - 1)
                            pe.matmul(bank[n % 2][:], qstack[rm][0:96, h, P * t:P * t + P], kstack[rm][0:96, h, :],
                                      start=True, stop=True).then_inc(s["f_s1"], 1)

                    def scoresT(u, pr):
                        n = 2 * u + pr
                        if n == 0:
                            pe.wait_ge(s["f_mq"], 16 * b_ + 16)
                        if n >= 2:
                            pe.wait_ge(s["f_exp"], 2 * STEPS * b_ + n - 1)
                        if u == 0:
                            todo = [(bank[2 + kt], P * (h - 4), h, kt) for kt in (2 * pr, 2 * pr + 1) for h in range(4, FH)]
                        elif pr == 0:
                            todo = [(bank[2], 0, 0, u - 1), (bank[3], 0, 1, u - 1)]
                        else:
                            todo = [(bank[4], 0, 2, u - 1), (bank[4], P * QT[2], 3, u - 1)]
                        for o, col, h, kt in todo:
                            m = pe.matmul(o[:, col:col + P * QT[h]], kstack[rb][0:98, h, P * kt:P * kt + P],
                                          qstack[rb][0:98, h, 0:P * QT[h]], start=True, stop=True)
                        m.then_inc(s["f_sT"], 1)

                    def pv(u):
                        if u == 0:
                            pe.wait_ge(s["f_V"], b_ + 1)
                        if u == 1:
                            pe.wait_ge(s["f_oc"], 2 * b_ + 1)
                        pe.wait_ge(s["f_exp"], 2 * STEPS * b_ + 2 * u + 2)
                        p_ = pT[:, 4 * (u % 2):4 * (u % 2) + 4, :].rearrange("p n t -> p (n t)")
                        if u == 0:
                            for kt in range(TPB):
                                for i in range(4):
                                    m = pe.matmul(obank[32 * i:32 * i + 32, 0:P], vaug[rb][:, kt, 4 + i, :],
                                                  p_[:, T * kt + P * i:T * kt + P * i + P], start=kt == 0, stop=kt == 3)
                        else:
                            for i, col in enumerate((0, T, 2 * T, 2 * T + P * QT[2])):
                                n = P * QT[i]
                                m = pe.matmul(obank[32 * i:32 * i + 32, 0:n], vaug[rb][:, u - 1, i, :], p_[:, col:col + n],
                                              start=u == 1, stop=u == STEPS - 1)
                        m.then_inc(s["f_pv"], 1)

                    def otrans(g):
                        pe.wait_ge(s["f_oc"], 2 * b_ + 2 - g)
                        for t in range(1 if g else TPB):
                            m = pe.transpose(bank[5][:, P * t:P * t + P], oc[g][:, P * t:P * t + P], ident)
                        m.then_inc(s["f_oT"], 1)

                    def proj(kind):
                        if kind == 0:
                            pe.wait_ge(s["f_xnT"], a_ + 1)
                            pe.matmul(misc[:], w2[:, 0, :], xnT, start=True, stop=True).then_inc(s["f_q"], 1)
                        elif kind == 1:
                            pe.wait_ge(s["f_qf"], a_ + 1)
                            pe.matmul(misc[:], w2[:, 1, :], xnT, start=True, stop=True).then_inc(s["f_k"], 1)
                        else:
                            pe.wait_ge(s["f_kf"], a_ + 1)
                            for t in range(TPB):
                                m = pe.matmul(misc[:, P * t:P * t + P], xnT[:, P * t:P * t + P], w2[:, 2, :], start=True, stop=True)
                            m.then_inc(s["f_v"], 1)

                    def atrans():
                        pe.wait_ge(s["f_at"], 2 * b_ + 2)
                        for t in range(TPB):
                            m = pe.transpose(misc[:, P * t:P * t + P], att[:, P * t:P * t + P], ident)
                        m.then_inc(s["f_aT"], 1)

                    def oproj():
                        pe.wait_ge(s["f_attT"], b_ + 1)
                        for t in range(TPB):
                            w = D >> t
                            m = pe.matmul(misc[:, P * t:P * t + w], attT[0:w, P * t:P * t + P], w2[0:w, 3, 0:w], start=True, stop=True)
                        m.then_inc(s["f_op"], 1)

                    for u in range(STEPS):
                        for pr in range(2):
                            if do_m:
                                pass1(*share(2 * u + pr))
                            if do_b:
                                scoresT(u, pr)
                        if do_b and u:
                            pv(u - 1)
                        if do_b and u == 2:
                            otrans(1)
                        if do_a and 1 <= u <= 3:
                            proj(u - 1)
                    if do_b:
                        pv(STEPS - 1)
                        pe.wait_ge(s["f_at"], 2 * b_ + 1)
                        otrans(0)
                    if do_m:
                        pass1(NW - TAIL, NW)
                    if do_a:
                        pe.wait_ge(s["f_V"], a_ + 1)
                    if do_b:
                        atrans()
                    if do_m:
                        pe.wait_ge(s["f_mm"], m_ + 1)
                        pe.transpose(obank[0:32, 0:64].bitcast(BF16), mm[:, 0:32], identb[:])
                        pe.transpose(obank[32:64, 0:64].bitcast(BF16), mm[:, 32:64], identb[:]).then_inc(s["f_mT"], 1)
                    if do_b:
                        oproj()
                    if do_m:
                        pe.wait_ge(s["f_mr"], m_ + 1)
                    if do_b:
                        pe.wait_ge(s["f_rcy"], b_ + 1)
                attention(pe, stage)

            @block.scalar
            def _(act):
                misc, obank = bank[7], bank[6]

                def stage(k, r, do_a, do_m, do_b):
                    a_, m_, b_ = k + 2, k + 1, k
                    static = isinstance(k, int)

                    def exps(u):
                        for pr in range(2):
                            n = 2 * u + pr
                            act.wait_ge(s["f_sT"], 2 * STEPS * b_ + n + 1)
                            if u >= 2:
                                act.wait_ge(s["f_pv"], STEPS * b_ + u - 1)
                            w = 2 * T if u == 0 else (T + P * QT[1], 2 * P * QT[2])[pr]
                            src = wide[pr].rearrange("p n t -> p (n t)")[:, 0:w]
                            dst = pT[:, 4 * (u % 2) + 2 * pr:4 * (u % 2) + 2 * pr + 2, :].rearrange("p n t -> p (n t)")[:, 0:w]
                            act.activation(dst, src, ACT.Exp).then_inc(s["f_exp"], 1)

                    def operand():
                        if not (static and k == -2):
                            act.wait_ge(s["f_v"], a_)
                        src = xnT_all[:, a_, :] if static else xnT_all[:, bass.ds(a_, 1), :].rearrange("p o t -> p (o t)")
                        act.activation(xnT, src, ACT.Copy).then_inc(s["f_xnT"], 1)

                    def qkevac(kind):
                        if kind == 0:
                            act.wait_ge(s["f_q"], a_ + 1)
                            if not (static and k == -2):
                                act.wait_ge(s["f_qsplit"], a_)
                            act.activation(qf, misc[:], ACT.Identity, bias=cols[:, 2:3], scale=scale).then_inc(s["f_qf"], 1)
                        else:
                            act.wait_ge(s["f_k"], a_ + 1)
                            if not (static and k == -2):
                                act.wait_ge(s["f_ksplit"], a_)
                            act.activation(kf, misc[:], ACT.Identity, bias=cols[:, 1:2]).then_inc(s["f_kf"], 1)

                    def ocevac(g):
                        act.wait_ge(s["f_pv"], STEPS * b_ + (1 if g else STEPS))
                        if g:
                            i = act.activation(oc[1][:, 0:P], obank[:, 0:P], ACT.Copy)
                        else:
                            for rows, c0, c1 in ((P, 0, 2 * P), (64, 2 * P, 3 * P), (32, 3 * P, 4 * P)):
                                i = act.activation(oc[0][0:rows, c0:c1], obank[0:rows, c0:c1], ACT.Copy)
                        i.then_inc(s["f_oc"], 1)

                    for u in range(STEPS):
                        if do_b:
                            exps(u)
                            if u == 1:
                                ocevac(1)
                        if do_a and u == 0:
                            operand()
                        if do_a and u in (1, 2):
                            qkevac(u - 1)
                    if do_b:
                        ocevac(0)
                        act.wait_ge(s["f_aT"], b_ + 1)
                        act.activation(attT, misc[:], ACT.Copy).then_inc(s["f_attT"], 1)
                    if do_m:
                        act.wait_ge(s["f_mT"], m_ + 1)
                        if not (static and k == -1):
                            act.wait_ge(s["f_mw"], 16 * m_)
                        act.activation(mT, obank[0:64, 0:64].bitcast(BF16), ACT.Copy).then_inc(s["f_mr"], 1)
                attention(act, stage)

            @block.gpsimd
            def _(pool):
                def stage(k, r, do_a, do_m, do_b):
                    a_, b_ = k + 2, k
                    static = isinstance(k, int)
                    round_ = lambda dst, src: pool.tensor_tensor(dst, src, one1.broadcast_to([P, T]), ALU.mult)
                    if do_a:
                        split(pool, qf, qparts, res, "f_qf", "f_spq", "f_ob", 4, 1, a_, static and k == -2, round_, "f_qsplit")
                    if static and k == -1:
                        pool.wait_ge(s["f_qsplit"], a_ + 1)
                        links = chain(pool, chain_pool)
                        for n in (1, 2):
                            links(pool.memset(kstack[n][96:98, :, :], 1.0))
                attention(pool, stage)

            @block.vector
            def _(dve):
                misc = bank[7]

                def batch(t, b):
                    if isinstance(b, int):
                        return t[:, TPB * b:TPB * b + TPB, :]
                    return t[:, bass.ds(b * TPB, TPB), :]

                def gb(b):
                    if isinstance(b, int):
                        return modR[:, b, 2, :]
                    return modR[:, bass.ds(b, 1), 2, :].rearrange("p o d -> p (o d)")

                def stage(k, r, do_a, do_m, do_b):
                    a_, m_, b_ = k + 2, k + 1, k
                    static = isinstance(k, int)

                    def maxima(n0, n1):
                        for n in range(n0, n1):
                            dve.wait_ge(s["f_s1"], NW * m_ + n + 1)
                            h, t = wanted[n]
                            dve.tensor_reduce(mx[:, TPB * h + t:TPB * h + t + 1], bank[n % 2][:], AX, ALU.max).then_inc(s["f_max"], 1)

                    def onorm_(g):
                        tiles = 1 if g else TPB
                        dve.wait_ge(s["f_oT"], 2 * b_ + 2 - g)
                        o = bank[5][:].rearrange("p (t h d) -> p t h d", t=TPB, h=4)[:, 0:tiles]
                        dve.reciprocal(rc[:, g, 0:tiles, :], o[:, :, :, FD]).then_inc(s["f_rc"], 1)
                        dve.wait_ge(s["f_rc"], 2 * b_ + 2 - g)
                        dst = att.rearrange("p (t h d) -> p t h d", t=TPB, h=FH)[:, :, 4 * g:4 * g + 4, :]
                        for t in range(tiles):
                            i = dve.tensor_tensor(dst[:, t], o[:, t, :, 0:FD], bc(rc[:, g, t, :], 2, FD), ALU.mult)
                        i.then_inc(s["f_at"], 1)

                    def final():
                        dve.wait_ge(s["f_op"], b_ + 1)
                        h = h2o[:, b_, :] if static else h2o[:, bass.ds(b_, 1), :].rearrange("p o t -> p (o t)")
                        for t in range(TPB):
                            w = D >> t
                            i = dve.tensor_tensor(h[:, P * t:P * t + w], h[:, P * t:P * t + w], misc[:, P * t:P * t + w], ALU.add)
                        i.then_inc(s["f_rcy"], 1)
                        dve.wait_ge(s["f_rcy"], b_ + 1)
                        dve.tensor_tensor(v3(outbuf), v3(h), bc(gb(b_), 1, TPB), ALU.mult).then_inc(s["f_y"], 1)
                        dve.wait_ge(s["f_y"], b_ + 1)
                        dve.tensor_tensor(batch(x1, b_), v3(outbuf), batch(x1, b_), ALU.add).then_inc(s["f_out"], 1)

                    for u in range(STEPS):
                        first, last = share(2 * u)[0], share(2 * u + 1)[1]
                        if do_m:
                            maxima(first, last)
                        if do_b and u == 2:
                            onorm_(1)
                        if do_a and u == 3:
                            split(dve, kf, kparts, kres, "f_kf", "f_spk", "f_kl", 4, 1, a_, static and k == -2, dve.tensor_copy, "f_ksplit")
                        if do_a and u == 4:
                            dve.wait_ge(s["f_v"], a_ + 1)
                            dst = vaug[(r + 2) % 3][:, :, :, 0:FD]
                            dve.tensor_tensor(dst, misc[:].rearrange("p (t h d) -> p t h d", t=TPB, h=FH),
                                              bc(vbR.rearrange("p (h d) -> p h d", h=FH), 1, TPB), ALU.add).then_inc(s["f_V"], 1)
                    if do_b:
                        onorm_(0)
                    if do_m:
                        maxima(NW - TAIL, NW)
                        dve.wait_ge(s["f_max"], NW * m_ + NW)
                        if not (static and k == -1):
                            dve.wait_ge(s["f_mT"], m_)
                        dve.tensor_scalar(mm[:, 0:32], mx, -1.0, None, ALU.mult).then_inc(s["f_mh"], 1)
                        dve.wait_ge(s["f_mh"], m_ + 1)
                        dve.scalar_tensor_tensor(mm[:, 32:64], mx, -1.0, mm[:, 0:32], ALU.mult, ALU.subtract).then_inc(s["f_mm"], 1)
                    if do_b:
                        final()
                attention(dve, stage)


def gate_sign(dve, link, dst, g, tmp):
    link(dve.tensor_scalar(dst, g, 0.0, 2.0, ALU.is_ge, ALU.mult))
    link(dve.scalar_tensor_tensor(tmp, g, -1.0, g, ALU.mult, ALU.max))
    link(dve.tensor_scalar(tmp, tmp, 0.25, None, ALU.max))
    link(dve.scalar_tensor_tensor(dst, dst, -1.0, tmp, ALU.add, ALU.mult))


def dump(nc, sem, out, slab, which):
    s = sem("s_dump")
    with nc.Block() as block:
        @block.sync
        def _(sp):
            for i, k in enumerate(which):
                sp.dma_start(out[i], slab[:, k, :]).then_inc(s, 16)
            sp.wait_ge(s, 16 * len(which))


def arrange(inputs):
    f = {k[3:]: np.asarray(v) for k, v in inputs.items()}
    d = {}
    d["x"] = f["attn_hidden_states"].reshape(NT, P, D)
    d["cT"] = f["c"].T
    wm = f["wmod"].reshape(D, 6, D)
    d["wmod1"] = wm[:, 0:2]
    d["wqkvT"] = np.stack([f["attn_W" + k].T for k in "qkv"], axis=1)
    d["taps"] = np.concatenate([f[f"attn_{k}conv_w"] for k in "qkv"], axis=1)
    d["wbrep"] = np.repeat(f["attn_Wb"].T, DH, axis=1)
    i32 = np.arange(C)
    part = np.arange(P) % C
    cst = np.zeros((P, C_END), np.float32)
    cst[:, C_IDENT:C_IDENT + P] = np.eye(P)
    cst[:, C_BONES:C_BONES + P] = np.kron(np.eye(H), np.ones((DH, DH)))
    cst[:, C_NEGA:C_NEGA + C] = -1.0 * (i32[None] > part[:, None])
    cst[:, C_CAUSAL:C_CAUSAL + C] = i32[None] >= part[:, None]
    cst[:, C_EYE:C_EYE + C] = i32[None] == part[:, None]
    cst[:, C_QUARTER:C_QUARTER + 4] = np.arange(P)[:, None] // C == np.arange(4)[None]
    d["consts"] = cst
    d["zeros"] = np.zeros((LONG - 1, D), np.float32)
    toep = np.zeros((WIN, D, C), np.float32)
    wl = f["attn_fir_long_w"].reshape(D, LONG)
    for i in range(C):
        toep[i:i + LONG, :, i] = wl.T
    d["toep"] = toep
    d["fsw"] = f["attn_fir_short_w"].reshape(D, SHORT)
    w1 = f["attn_gate_w1"]
    d["w1T"] = w1[:, :D].T
    d["w1s"] = np.zeros((P, 4, HID), np.float32)
    for i in range(4):
        d["w1s"][C * i:C * i + C, i] = w1[:, D:].T
    d["w2T"] = np.zeros((P, 2, C), np.float32)
    d["w2T"][:, :, 0:4 * H] = f["attn_gate_w2"].T.reshape(2, P, 4 * H).transpose(1, 0, 2)
    d["b1"] = f["attn_gate_b1"].reshape(2, P).T
    d["temp_bias"] = np.stack([np.repeat(f["attn_log_temp"], 4), f["attn_base_bias"].reshape(-1)])
    d["floor"] = f["attn_floor_raw"].reshape(-1)
    d["woT"] = f["attn_Wo"].T
    d["onorm"] = np.tile(f["attn_onorm_w"], H).reshape(D, 1)
    d["wga"] = wm[:, 2]
    d["w2"] = np.stack([f[f"ffn_{k}_w"].T for k in "qkvo"], axis=1)
    d["wmod2"] = wm[:, 3:6].reshape(D, 3 * D)
    d["cols"] = np.zeros((P, 12), np.float32)
    d["cols"][:, 0], d["cols"][:, 1] = f["ffn_q_b"], f["ffn_k_b"]
    for t in range(TPB):
        d["cols"][:D >> t, 4 + t], d["cols"][:D >> t, 8 + t] = f["ffn_norm_w"][:D >> t], f["ffn_norm_b"][:D >> t]
    d["v_b"] = f["ffn_v_b"]
    ob = np.zeros((TPB, D), np.float32)
    for t in range(TPB):
        ob[t, :D >> t] = f["ffn_o_b"][:D >> t]
    d["obR"] = ob.reshape(-1)
    return {k: np.ascontiguousarray(v) for k, v in d.items()}


def kernel(**inputs):
    import numpy as _np
    import concourse.bacc as _bacc
    from concourse import mybir as _mybir
    from concourse.bass_utils import run_bass_kernel_spmd as _run

    nc = _bacc.Bacc("TRN2", target_bir_lowering=False, num_devices=1)
    arrays = {"in_" + k: v for k, v in arrange(inputs).items()}
    a = {k: nc.dram_tensor(k, v.shape, _mybir.dt.from_np(v.dtype), kind="ExternalInput").ap() for k, v in arrays.items()}
    out = nc.dram_tensor("out", (NT, P, D), F32, kind="ExternalOutput").ap()
    build(nc, {k[3:]: v for k, v in a.items()}, out)
    r = _run(nc, [arrays], core_ids=[0])
    return r.results[0]["out"].reshape(B, T, D)
```
